# Optimizing a Trainium2 kernel written in Bass

```python
import numpy as np
import jax
import jax.numpy as jnp

def _softmax(x, axis=-1):
    return jax.nn.softmax(x, axis=axis)

def _gelu(x):
    return jax.nn.gelu(x, approximate=True)

def _silu(x):
    return jax.nn.silu(x)

def _sigmoid(x):
    return jax.nn.sigmoid(x)

def _layernorm(x, axis=-1, eps=1e-05):
    m = jnp.mean(x, axis=axis, keepdims=True)
    v = jnp.var(x, axis=axis, keepdims=True)
    return (x - m) / jnp.sqrt(v + eps)

def _scatter_add(tgt, idx, src, axis=0):
    return tgt.at[idx].add(src)

def _segment_sum(src, seg, n):
    return jax.ops.segment_sum(src, seg, n)
kernel_name = 'mk_flamingo_gated_d2_seqx_r2_44c8f0'

def setup_inputs(seed: int=0):
    np.random.seed(seed)
    _w = jnp.asarray

    def _rec_inputs():
        import jax
        import jax.numpy as jnp
        _rk = jax.random.key(seed)
        x = -0.000125 + 0.9999 * jax.random.normal(jax.random.fold_in(_rk, 1), (8, 512, 512), jnp.float32)
        _lenS = 512 - jax.random.randint(jax.random.fold_in(_rk, 7), (8,), 0, max(1, 512 // 4) + 1, jnp.int32)
        _lenS2 = 512 - jax.random.randint(jax.random.fold_in(_rk, 8), (8,), 0, max(1, 512 // 4) + 1, jnp.int32)
        _ctx_1024P = jax.random.normal(jax.random.fold_in(_rk, 11), (8, 16, 512), jnp.float32)
        _ctx_1024c = jax.random.dirichlet(jax.random.fold_in(_rk, 511), 0.3 * jnp.ones((16,), jnp.float32), (8, 512))
        _ctx_1024t = jnp.einsum('bsk,bkd->bsd', _ctx_1024c, _ctx_1024P)
        _ctx_1024t = _ctx_1024t * jax.lax.rsqrt(jnp.mean(jnp.square(_ctx_1024t)) + 1e-12) * 0.953939
        ctx_1024 = -1.52775e-05 + 0.999936 * (_ctx_1024t + 0.3 * jax.random.normal(jax.random.fold_in(_rk, 611), (8, 512, 512), jnp.float32))
        _g = jax.random.normal(jax.random.fold_in(_rk, 9001), (2, 2), jnp.float32)
        _g = jnp.sign(_g) * jnp.maximum(jnp.abs(_g), 1.0) + (_g == 0) * 1.0
        g_xattn = _g[0]
        g_ffn = _g[1]
        return (x, ctx_1024, g_xattn, g_ffn)
    x, ctx_1024, g_xattn, g_ffn = _rec_inputs()

    def _L0_xattn_setup():
        import jax, jax.numpy as jnp
        import numpy as np
        import math
        NHEADS = 16
        CAUSAL = True
        NEG_INF = -1e+18
        key = jax.random.key(seed)
        kq, kk, kv = jax.random.split(key, 3)
        B, S, D = (4, 4096, 512)
        q = jax.random.normal(kq, (B, S, D), dtype=jnp.float32)
        k = jax.random.normal(kk, (B, S, D), dtype=jnp.float32)
        v = jax.random.normal(kv, (B, S, D), dtype=jnp.float32)
        return {'q': q, 'k': k, 'v': v}
    _L0_xattn_all = _L0_xattn_setup()
    _L0_xattn_in = {k: v for k, v in _L0_xattn_all.items() if k in ()}
    del _L0_xattn_all

    def _L0_ffn_setup():
        import jax, jax.numpy as jnp
        import numpy as np
        DIM = 512
        H = 8
        DH = 64
        W = 64
        NQ = 256
        NKV = 512
        EPS = 1.0
        NITERS = 50
        FETCH = 9.0 / 8.0
        SCALE = DH ** (-0.5)

        def _ln(x, w, b):
            m = x.mean(-1, keepdims=True)
            v = ((x - m) ** 2).mean(-1, keepdims=True)
            return (x - m) * jax.lax.rsqrt(v + 1e-05) * w + b

        def _rms(x, g):
            n = jnp.maximum(jnp.linalg.norm(x, axis=-1, keepdims=True), 1e-12)
            return x / n * np.sqrt(DIM).astype(np.float32) * g

        def local_attn(x, Wqkv, Wout):
            b, n, _ = x.shape
            nw = n // W
            qkv = x @ Wqkv.T
            q, k, v = jnp.split(qkv, 3, axis=-1)

            def towin(t):
                return t.reshape(b, nw, W, H, DH).transpose(0, 3, 1, 2, 4)
            q, k, v = map(towin, (q, k, v))

            def expand(t):
                tp = jnp.pad(t, ((0, 0), (0, 0), (1, 1), (0, 0), (0, 0)))
                return jnp.concatenate([tp[:, :, :-2], tp[:, :, 1:-1], tp[:, :, 2:]], axis=3)
            ke, ve = (expand(k), expand(v))
            sim = jnp.einsum('bhnid,bhnjd->bhnij', q, ke) * SCALE
            win = jnp.arange(nw)
            valid = jnp.concatenate([jnp.repeat((win > 0)[:, None], W, 1), jnp.ones((nw, W), bool), jnp.repeat((win < nw - 1)[:, None], W, 1)], axis=1)
            sim = jnp.where(valid[None, None, :, None, :], sim, -1000000000.0)
            attn = jax.nn.softmax(sim, axis=-1)
            o = jnp.einsum('bhnij,bhnjd->bhnid', attn, ve)
            o = o.transpose(0, 2, 3, 1, 4).reshape(b, n, H * DH)
            return o @ Wout.T

        def route(x, routing_token, num_tokens):
            s = jnp.einsum('bnd,rd->brn', x, routing_token).reshape(x.shape[0], x.shape[1])
            n = s.shape[-1]
            logk = jnp.log(jnp.asarray(min(num_tokens * FETCH, float(n)), s.dtype))

            def body(ab, _):
                a, bb = ab
                a = EPS * (logk - jax.nn.logsumexp((s + bb) / EPS, axis=-1, keepdims=True))
                bb = -jax.nn.relu(s + a)
                return ((a, bb), None)
            (a, bb), _ = jax.lax.scan(body, (jnp.zeros((s.shape[0], 1), s.dtype), -s), None, length=NITERS)
            scores = jnp.exp((s + a + bb) / EPS)
            sel_scores, sel_idx = jax.lax.top_k(scores, num_tokens)
            sel_scores = sel_scores + jax.lax.stop_gradient(1.0 - sel_scores)
            return (sel_scores, sel_idx)

        def heavy_attn(xq, ctx, scores_kv, gamma, Wq, Wkv, Wout, null_kv):
            b = xq.shape[0]
            xq = _rms(xq, gamma)
            ctx = _rms(ctx, gamma)
            q = (xq @ Wq.T).reshape(b, -1, H, DH).transpose(0, 2, 1, 3)
            kv = (ctx @ Wkv.T).reshape(b, -1, H, 2 * DH).transpose(0, 2, 1, 3)
            k, v = (kv[..., :DH], kv[..., DH:])
            v = v * scores_kv[:, None, :, None]
            nk = jnp.broadcast_to(null_kv[0][None, :, None, :], (b, H, 1, DH))
            nv = jnp.broadcast_to(null_kv[1][None, :, None, :], (b, H, 1, DH))
            k = jnp.concatenate([nk, k], axis=2)
            v = jnp.concatenate([nv, v], axis=2)
            sim = jnp.einsum('bhid,bhjd->bhij', q, k) * SCALE
            attn = jax.nn.softmax(sim, axis=-1)
            o = jnp.einsum('bhij,bhjd->bhid', attn, v)
            o = o.transpose(0, 2, 1, 3).reshape(b, -1, H * DH)
            return o @ Wout.T
        key = jax.random.key(seed)
        ks = jax.random.split(key, 12)
        D, IN = (DIM, H * DH)
        w = lambda k, shape: jax.random.normal(k, shape, jnp.float32) * 0.02
        return {'x': jax.random.normal(ks[0], (4, 2048, D), jnp.float32), 'ln_w': jnp.ones((D,), jnp.float32), 'ln_b': jnp.zeros((D,), jnp.float32), 'Wqkv': w(ks[1], (3 * IN, D)), 'Wout_l': w(ks[2], (D, IN)), 'rt_q': jax.random.normal(ks[3], (1, D), jnp.float32), 'rt_kv': jax.random.normal(ks[4], (1, D), jnp.float32), 'gamma': jnp.ones((D,), jnp.float32), 'Wq': w(ks[5], (IN, D)), 'Wkv': w(ks[6], (2 * IN, D)), 'Wout_h': w(ks[7], (D, IN)), 'null_kv': jax.random.normal(ks[8], (2, H, DH), jnp.float32), 'null_q': jax.random.normal(ks[9], (D,), jnp.float32)}
    _L0_ffn_all = _L0_ffn_setup()
    _L0_ffn_in = {k: v for k, v in _L0_ffn_all.items() if k in ('ln_w', 'ln_b', 'Wqkv', 'Wout_l', 'rt_q', 'rt_kv', 'gamma', 'Wq', 'Wkv', 'Wout_h', 'null_kv', 'null_q')}
    del _L0_ffn_all

    def _L1_xattn_setup():
        import jax, jax.numpy as jnp
        import numpy as np
        EMBED = 512
        HEADS = 16
        HEAD_DIM = EMBED // HEADS
        WINDOW = 512
        HALF = WINDOW // 2
        SCALE = HEAD_DIM ** (-0.5)
        B, T = (2, 2048)

        def _sliding_window_attn(q, k, v):
            Bq, H, Tq, D = q.shape
            Bk = HALF
            nb = Tq // Bk
            qb = q.reshape(Bq, H, nb, Bk, D)

            def ctx(x):
                xb = x.reshape(Bq, H, nb, Bk, D)
                prev = jnp.concatenate([jnp.zeros_like(xb[:, :, :1]), xb[:, :, :-1]], axis=2)
                return jnp.concatenate([prev, xb], axis=3)
            kc, vc = (ctx(k), ctx(v))
            scores = jnp.einsum('bhnrd,bhncd->bhnrc', qb, kc)
            r = jnp.arange(Bk)[:, None]
            c = jnp.arange(2 * Bk)[None, :]
            band = (c >= r) & (c <= r + Bk)
            b_idx = jnp.arange(nb)[:, None, None]
            valid = band[None] & ((b_idx > 0) | (c[None] >= Bk))
            neg_inf = jnp.finfo(jnp.float32).min
            scores = jnp.where(valid[None, None], scores.astype(jnp.float32), neg_inf)
            attn = jax.nn.softmax(scores, axis=-1).astype(q.dtype)
            out = jnp.einsum('bhnrc,bhncd->bhnrd', attn, vc)
            return out.reshape(Bq, H, Tq, D)
        key = jax.random.key(seed)
        ks = jax.random.split(key, 11)
        f = jnp.float32
        return {'query': jax.random.normal(ks[0], (B, T, EMBED), f), 'key': jax.random.normal(ks[1], (B, T, EMBED), f), 'value': jax.random.normal(ks[2], (B, T, EMBED), f), 'wq': jax.random.normal(ks[3], (EMBED, EMBED), f) * 0.02, 'bq': jax.random.normal(ks[4], (EMBED,), f) * 0.02, 'wk': jax.random.normal(ks[5], (EMBED, EMBED), f) * 0.02, 'bk': jax.random.normal(ks[6], (EMBED,), f) * 0.02, 'wv': jax.random.normal(ks[7], (EMBED, EMBED), f) * 0.02, 'bv': jax.random.normal(ks[8], (EMBED,), f) * 0.02, 'wo': jax.random.normal(ks[9], (EMBED, EMBED), f) * 0.02, 'bo': jax.random.normal(ks[10], (EMBED,), f) * 0.02}
    _L1_xattn_all = _L1_xattn_setup()
    _L1_xattn_in = {k: v for k, v in _L1_xattn_all.items() if k in ('wq', 'bq', 'wk', 'bk', 'wv', 'bv', 'wo', 'bo')}
    del _L1_xattn_all

    def _L1_ffn_setup():
        import jax, jax.numpy as jnp
        import numpy as np
        BITS = 8
        LORA_RANK = 16
        LORA_ALPHA = 32
        SCALING = LORA_ALPHA / LORA_RANK

        def fake_quant_weight(w, bits=BITS):
            qmax = 2.0 ** (bits - 1) - 1
            scale = jnp.max(jnp.abs(w)) / qmax
            wq = jnp.clip(jnp.round(w / scale), -qmax - 1, qmax) * scale
            return w + jax.lax.stop_gradient(wq - w)

        def qat_lora_linear(x, W, b, A, B):
            Wq = fake_quant_weight(W)
            base = jnp.einsum('bsi,oi->bso', x, Wq) + b
            lora = jnp.einsum('bsr,or->bso', jnp.einsum('bsi,ri->bsr', x, A), B)
            return base + SCALING * lora
        key = jax.random.key(seed)
        ks = jax.random.split(key, 9)
        d, f = (512, 2048)
        s_in = 1.0 / np.sqrt(d)
        s_ff = 1.0 / np.sqrt(f)
        return {'hidden_states': jax.random.normal(ks[0], (4, 1024, d), jnp.float32), 'W_fc': jax.random.normal(ks[1], (f, d), jnp.float32) * s_in, 'b_fc': jnp.zeros((f,), jnp.float32), 'A_fc': jax.random.normal(ks[2], (LORA_RANK, d), jnp.float32) * s_in, 'B_fc': jnp.zeros((f, LORA_RANK), jnp.float32), 'W_proj': jax.random.normal(ks[3], (d, f), jnp.float32) * s_ff, 'b_proj': jnp.zeros((d,), jnp.float32), 'A_proj': jax.random.normal(ks[4], (LORA_RANK, f), jnp.float32) * s_ff, 'B_proj': jnp.zeros((d, LORA_RANK), jnp.float32)}
    _L1_ffn_all = _L1_ffn_setup()
    _L1_ffn_in = {k: v for k, v in _L1_ffn_all.items() if k in ('W_fc', 'b_fc', 'A_fc', 'B_fc', 'W_proj', 'b_proj', 'A_proj', 'B_proj')}
    del _L1_ffn_all
    return {'x': x, 'ctx_1024': ctx_1024, 'g_xattn': g_xattn, 'g_ffn': g_ffn, 'L0_ffn_ln_w': _L0_ffn_in['ln_w'], 'L0_ffn_ln_b': _L0_ffn_in['ln_b'], 'L0_ffn_Wqkv': _L0_ffn_in['Wqkv'], 'L0_ffn_Wout_l': _L0_ffn_in['Wout_l'], 'L0_ffn_rt_q': _L0_ffn_in['rt_q'], 'L0_ffn_rt_kv': _L0_ffn_in['rt_kv'], 'L0_ffn_gamma': _L0_ffn_in['gamma'], 'L0_ffn_Wq': _L0_ffn_in['Wq'], 'L0_ffn_Wkv': _L0_ffn_in['Wkv'], 'L0_ffn_Wout_h': _L0_ffn_in['Wout_h'], 'L0_ffn_null_kv': _L0_ffn_in['null_kv'], 'L0_ffn_null_q': _L0_ffn_in['null_q'], 'L1_xattn_wq': _L1_xattn_in['wq'], 'L1_xattn_bq': _L1_xattn_in['bq'], 'L1_xattn_wk': _L1_xattn_in['wk'], 'L1_xattn_bk': _L1_xattn_in['bk'], 'L1_xattn_wv': _L1_xattn_in['wv'], 'L1_xattn_bv': _L1_xattn_in['bv'], 'L1_xattn_wo': _L1_xattn_in['wo'], 'L1_xattn_bo': _L1_xattn_in['bo'], 'L1_ffn_W_fc': _L1_ffn_in['W_fc'], 'L1_ffn_b_fc': _L1_ffn_in['b_fc'], 'L1_ffn_A_fc': _L1_ffn_in['A_fc'], 'L1_ffn_B_fc': _L1_ffn_in['B_fc'], 'L1_ffn_W_proj': _L1_ffn_in['W_proj'], 'L1_ffn_b_proj': _L1_ffn_in['b_proj'], 'L1_ffn_A_proj': _L1_ffn_in['A_proj'], 'L1_ffn_B_proj': _L1_ffn_in['B_proj']}

def reference(x, ctx_1024, g_xattn, g_ffn, L0_ffn_ln_w, L0_ffn_ln_b, L0_ffn_Wqkv, L0_ffn_Wout_l, L0_ffn_rt_q, L0_ffn_rt_kv, L0_ffn_gamma, L0_ffn_Wq, L0_ffn_Wkv, L0_ffn_Wout_h, L0_ffn_null_kv, L0_ffn_null_q, L1_xattn_wq, L1_xattn_bq, L1_xattn_wk, L1_xattn_bk, L1_xattn_wv, L1_xattn_bv, L1_xattn_wo, L1_xattn_bo, L1_ffn_W_fc, L1_ffn_b_fc, L1_ffn_A_fc, L1_ffn_B_fc, L1_ffn_W_proj, L1_ffn_b_proj, L1_ffn_A_proj, L1_ffn_B_proj):
    import jax
    import jax.numpy as jnp

    def _L0_xattn_ref(q, k, v):
        import jax, jax.numpy as jnp
        import numpy as np
        import math
        NHEADS = 16
        CAUSAL = True
        NEG_INF = -1e+18
        B, S, D = q.shape
        hd = D // NHEADS
        qh = q.reshape(B, S, NHEADS, hd)
        kh = k.reshape(B, S, NHEADS, hd)
        vh = v.reshape(B, S, NHEADS, hd)
        scores = jnp.einsum('bsqd,bskd->bsqk', qh, kh) / math.sqrt(hd)
        if CAUSAL:
            mask = jnp.tril(jnp.ones((NHEADS, NHEADS), dtype=bool))
            scores = jnp.where(mask, scores, jnp.asarray(NEG_INF, scores.dtype))
        attn = jax.nn.softmax(scores, axis=-1)
        out = jnp.einsum('bsqk,bskd->bsqd', attn, vh)
        return out.reshape(B, S, D)

    def _L0_ffn_ref(x, ln_w, ln_b, Wqkv, Wout_l, rt_q, rt_kv, gamma, Wq, Wkv, Wout_h, null_kv, null_q):
        import jax, jax.numpy as jnp
        import numpy as np
        DIM = 512
        H = 8
        DH = 64
        W = 64
        NQ = 256
        NKV = 512
        EPS = 1.0
        NITERS = 50
        FETCH = 9.0 / 8.0
        SCALE = DH ** (-0.5)

        def _ln(x, w, b):
            m = x.mean(-1, keepdims=True)
            v = ((x - m) ** 2).mean(-1, keepdims=True)
            return (x - m) * jax.lax.rsqrt(v + 1e-05) * w + b

        def _rms(x, g):
            n = jnp.maximum(jnp.linalg.norm(x, axis=-1, keepdims=True), 1e-12)
            return x / n * np.sqrt(DIM).astype(np.float32) * g

        def local_attn(x, Wqkv, Wout):
            b, n, _ = x.shape
            nw = n // W
            qkv = x @ Wqkv.T
            q, k, v = jnp.split(qkv, 3, axis=-1)

            def towin(t):
                return t.reshape(b, nw, W, H, DH).transpose(0, 3, 1, 2, 4)
            q, k, v = map(towin, (q, k, v))

            def expand(t):
                tp = jnp.pad(t, ((0, 0), (0, 0), (1, 1), (0, 0), (0, 0)))
                return jnp.concatenate([tp[:, :, :-2], tp[:, :, 1:-1], tp[:, :, 2:]], axis=3)
            ke, ve = (expand(k), expand(v))
            sim = jnp.einsum('bhnid,bhnjd->bhnij', q, ke) * SCALE
            win = jnp.arange(nw)
            valid = jnp.concatenate([jnp.repeat((win > 0)[:, None], W, 1), jnp.ones((nw, W), bool), jnp.repeat((win < nw - 1)[:, None], W, 1)], axis=1)
            sim = jnp.where(valid[None, None, :, None, :], sim, -1000000000.0)
            attn = jax.nn.softmax(sim, axis=-1)
            o = jnp.einsum('bhnij,bhnjd->bhnid', attn, ve)
            o = o.transpose(0, 2, 3, 1, 4).reshape(b, n, H * DH)
            return o @ Wout.T

        def route(x, routing_token, num_tokens):
            s = jnp.einsum('bnd,rd->brn', x, routing_token).reshape(x.shape[0], x.shape[1])
            n = s.shape[-1]
            logk = jnp.log(jnp.asarray(min(num_tokens * FETCH, float(n)), s.dtype))

            def body(ab, _):
                a, bb = ab
                a = EPS * (logk - jax.nn.logsumexp((s + bb) / EPS, axis=-1, keepdims=True))
                bb = -jax.nn.relu(s + a)
                return ((a, bb), None)
            (a, bb), _ = jax.lax.scan(body, (jnp.zeros((s.shape[0], 1), s.dtype), -s), None, length=NITERS)
            scores = jnp.exp((s + a + bb) / EPS)
            sel_scores, sel_idx = jax.lax.top_k(scores, num_tokens)
            sel_scores = sel_scores + jax.lax.stop_gradient(1.0 - sel_scores)
            return (sel_scores, sel_idx)

        def heavy_attn(xq, ctx, scores_kv, gamma, Wq, Wkv, Wout, null_kv):
            b = xq.shape[0]
            xq = _rms(xq, gamma)
            ctx = _rms(ctx, gamma)
            q = (xq @ Wq.T).reshape(b, -1, H, DH).transpose(0, 2, 1, 3)
            kv = (ctx @ Wkv.T).reshape(b, -1, H, 2 * DH).transpose(0, 2, 1, 3)
            k, v = (kv[..., :DH], kv[..., DH:])
            v = v * scores_kv[:, None, :, None]
            nk = jnp.broadcast_to(null_kv[0][None, :, None, :], (b, H, 1, DH))
            nv = jnp.broadcast_to(null_kv[1][None, :, None, :], (b, H, 1, DH))
            k = jnp.concatenate([nk, k], axis=2)
            v = jnp.concatenate([nv, v], axis=2)
            sim = jnp.einsum('bhid,bhjd->bhij', q, k) * SCALE
            attn = jax.nn.softmax(sim, axis=-1)
            o = jnp.einsum('bhij,bhjd->bhid', attn, v)
            o = o.transpose(0, 2, 1, 3).reshape(b, -1, H * DH)
            return o @ Wout.T
        b, n, d = x.shape
        light = local_attn(_ln(x, ln_w, ln_b), Wqkv, Wout_l)
        sq, iq = route(x, rt_q, NQ)
        skv, ikv = route(x, rt_kv, NKV)
        br = jnp.arange(b)[:, None]
        xq = x[br, iq]
        xkv = x[br, ikv]
        heavy = heavy_attn(xq, xkv, skv, gamma, Wq, Wkv, Wout_h, null_kv)
        heavy = heavy * sq[..., None]
        out = jnp.broadcast_to(null_q[None, None, :], (b, n, d))
        out = out.at[br, iq].set(heavy)
        return out + light

    def _L1_xattn_ref(query, key, value, wq, bq, wk, bk, wv, bv, wo, bo):
        import jax, jax.numpy as jnp
        import numpy as np
        EMBED = 512
        HEADS = 16
        HEAD_DIM = EMBED // HEADS
        WINDOW = 512
        HALF = WINDOW // 2
        SCALE = HEAD_DIM ** (-0.5)
        B, T = (2, 2048)

        def _sliding_window_attn(q, k, v):
            Bq, H, Tq, D = q.shape
            Bk = HALF
            nb = Tq // Bk
            qb = q.reshape(Bq, H, nb, Bk, D)

            def ctx(x):
                xb = x.reshape(Bq, H, nb, Bk, D)
                prev = jnp.concatenate([jnp.zeros_like(xb[:, :, :1]), xb[:, :, :-1]], axis=2)
                return jnp.concatenate([prev, xb], axis=3)
            kc, vc = (ctx(k), ctx(v))
            scores = jnp.einsum('bhnrd,bhncd->bhnrc', qb, kc)
            r = jnp.arange(Bk)[:, None]
            c = jnp.arange(2 * Bk)[None, :]
            band = (c >= r) & (c <= r + Bk)
            b_idx = jnp.arange(nb)[:, None, None]
            valid = band[None] & ((b_idx > 0) | (c[None] >= Bk))
            neg_inf = jnp.finfo(jnp.float32).min
            scores = jnp.where(valid[None, None], scores.astype(jnp.float32), neg_inf)
            attn = jax.nn.softmax(scores, axis=-1).astype(q.dtype)
            out = jnp.einsum('bhnrc,bhncd->bhnrd', attn, vc)
            return out.reshape(Bq, H, Tq, D)
        Bq, Tq, C = query.shape
        split = lambda x: x.reshape(Bq, Tq, HEADS, HEAD_DIM).transpose(0, 2, 1, 3)
        q = split(jnp.einsum('btc,oc->bto', query, wq) + bq) * SCALE
        k = split(jnp.einsum('btc,oc->bto', key, wk) + bk)
        v = split(jnp.einsum('btc,oc->bto', value, wv) + bv)
        o = _sliding_window_attn(q, k, v)
        o = o.transpose(0, 2, 1, 3).reshape(Bq, Tq, C)
        return jnp.einsum('btc,oc->bto', o, wo) + bo

    def _L1_ffn_ref(hidden_states, W_fc, b_fc, A_fc, B_fc, W_proj, b_proj, A_proj, B_proj):
        import jax, jax.numpy as jnp
        import numpy as np
        BITS = 8
        LORA_RANK = 16
        LORA_ALPHA = 32
        SCALING = LORA_ALPHA / LORA_RANK

        def fake_quant_weight(w, bits=BITS):
            qmax = 2.0 ** (bits - 1) - 1
            scale = jnp.max(jnp.abs(w)) / qmax
            wq = jnp.clip(jnp.round(w / scale), -qmax - 1, qmax) * scale
            return w + jax.lax.stop_gradient(wq - w)

        def qat_lora_linear(x, W, b, A, B):
            Wq = fake_quant_weight(W)
            base = jnp.einsum('bsi,oi->bso', x, Wq) + b
            lora = jnp.einsum('bsr,or->bso', jnp.einsum('bsi,ri->bsr', x, A), B)
            return base + SCALING * lora
        h = qat_lora_linear(hidden_states, W_fc, b_fc, A_fc, B_fc)
        h = jax.nn.gelu(h, approximate=False)
        h = qat_lora_linear(h, W_proj, b_proj, A_proj, B_proj)
        return h
    x = x + jnp.tanh(g_xattn[0]) * _L0_xattn_ref(_layernorm(x, axis=-1), ctx_1024, ctx_1024)
    x = x + jnp.tanh(g_ffn[0]) * _L0_ffn_ref(_layernorm(x, axis=-1), L0_ffn_ln_w, L0_ffn_ln_b, L0_ffn_Wqkv, L0_ffn_Wout_l, L0_ffn_rt_q, L0_ffn_rt_kv, L0_ffn_gamma, L0_ffn_Wq, L0_ffn_Wkv, L0_ffn_Wout_h, L0_ffn_null_kv, L0_ffn_null_q)
    x = x + jnp.tanh(g_xattn[1]) * _L1_xattn_ref(_layernorm(x, axis=-1), ctx_1024, ctx_1024, L1_xattn_wq, L1_xattn_bq, L1_xattn_wk, L1_xattn_bk, L1_xattn_wv, L1_xattn_bv, L1_xattn_wo, L1_xattn_bo)
    x = x + jnp.tanh(g_ffn[1]) * _L1_ffn_ref(_layernorm(x, axis=-1), L1_ffn_W_fc, L1_ffn_b_fc, L1_ffn_A_fc, L1_ffn_B_fc, L1_ffn_W_proj, L1_ffn_b_proj, L1_ffn_A_proj, L1_ffn_B_proj)
    return x

_drawn_inputs = setup_inputs


def setup_inputs(seed=0):
    import zlib

    import numpy as np

    out = dict(_drawn_inputs(seed))
    spreads = {'g_ffn': (-1.0, 0.6),
     'L0_ffn_ln_w': (1.0, 0.6),
     'L0_ffn_ln_b': (0.0, 0.712),
     'L0_ffn_gamma': (1.0, 0.6),
     'L1_ffn_b_fc': (0.0, 0.428),
     'L1_ffn_B_fc': (0.0, 0.1),
     'L1_ffn_b_proj': (0.0, 0.35),
     'L1_ffn_B_proj': (0.0, 0.1)}
    factors = {'L0_ffn_rt_kv': 64.0,
     'L0_ffn_Wq': 8.0,
     'L0_ffn_Wkv': 3.914,
     'L0_ffn_Wout_h': 3.889,
     'L0_ffn_null_kv': 8.0,
     'L1_xattn_wq': 8.0,
     'L1_xattn_bq': 64.0,
     'L1_xattn_wk': 8.0,
     'L1_xattn_bk': 64.0,
     'L1_xattn_bv': 24.275,
     'L1_xattn_bo': 9.694}
    for name, (base, spread) in spreads.items():
        noise = np.random.default_rng([zlib.crc32(name.encode()), seed]).standard_normal(out[name].shape)
        drawn = base * np.exp(spread * noise) if base else spread * noise
        out[name] = jnp.asarray(drawn.astype(out[name].dtype))
    for name, factor in factors.items():
        out[name] = (out[name] * factor).astype(out[name].dtype)
    return out
```

```python
import concourse.bass as bass
from concourse import mybir
from contextlib import ExitStack
import numpy as np

f32 = mybir.dt.float32
bf16 = mybir.dt.bfloat16
ALU = mybir.AluOpType
ACT = mybir.ActivationFunctionType
AX = mybir.AxisListType

B, S, D = 8, 512, 512
P = 128
TT = S // P
CT = D // P
EPS = 1e-5
NEG = -1e30

SEED = 48


def after(i, per, k):
    return i * per + (SEED + k + 1)


class Steps:

    def __init__(self, i, per):
        self.i, self.per, self.k = i, per, 0

    def next(self):
        self.k += 1
        return after(self.i, self.per, self.k - 1)

    def close(self):
        assert self.k == self.per, (self.k, self.per)


def open_phase(nc, keep, names):
    sems = {n: keep.enter_context(nc.semaphore(n)) for n in names}
    with nc.Block() as block:
        @block.gpsimd
        def _(pool):
            for s in sems.values():
                pool.sem_inc(s, SEED)
    return sems


def phase_token_heads(nc, keep, x_th, v_th, kT_th, consts, gates, x1):
    H, DH = 16, 32
    G = S // 8
    R = G // 4
    W = G * DH
    SCALE = DH ** -0.5
    with ExitStack() as ctx:
        def sb(name, shape, dt=f32):
            return ctx.enter_context(nc.sbuf_tensor(name, shape, dt))

        a_stored = keep.enter_context(nc.semaphore("a_stored"))
        names = ["a_const", "a_loaded0", "a_loaded1", "a_kv0", "a_kv1", "a_tanh", "a_sums", "a_mean", "a_sqsums", "a_var", "a_vareps", "a_rstd",
                 "a_q", "a_qturn", "a_qcopy", "a_scores", "a_shift", "a_probs", "a_psum", "a_pturn", "a_pcopy",
                 "a_outT", "a_outTcopy", "a_outrow", "a_done", "a_vstep", "a_xfree", "a_zeroed"]
        sem = open_phase(nc, keep, names)
        X = sb("a_x", [P, 2, W])
        V = sb("a_v", [P, 2, W])
        KH = sb("a_kh", [P, 2, R, 4 * P])
        XC = sb("a_xc", [P, W])
        SQ = sb("a_sq", [P, W])
        Q = sb("a_qn", [P, W])
        ST = sb("a_st", [P, 4, G])
        POWT = sb("a_pow", [P, G])
        QT = sb("a_qT", [P, 2, P])
        Z = sb("a_z", [P, 2, 4, P])
        PR = sb("a_pr", [P, 2, 4, P])
        PT = sb("a_pT", [P, 2, 4 * P])
        OT = sb("a_oT", [P, 2, P])
        MX = sb("a_mx", [P, 2, 4])
        SM = sb("a_sm", [P, 2, 16])
        RS = sb("a_rs", [P, 16])
        TO = sb("a_to", [P, 16, DH])
        IDF, IDB, BM, MASK = (sb("a_idf", [P, P]), sb("a_idb", [P, P], bf16), sb("a_bm", [P, P]), sb("a_mask", [P, 4 * P], bf16))
        GT = sb("a_gt", [P, 4])
        TG = sb("a_tg", [P, 4])
        bank = [ctx.enter_context(nc.psum_tensor(f"a_ps{i}", [P, 512], f32)) for i in range(8)]
        pS, pP, pQ, pOT, pO, pL = bank[0:2], bank[2:4], bank[4], bank[5], bank[6], bank[7]
        NV = 2 + R + 3 * (R // 4)

        with nc.Block() as block:
            @block.sync
            def _(sp):
                sp.wait_ge(sem["a_zeroed"], SEED + 2)
                sp.dma_start(IDF[:, :], consts["idf"]).then_inc(sem["a_const"], 16)
                sp.dma_start(IDB[:, :], consts["idb"]).then_inc(sem["a_const"], 16)
                sp.dma_start(BM[:, :], consts["blockmean"]).then_inc(sem["a_const"], 16)
                sp.dma_start(MASK[:, :], consts["mask_th"]).then_inc(sem["a_const"], 16)
                sp.dma_start(GT[:, :], gates).then_inc(sem["a_const"], 16)
                with sp.Fori(0, B // 2) as i:
                    for u in range(2):
                        b = i * 2 + u
                        sp.wait_ge(sem["a_xfree"], after(i, 2, u - 2))
                        sp.dma_start(X[:, u, :], x_th[bass.ds(b, 1), :, :].rearrange("o p w -> (o p) w")).then_inc(sem[f"a_loaded{u}"], 16)
                        sp.wait_ge(sem["a_outT"], after(i, 2 * R, (u - 2) * R + R - 1))
                        sp.dma_start(V[:, u, :], v_th[bass.ds(b, 1), :, :].rearrange("o p w -> (o p) w")).then_inc(sem[f"a_kv{u}"], 16)
                        for g in range(4):
                            sp.dma_start(KH[32 * g:32 * g + 32, u, :, P * g:P * g + P],
                                         kT_th[bass.ds(b, 1), 32 * g:32 * g + 32, :, :].rearrange("o p r n -> (o p) r n")).then_inc(sem[f"a_kv{u}"], 16)

            @block.gpsimd
            def _(pool):
                with pool.Fori(0, B // 2) as i:
                    for u in range(2):
                        b = i * 2 + u
                        pool.wait_ge(sem["a_vareps"], after(i, 2, u))
                        pool.tensor_tensor(ST[:, 3, :], ST[:, 2, :], POWT[:, :], ALU.pow).then_inc(sem["a_rstd"], 1)
                        pool.wait_ge(sem["a_done"], after(i, 2 * (R // 4), u * (R // 4) + R // 4 - 1))
                        pool.dma_start(x1[bass.ds(b, 1), :, :].rearrange("o (g t) (h d) -> (o t h) g d", t=8, d=DH),
                                       X[:, u, :].rearrange("p (g d) -> p g d", d=DH)).then_inc(a_stored, 16)
                        pool.wait_ge(a_stored, b * 16 + 16)
                        pool.sem_inc(sem["a_xfree"], 1)

            @block.scalar
            def _(act):
                act.wait_ge(sem["a_const"], SEED + 80)
                act.activation(TG[:, :], GT[:, :], ACT.Tanh).then_inc(sem["a_tanh"], 1)
                with act.Fori(0, B // 2) as i:
                    for u in range(2):
                        n = lambda k: after(i, 2 * R, u * R + k)

                        def copy_q(r):
                            act.wait_ge(sem["a_qturn"], n(r))
                            act.wait_ge(sem["a_scores"], n(r - 2))
                            act.copy(QT[:, r % 2, :], pQ[:, 0:P]).then_inc(sem["a_qcopy"], 1)

                        copy_q(0)
                        for r in range(R + 2):
                            if r + 1 < R:
                                copy_q(r + 1)
                            if r < R:
                                act.wait_ge(sem["a_shift"], n(r))
                                act.wait_ge(sem["a_pturn"], n(r - 2))
                                act.wait_ge(sem["a_psum"], n(r - 2))
                                act.activation(PR[:, r % 2, :, :], Z[:, r % 2, :, :], ACT.Exp, scale=SCALE).then_inc(sem["a_probs"], 1)
                            if 1 <= r <= R:
                                act.wait_ge(sem["a_pturn"], n(r - 1))
                                act.wait_ge(sem["a_outT"], n(r - 3))
                                act.copy(PT[:, (r - 1) % 2, :], pP[(r - 1) % 2][:, :]).then_inc(sem["a_pcopy"], 1)
                            if r >= 2:
                                act.wait_ge(sem["a_outT"], n(r - 2))
                                act.wait_ge(sem["a_outrow"], n(r - 4))
                                act.copy(OT[:, r % 2, :], pOT[:, 0:P]).then_inc(sem["a_outTcopy"], 1)

            @block.vector
            def _(dve):
                dve.memset(POWT[:, :], -0.5).then_inc(sem["a_zeroed"], 1)
                dve.memset(KH[:, :, :, :], 0.0).then_inc(sem["a_zeroed"], 1)
                with dve.Fori(0, B // 2) as i:
                    for u in range(2):
                        steps = Steps(i * 2 + u, NV)
                        n = lambda k: after(i, 2 * R, u * R + k)
                        x3 = X[:, u, :].rearrange("p (g d) -> p g d", d=DH)
                        xc3, sq3, q3 = (t[:, :].rearrange("p (g d) -> p g d", d=DH) for t in (XC, SQ, Q))
                        dve.wait_ge(sem[f"a_loaded{u}"], i * 16 + (SEED + 16))
                        dve.wait_ge(sem["a_mean"], after(i, 2, u - 1))
                        dve.reduce_sum(ST[:, 0, :], x3, axis=AX.X).then_inc(sem["a_sums"], 1)
                        dve.wait_ge(sem["a_mean"], after(i, 2, u))
                        dve.tensor_tensor(xc3, x3, pL[:, 0:G].unsqueeze(2).broadcast_to([P, G, DH]), ALU.subtract).then_inc(sem["a_vstep"], 1)
                        dve.wait_ge(sem["a_vstep"], steps.next())
                        dve.tensor_tensor(SQ[:, :], XC[:, :], XC[:, :], ALU.mult).then_inc(sem["a_vstep"], 1)
                        dve.wait_ge(sem["a_vstep"], steps.next())
                        dve.reduce_sum(ST[:, 1, :], sq3, axis=AX.X).then_inc(sem["a_sqsums"], 1)
                        dve.wait_ge(sem["a_var"], after(i, 2, u))
                        dve.tensor_scalar(ST[:, 2, :], pL[:, G:2 * G], EPS, None, ALU.add).then_inc(sem["a_vareps"], 1)
                        dve.wait_ge(sem["a_rstd"], after(i, 2, u))
                        dve.wait_ge(sem["a_qturn"], n(-1))
                        dve.tensor_tensor(q3, xc3, ST[:, 3, :].unsqueeze(2).broadcast_to([P, G, DH]), ALU.mult).then_inc(sem["a_q"], 1)

                        def finish(j):
                            rs = RS[:, :]
                            dve.wait_ge(sem["a_psum"], n(4 * j + 3))
                            dve.reciprocal(rs, SM[:, j % 2, :]).then_inc(sem["a_vstep"], 1)
                            dve.wait_ge(sem["a_vstep"], steps.next())
                            dve.tensor_scalar(rs, rs, TG[:, 0:1], None, ALU.mult).then_inc(sem["a_vstep"], 1)
                            dve.wait_ge(sem["a_vstep"], steps.next())
                            dve.wait_ge(sem["a_outrow"], n(4 * j + 3))
                            dve.tensor_tensor(TO[:, :, :], pO[:, :].rearrange("p (g d) -> p g d", d=DH),
                                              rs.unsqueeze(2).broadcast_to([P, 16, DH]), ALU.mult).then_inc(sem["a_vstep"], 1)
                            dve.wait_ge(sem["a_vstep"], steps.next())
                            xs = x3[:, 16 * j:16 * j + 16, :]
                            dve.tensor_tensor(xs, xs, TO[:, :, :], ALU.add).then_inc(sem["a_done"], 1)

                        dve.wait_ge(sem["a_tanh"], SEED + 1)
                        for r in range(R + 4):
                            if r < R:
                                dve.wait_ge(sem["a_scores"], n(r))
                                dve.reduce_max(MX[:, r % 2, :], pS[r % 2][:, :].rearrange("p (g n) -> p g n", n=P), axis=AX.X).then_inc(sem["a_vstep"], 1)
                                dve.wait_ge(sem["a_vstep"], steps.next())
                                dve.wait_ge(sem["a_probs"], n(r - 2))
                                dve.tensor_tensor(Z[:, r % 2, :, :], pS[r % 2][:, :].rearrange("p (g n) -> p g n", n=P),
                                                  MX[:, r % 2, :].unsqueeze(2).broadcast_to([P, 4, P]), ALU.subtract).then_inc(sem["a_shift"], 1)
                            if 1 <= r <= R:
                                dve.wait_ge(sem["a_probs"], n(r - 1))
                                dve.reduce_sum(SM[:, (r - 1) // 4 % 2, 4 * ((r - 1) % 4):4 * ((r - 1) % 4) + 4], PR[:, (r - 1) % 2, :, :], axis=AX.X).then_inc(sem["a_psum"], 1)
                            if r >= 7 and (r - 7) % 4 == 0:
                                finish((r - 7) // 4)
                        steps.close()

            @block.tensor
            def _(pe):
                pe.wait_ge(sem["a_const"], SEED + 80)
                with pe.Fori(0, B // 2) as i:
                    for u in range(2):
                        n = lambda k: after(i, 2 * R, u * R + k)
                        pe.wait_ge(sem["a_sums"], after(i, 2, u))
                        pe.wait_ge(sem["a_vareps"], after(i, 2, u - 1))
                        pe.matmul(pL[:, 0:G], BM[:, :], ST[:, 0, :], start=True, stop=True).then_inc(sem["a_mean"], 1)
                        pe.wait_ge(sem["a_sqsums"], after(i, 2, u))
                        pe.matmul(pL[:, G:2 * G], BM[:, :], ST[:, 1, :], start=True, stop=True).then_inc(sem["a_var"], 1)
                        pe.wait_ge(sem[f"a_kv{u}"], i * 80 + (SEED + 80))

                        def turn_q(r):
                            pe.wait_ge(sem["a_qcopy"], n(r - 1))
                            pe.transpose(pQ[:, 0:P], Q[:, P * r:P * r + P], IDF[:, :]).then_inc(sem["a_qturn"], 1)

                        pe.wait_ge(sem["a_q"], after(i, 2, u))
                        turn_q(0)
                        for r in range(R + 3):
                            if r + 1 < R:
                                turn_q(r + 1)
                            if r < R:
                                pe.wait_ge(sem["a_qcopy"], n(r))
                                pe.wait_ge(sem["a_shift"], n(r - 2))
                                pe.matmul(pS[r % 2][:, :], IDB[:, :], MASK[:, :], start=True, stop=False)
                                pe.matmul(pS[r % 2][:, :], QT[:, r % 2, :], KH[:, u, r, :], start=False, stop=True).then_inc(sem["a_scores"], 1)
                            if 1 <= r <= R:
                                pe.wait_ge(sem["a_probs"], n(r - 1))
                                pe.wait_ge(sem["a_pcopy"], n(r - 3))
                                for g in range(4):
                                    last = pe.transpose(pP[(r - 1) % 2][:, P * g:P * g + P], PR[:, (r - 1) % 2, g, :], IDF[:, :])
                                last.then_inc(sem["a_pturn"], 1)
                            if 2 <= r <= R + 1:
                                pe.wait_ge(sem["a_pcopy"], n(r - 2))
                                pe.wait_ge(sem["a_outTcopy"], n(r - 3))
                                for g in range(4):
                                    gg = 4 * (r - 2) + g
                                    last = pe.matmul(pOT[32 * g:32 * g + 32, 0:P], V[:, u, 32 * gg:32 * gg + 32],
                                                     PT[:, r % 2, P * g:P * g + P], start=True, stop=True)
                                last.then_inc(sem["a_outT"], 1)
                            if r >= 3:
                                pe.wait_ge(sem["a_outTcopy"], n(r - 3))
                                if (r - 3) % 4 == 0:
                                    pe.wait_ge(sem["a_done"], after(i, 2 * (R // 4), u * (R // 4) + (r - 3) // 4 - 1))
                                c = (r - 3) % 4
                                pe.transpose(pO[:, P * c:P * c + P], OT[:, (r - 3) % 2, :], IDF[:, :]).then_inc(sem["a_outrow"], 1)


class Banks:

    def __init__(self, jobs, engine_of):
        self.jobs = jobs
        self.engine = [engine_of(m, job) for m, job in enumerate(jobs)]
        self.per = {e: self.engine.count(e) for e in ("act", "dve")}

    def of(self, kind):
        return [m for m, job in enumerate(self.jobs) if job[0] == kind]

    def emptied(self, i, m, e):
        back = 0
        while m < 0:
            m, back = m + len(self.jobs), back + 1
        return after(i, self.per[e], self.engine[:m + 1].count(e) - 1 - back * self.per[e])


def phase_local(nc, keep, a, x1, x1l, xr, s_route):
    H, DH, WIN = 8, 64, 64
    SCALE = DH ** -0.5
    J = 4
    U = J * TT
    jobs = [("x", c) for c in range(4)] + [("q", j) for j in range(4)] + [("k", j) for j in range(4)] + \
           [("v", t) for t in range(4)] + [("o", t) for t in range(4)]
    banks = Banks(jobs, lambda m, job: "dve" if job[0] == "o" else ("act", "dve")[m % 2])
    NX, NQ, NK, NVV, NO = (banks.of(k) for k in "xqkvo")
    with ExitStack() as ctx:
        def sb(name, shape, dt=f32):
            return ctx.enter_context(nc.sbuf_tensor("b_" + name, shape, dt))

        names = ["const", "loaded", "resid", "read", "stats", "rstd", "xr", "s", "route_out", "xr_out", "norm",
                 "full", "act_empty", "dve_empty", "scores", "negmax", "probs", "scaled", "pturn", "pmain", "pextra",
                 "outT", "outTcopy", "tanh", "step", "out", "rows", "zero"]
        sem = open_phase(nc, keep, ["b_" + n for n in names])
        sem = {n: sem["b_" + n] for n in names}
        emptied = {"act": sem["act_empty"], "dve": sem["dve_empty"]}
        WQKV = sb("wqkv", [P, CT, 3 * D])
        WO = sb("wo", [P, CT, D])
        RT = sb("rt", [P, 2, D])
        LNW, LNB = sb("lnw", [P, CT]), sb("lnb", [P, CT])
        IDF, IDB, NEGB = sb("idf", [P, P]), sb("idb", [P, P], bf16), sb("negb", [P, WIN], bf16)
        GT, TG = sb("gt", [P, 4]), sb("tg", [P, 4])
        X, XL, XA, XB, XR = (sb(n, [P, TT, D]) for n in ("x", "xl", "xa", "xb", "xr"))
        XBT = sb("xbT", [P, CT, S])
        QT, KT, V = sb("qT", [P, J, S]), sb("kT", [P, J, 2, S]), sb("v", [P, TT, D])
        VL = sb("vlo", [WIN, TT, D])
        BN, MV, RD, POWT = sb("bn", [P, TT, 6]), sb("mv", [P, 3 * TT, 2]), sb("rd", [P, 3 * TT]), sb("pow", [P, 2 * TT])
        VE = sb("ve", [P, 3 * TT])
        SS, SCR = sb("ss", [P, 2, TT]), sb("scr", [P, D])
        PR, NM, SM, RI = sb("pr", [P, 2, 2, 192]), sb("nm", [P, 2, 2]), sb("sm", [P, 2, 2]), sb("ri", [P, 2, 2])
        PTM, PTE = sb("pTm", [P, 2, 2, P]), sb("pTe", [WIN, 2, 2, P])
        OT, Y = sb("oT", [P, J, S]), sb("y", [P, TT, D])
        bank = [ctx.enter_context(nc.psum_tensor(f"b_ps{i}", [P, 512], f32)) for i in range(8)]
        pW, pS, pP, pO = bank[0:2], bank[2:4], bank[4:6], bank[6:8]

        with nc.Block() as block:
            @block.sync
            def _(sp):
                for dst, src in ((WQKV[:, :, :], a["wqkvT"]), (WO[:, :, :], a["woutlT"]), (RT[:, :, :], a["rt"]), (LNW[:, :], a["ln_w"]),
                                 (LNB[:, :], a["ln_b"]), (IDF[:, :], a["idf"]), (IDB[:, :], a["idb"]), (NEGB[:, :], a["neg64"]),
                                 (GT[:, :], a["gates"])):
                    sp.dma_start(dst, src).then_inc(sem["const"], 16)
                with sp.Fori(0, B) as i:
                    row = lambda t: t[bass.ds(i, 1), :, :].rearrange("o (t p) d -> p (o t) d", p=P)
                    sp.wait_ge(sem["read"], after(i, 1, -1))
                    sp.dma_start(X[:, :, :], row(x1)).then_inc(sem["loaded"], 16)
                    sp.wait_ge(sem["dve_empty"], banks.emptied(i, -1, "dve"))
                    sp.dma_start(XL[:, :, :], row(x1)).then_inc(sem["resid"], 16)
                    sp.wait_ge(sem["xr"], after(i, 1, 0))
                    sp.dma_start(row(xr), XR[:, :, :]).then_inc(sem["xr_out"], 16)
                    sp.wait_ge(sem["s"], after(i, 1, 0))
                    sp.dma_start(s_route[bass.ds(i, 1), :, :].rearrange("o p n -> (o p) n"), SS[:, :, :].rearrange("p r t -> p (r t)")).then_inc(sem["route_out"], 16)
                    sp.wait_ge(sem["dve_empty"], banks.emptied(i, NO[-1], "dve"))
                    sp.dma_start(row(x1l), Y[:, :, :]).then_inc(sem["out"], 16)
                sp.wait_ge(sem["xr_out"], SEED + 16 * B)
                sp.wait_ge(sem["route_out"], SEED + 16 * B)
                sp.wait_ge(sem["out"], SEED + 16 * B)

            @block.gpsimd
            def _(pool):
                with pool.Fori(0, B) as i:
                    pool.wait_ge(sem["stats"], after(i, 2, 0))
                    pool.tensor_tensor(RD[:, 0:TT], VE[:, 0:TT], POWT[:, 0:TT], ALU.pow).then_inc(sem["rstd"], 1)
                    pool.wait_ge(sem["stats"], after(i, 2, 1))
                    pool.tensor_tensor(RD[:, TT:3 * TT], VE[:, TT:3 * TT], POWT[:, :], ALU.pow).then_inc(sem["rstd"], 1)

            @block.scalar
            def _(act):
                act.wait_ge(sem["const"], SEED + 16 * 9)
                act.activation(TG[:, :], GT[:, :], ACT.Tanh).then_inc(sem["tanh"], 1)
                with act.Fori(0, B) as i:
                    for m, (kind, k) in enumerate(jobs):
                        if banks.engine[m] != "act":
                            continue
                        w = pW[m % 2]
                        act.wait_ge(sem["full"], after(i, len(jobs), m))
                        if kind == "x":
                            act.activation(XBT[:, k, :], w[:, :], ACT.Identity, bias=LNB[:, k:k + 1], scale=LNW[:, k:k + 1]).then_inc(sem["act_empty"], 1)
                        if kind == "q":
                            act.mul(QT[:, k, :], w[:, :], SCALE).then_inc(sem["act_empty"], 1)
                        if kind == "k":
                            act.copy(KT[0:64, k, 0, :], w[0:64, :])
                            act.copy(KT[64:128, k, 1, :], w[64:128, :]).then_inc(sem["act_empty"], 1)
                        if kind == "v":
                            act.copy(V[:, k, :], w[:, :])
                            act.copy(VL[:, k, :], w[64:128, :]).then_inc(sem["act_empty"], 1)
                    n = lambda k: after(i, U, k)
                    for r in range(U + 2):
                        if r < U:
                            act.wait_ge(sem["negmax"], n(r))
                            act.wait_ge(sem["pturn"], n(r - 2))
                            for v in range(2):
                                last = act.activation(PR[:, r % 2, v, :], pS[r % 2][:, 256 * v:256 * v + 192], ACT.Exp,
                                                      bias=NM[:, r % 2, v:v + 1], accum_out=SM[:, r % 2, v:v + 1])
                            last.then_inc(sem["probs"], 1)
                        if 1 <= r <= U:
                            q = (r - 1) % 2
                            act.wait_ge(sem["pturn"], n(r - 1))
                            act.wait_ge(sem["outT"], n(r - 3))
                            act.copy(PTM[:, q, :, :], pP[0][:, 0:256].rearrange("p (v n) -> p v n", v=2)).then_inc(sem["pmain"], 1)
                        if r >= 2 and (r - 2) % TT == TT - 1:
                            j = (r - 2) // TT
                            act.wait_ge(sem["outT"], n(r - 2))
                            act.copy(OT[:, j, :], pO[j % 2][:, :]).then_inc(sem["outTcopy"], 1)

            @block.vector
            def _(dve):
                dve.memset(POWT[:, :], -0.5).then_inc(sem["zero"], 1)
                dve.memset(KT[:, :, :, :], 0.0).then_inc(sem["zero"], 1)
                dve.wait_ge(sem["const"], SEED + 16 * 9)
                dve.wait_ge(sem["zero"], SEED + 2)
                PER = 6 + U
                with dve.Fori(0, B) as i:
                    steps = Steps(i, PER)

                    def norm(src, dst, at, e):
                        for t in range(TT):
                            last = dve.bn_stats(BN[:, t, :], src[:, t, :])
                        last.then_inc(sem["step"], 1)
                        dve.wait_ge(sem["step"], steps.next())
                        dve.memset(VE[:, 0:1], 0.0)
                        for t in range(TT):
                            last = dve.bn_aggr(MV[:, at + t, :], BN[:, t, :])
                        last.then_inc(sem["step"], 1)
                        dve.wait_ge(sem["step"], steps.next())
                        if e:
                            dve.tensor_tensor(MV[:, 2 * TT:3 * TT, 0], MV[:, at:at + TT, 0], MV[:, at:at + TT, 0], ALU.mult).then_inc(sem["step"], 1)
                            dve.wait_ge(sem["step"], steps.next())
                            dve.tensor_tensor(MV[:, 2 * TT:3 * TT, 1], MV[:, 2 * TT:3 * TT, 0], MV[:, at:at + TT, 1], ALU.add).then_inc(sem["step"], 1)
                            dve.wait_ge(sem["step"], steps.next())
                            dve.tensor_scalar(VE[:, 2 * TT:3 * TT], MV[:, 2 * TT:3 * TT, 1], 1e-24 / D, None, ALU.max)
                        dve.tensor_scalar(VE[:, at:at + TT], MV[:, at:at + TT, 1], EPS, None, ALU.add).then_inc(sem["stats"], 1)
                        dve.wait_ge(sem["rstd"], after(i, 2, e))
                        for t in range(TT):
                            last = dve.tensor_scalar(dst[:, t, :], src[:, t, :], MV[:, at + t, 0:1], RD[:, at + t:at + t + 1], ALU.subtract, ALU.mult)
                        return last

                    dve.wait_ge(sem["loaded"], i * 16 + (SEED + 16))
                    norm(X, XA, 0, 0).then_inc(sem["read"], 1)
                    dve.wait_ge(sem["read"], after(i, 1, 0))
                    dve.wait_ge(sem["full"], after(i, len(jobs), NX[-1] - len(jobs)))
                    norm(XA, XB, TT, 1).then_inc(sem["norm"], 1)
                    dve.wait_ge(sem["xr_out"], i * 16 + SEED)
                    for t in range(TT):
                        last = dve.tensor_scalar(XR[:, t, :], XA[:, t, :], RD[:, 2 * TT + t:2 * TT + t + 1], None, ALU.mult)
                    last.then_inc(sem["xr"], 1)
                    dve.wait_ge(sem["route_out"], i * 16 + SEED)
                    dve.wait_ge(sem["s"], after(i, 1, -1))
                    for t in range(TT):
                        for r in range(2):
                            last = dve.tensor_tensor_reduce(out=SCR[:, :].unsqueeze(1), in0=XA[:, t, :].unsqueeze(1), in1=RT[:, r, :].unsqueeze(1), scale=1.0, scalar=0.0,
                                                            op0=ALU.mult, op1=ALU.add, accum_out=SS[:, r, t:t + 1])
                            if not (t == TT - 1 and r == 1):
                                last.then_inc(sem["rows"], 1)
                                dve.wait_ge(sem["rows"], after(i, 7, t * 2 + r))
                    last.then_inc(sem["s"], 1)

                    def empty(m):
                        kind, k = jobs[m]
                        w = pW[m % 2]
                        dve.wait_ge(sem["full"], after(i, len(jobs), m))
                        if kind == "x":
                            dve.tensor_scalar(XBT[:, k, :], w[:, :], LNW[:, k:k + 1], LNB[:, k:k + 1], ALU.mult, ALU.add).then_inc(sem["dve_empty"], 1)
                        if kind == "q":
                            dve.tensor_scalar(QT[:, k, :], w[:, :], SCALE, None, ALU.mult).then_inc(sem["dve_empty"], 1)
                        if kind == "k":
                            dve.tensor_copy(KT[0:64, k, 0, :], w[0:64, :])
                            dve.tensor_copy(KT[64:128, k, 1, :], w[64:128, :]).then_inc(sem["dve_empty"], 1)
                        if kind == "v":
                            dve.tensor_copy(V[:, k, :], w[:, :])
                            dve.tensor_copy(VL[:, k, :], w[64:128, :]).then_inc(sem["dve_empty"], 1)
                        if kind == "o":
                            dve.scalar_tensor_tensor(out=Y[:, k, :], in0=w[:, :], scalar=TG[:, 2:3], in1=XL[:, k, :],
                                                     op0=ALU.mult, op1=ALU.add).then_inc(sem["dve_empty"], 1)

                    for m in range(NO[0]):
                        if banks.engine[m] == "dve":
                            empty(m)
                    n = lambda k: after(i, U, k)
                    for r in range(U + 1):
                        if r < U:
                            dve.wait_ge(sem["scores"], n(r))
                            dve.wait_ge(sem["probs"], n(r - 2))
                            dve.tensor_reduce(NM[:, r % 2, :], pS[r % 2][:, :].rearrange("p (v n) -> p v n", v=2)[:, :, 0:192],
                                              axis=AX.X, op=ALU.max, negate=True).then_inc(sem["negmax"], 1)
                        if r >= 1:
                            q = (r - 1) % 2
                            dve.wait_ge(sem["probs"], n(r - 1))
                            dve.reciprocal(RI[:, q, :], SM[:, q, :]).then_inc(sem["step"], 1)
                            dve.wait_ge(sem["step"], steps.next())
                            for v in range(2):
                                last = dve.tensor_scalar(PR[:, q, v, :], PR[:, q, v, :], RI[:, q, v:v + 1], None, ALU.mult)
                            last.then_inc(sem["scaled"], 1)
                        if r >= 1:
                            dve.wait_ge(sem["pturn"], n(r - 1))
                            dve.wait_ge(sem["outT"], n(r - 3))
                            dve.tensor_copy(PTE[:, q, :, :], pP[1][0:64, 0:256].rearrange("p (v n) -> p v n", v=2)).then_inc(sem["pextra"], 1)
                    steps.close()
                    dve.wait_ge(sem["tanh"], SEED + 1)
                    dve.wait_ge(sem["resid"], i * 16 + (SEED + 16))
                    dve.wait_ge(sem["out"], i * 16 + SEED)
                    for m in NO:
                        empty(m)

            @block.tensor
            def _(pe):
                pe.wait_ge(sem["const"], SEED + 16 * 9)
                pe.wait_ge(sem["zero"], SEED + 2)
                with pe.Fori(0, B) as i:
                    def ready(m):
                        for e in ("act", "dve"):
                            pe.wait_ge(emptied[e], banks.emptied(i, m, e))

                    def free(m):
                        before = banks.engine[(m - 2) % len(jobs)]
                        pe.wait_ge(emptied[before], banks.emptied(i, m - 2, before))

                    for m, (kind, k) in enumerate(jobs):
                        if kind == "o":
                            continue
                        if kind == "x" and k == 0:
                            pe.wait_ge(sem["norm"], after(i, 1, 0))
                        if kind == "q" and k == 0:
                            ready(NX[-1])
                        free(m)
                        w = pW[m % 2]
                        for c in range(4):
                            if kind == "x":
                                last = pe.transpose(w[:, P * c:P * c + P], XB[:, c, P * k:P * k + P], IDF[:, :])
                            if kind in "qk":
                                o = (kind == "k") * D + P * k
                                last = pe.matmul(w[:, :], WQKV[:, c, o:o + P], XBT[:, c, :], start=c == 0, stop=c == 3)
                            if kind == "v":
                                last = pe.matmul(w[:, :], XBT[:, c, P * k:P * k + P], WQKV[:, c, 2 * D:3 * D], start=c == 0, stop=c == 3)
                        last.then_inc(sem["full"], 1)
                    ready(NVV[-1])
                    n = lambda k: after(i, U, k)
                    for r in range(U + 2):
                        if r < U:
                            j, t = r // TT, r % TT
                            pe.wait_ge(sem["probs"], n(r - 2))
                            for v in range(2):
                                o = 256 * v
                                pe.matmul(pS[r % 2][:, o:o + P], QT[:, j, P * t:P * t + P], KT[:, j, v, P * t:P * t + P], start=True, stop=True)
                                if t == 0:
                                    pe.matmul(pS[r % 2][0:64, o + P:o + 192], IDB[:, 0:64], NEGB[:, :], start=True, stop=True)
                                else:
                                    pe.matmul(pS[r % 2][0:64, o + P:o + 192], QT[:, j, P * t:P * t + 64], KT[:, j, v, P * t - 64:P * t], start=True, stop=True)
                                if t == TT - 1:
                                    last = pe.matmul(pS[r % 2][64:128, o + P:o + 192], IDB[:, 64:128], NEGB[:, :], start=True, stop=True)
                                else:
                                    last = pe.matmul(pS[r % 2][64:128, o + P:o + 192], QT[:, j, P * t + 64:P * t + P],
                                                     KT[:, j, v, P * t + P:P * t + 192], start=True, stop=True)
                            last.then_inc(sem["scores"], 1)
                        if 1 <= r <= U:
                            q = (r - 1) % 2
                            pe.wait_ge(sem["scaled"], n(r - 1))
                            pe.wait_ge(sem["pmain"], n(r - 2))
                            pe.wait_ge(sem["pextra"], n(r - 2))
                            for v in range(2):
                                pe.transpose(pP[0][:, P * v:P * v + P], PR[:, q, v, 0:P], IDF[:, :])
                                last = pe.transpose(pP[1][0:64, P * v:P * v + P], PR[:, q, v, P:192], IDF[:, :])
                            last.then_inc(sem["pturn"], 1)
                        if r >= 2:
                            q = r % 2
                            j, t = (r - 2) // TT, (r - 2) % TT
                            pe.wait_ge(sem["pmain"], n(r - 2))
                            pe.wait_ge(sem["pextra"], n(r - 2))
                            if t == 0:
                                pe.wait_ge(sem["outTcopy"], after(i, J, j - 2))
                            for v in range(2):
                                h = 2 * j + v
                                vc = slice(64 * h, 64 * h + 64)
                                dst = pO[j % 2][64 * v:64 * v + 64, P * t:P * t + P]
                                last = pe.matmul(dst, V[:, t, vc], PTM[:, q, v, :], start=True, stop=False, skip_group_check=True)
                                if t > 0:
                                    last = pe.matmul(dst[:, 0:64], VL[:, t - 1, vc], PTE[:, q, v, 0:64], start=False, stop=t == TT - 1, skip_group_check=True)
                                if t < TT - 1:
                                    last = pe.matmul(dst[:, 64:P], V[0:64, t + 1, vc], PTE[:, q, v, 64:P], start=False, stop=True, skip_group_check=True)
                            last.then_inc(sem["outT"], 1)
                    pe.wait_ge(sem["outTcopy"], after(i, J, J - 1))
                    for m in NO:
                        k = jobs[m][1]
                        free(m)
                        for c in range(4):
                            last = pe.matmul(pW[m % 2][:, :], OT[:, c, P * k:P * k + P], WO[:, c, :], start=c == 0, stop=c == 3)
                        last.then_inc(sem["full"], 1)


def phase_route(nc, keep, a, s_route, sel):
    NQ, ITERS = 256, 50
    K_OF = (min(256 * 9.0 / 8.0, float(S)), min(512 * 9.0 / 8.0, float(S)))
    R2 = 2 * B
    with ExitStack() as ctx:
        def sb(name, shape, dt=f32):
            return ctx.enter_context(nc.sbuf_tensor("r_" + name, shape, dt))

        names = ["const", "loaded", "turned", "copied", "step", "low", "sum", "log", "kth", "expd", "rows", "turned2", "out", "stored"]
        sem = open_phase(nc, keep, ["r_" + n for n in names])
        sem = {n: sem["r_" + n] for n in names}
        SA = sb("sa", [P, B, 2, TT])
        SG = sb("sg", [P, TT, R2])
        IDF, LK = sb("idf", [P, P]), sb("lk", [R2, 2])
        SR, T, E = sb("sr", [R2, S]), sb("t", [R2, S]), sb("e", [R2, S])
        SMX, NA, ML, SU, LG = (sb(n, [R2, 1]) for n in ("smx", "na", "ml", "su", "lg"))
        WK, M8, OUTW, OUTN = sb("wk", [R2, S]), sb("m8", [R2, 8]), sb("outw", [R2, S]), sb("outn", [R2, S])
        TMP, SEL = sb("tmp", [R2, S]), sb("sel", [P, TT, 3 * B])
        ps = [ctx.enter_context(nc.psum_tensor(f"r_ps{i}", [P, 512], f32)) for i in range(2)]
        with nc.Block() as block:
            @block.sync
            def _(sp):
                sp.dma_start(IDF[:, :], a["idf"]).then_inc(sem["const"], 16)
                sp.dma_start(LK[:, :], a["logk"]).then_inc(sem["const"], 16)
                sp.dma_start(SA[:, :, :, :].rearrange("p b r t -> p b (r t)"), s_route.rearrange("b p n -> p b n")).then_inc(sem["loaded"], 16)
                sp.wait_ge(sem["out"], SEED + 1)
                sp.dma_start(sel, SEL[:, :, :]).then_inc(sem["stored"], 16)
                sp.wait_ge(sem["stored"], SEED + 16)

            @block.tensor
            def _(pe):
                pe.wait_ge(sem["const"], SEED + 32)
                pe.wait_ge(sem["copied"], SEED + 1)
                for t in range(TT):
                    last = pe.transpose(ps[0][0:R2, P * t:P * t + P], SG[:, t, :], IDF[:, :])
                last.then_inc(sem["turned"], 1)
                pe.wait_ge(sem["rows"], SEED + 1)
                pe.wait_ge(sem["copied"], SEED + 2)
                for t in range(TT):
                    pe.transpose(ps[1][:, 24 * t:24 * t + R2], OUTW[:, P * t:P * t + P], IDF[0:R2, 0:R2])
                    last = pe.transpose(ps[1][:, 24 * t + R2:24 * t + 24], OUTN[0:B, P * t:P * t + P], IDF[0:B, 0:B])
                last.then_inc(sem["turned2"], 1)

            @block.scalar
            def _(act):
                with act.Fori(0, ITERS - 1) as i:
                    act.wait_ge(sem["low"], after(i, 1, 0))
                    act.activation(E[:, :], T[:, :], ACT.Exp, bias=ML[:, 0:1], accum_out=SU[:, 0:1]).then_inc(sem["sum"], 1)
                    act.wait_ge(sem["sum"], after(i, 1, 0))
                    act.activation(LG[:, :], SU[:, :], ACT.Ln).then_inc(sem["log"], 1)
                act.wait_ge(sem["kth"], SEED + 1)
                act.activation(E[:, :], T[:, :], ACT.Exp).then_inc(sem["expd"], 1)

            @block.vector
            def _(dve):
                dve.wait_ge(sem["loaded"], SEED + 16)
                dve.tensor_copy(SG[:, :, :].rearrange("p t (r b) -> p t r b", r=2), SA[:, :, :, :].rearrange("p b r t -> p t r b")).then_inc(sem["copied"], 1)
                dve.wait_ge(sem["turned"], SEED + 1)
                dve.tensor_copy(SR[:, :], ps[0][0:R2, :]).then_inc(sem["copied"], 1)
                dve.wait_ge(sem["copied"], SEED + 2)
                dve.reduce_max(SMX[:, :], SR[:, :], axis=AX.X)
                dve.wait_ge(sem["const"], SEED + 32)
                dve.tensor_copy(NA[:, :], LK[:, 1:2]).then_inc(sem["step"], 1)
                dve.wait_ge(sem["step"], SEED + 1)
                with dve.Fori(0, ITERS - 1) as i:
                    dve.tensor_scalar(T[:, :], SR[:, :], NA[:, 0:1], None, ALU.min)
                    dve.tensor_scalar(ML[:, :], SMX[:, :], NA[:, 0:1], -1.0, ALU.min, ALU.mult).then_inc(sem["low"], 1)
                    dve.wait_ge(sem["log"], after(i, 1, 0))
                    dve.wait_ge(sem["low"], after(i, 1, 0))
                    dve.tensor_scalar(NA[:, :], LG[:, :], ML[:, 0:1], LK[:, 0:1], ALU.subtract, ALU.subtract).then_inc(sem["step"], 1)
                    dve.wait_ge(sem["step"], after(i, 1, 1))
                dve.tensor_scalar(T[:, :], SR[:, :], NA[:, 0:1], 0.0, ALU.subtract, ALU.min).then_inc(sem["kth"], 1)
                dve.wait_ge(sem["expd"], SEED + 1)
                dve.tensor_scalar(OUTW[:, :], E[:, :], -1.0, 1.0, ALU.mult, ALU.add)
                dve.tensor_copy(WK[:, :], E[:, :]).then_inc(sem["step"], 1)
                dve.wait_ge(sem["step"], SEED + ITERS + 1)
                dve.tensor_tensor(OUTW[:, :], OUTW[:, :], E[:, :], ALU.add)
                k = ITERS + 1
                for r in range(NQ // 8):
                    dve.max(M8[:, :], WK[:, :]).then_inc(sem["step"], 1)
                    k += 1
                    dve.wait_ge(sem["step"], SEED + k)
                    dve.match_replace(WK[:, :], M8[:, :], WK[:, :], -1.0).then_inc(sem["step"], 1)
                    k += 1
                    dve.wait_ge(sem["step"], SEED + k)
                dve.tensor_scalar(OUTN[0:B, :], WK[0:B, :], 0.0, None, ALU.is_ge)
                dve.tensor_scalar(TMP[0:B, :], WK[0:B, :], 0.0, None, ALU.is_lt).then_inc(sem["step"], 1)
                dve.wait_ge(sem["step"], SEED + k + 1)
                dve.tensor_tensor(OUTW[0:B, :], OUTW[0:B, :], TMP[0:B, :], ALU.mult).then_inc(sem["rows"], 1)
                dve.wait_ge(sem["turned2"], SEED + 1)
                dve.tensor_copy(SEL[:, :, :], ps[1][:, 0:24 * TT].rearrange("p (t n) -> p t n", n=24)).then_inc(sem["out"], 1)


def phase_heavy(nc, keep, a, xr, x1l, sel, x2):
    H, DH = 8, 64
    SCALE = DH ** -0.5
    J = 4
    U = H * TT
    jobs = [("x", c) for c in range(4)] + [("q", j) for j in range(4)] + [("k", j) for j in range(4)] + \
           [("v", t) for t in range(4)] + [("n", 0)] + [("z", j) for j in range(4)] + [("o", t) for t in range(4)]
    banks = Banks(jobs, lambda m, job: "dve" if job[0] in "on" else "act" if job[0] == "z" else ("act", "dve")[m % 2])
    NX, NQ, NK, NVV, NN, NZ, NO = (banks.of(k) for k in "xqkvnzo")
    with ExitStack() as ctx:
        def sb(name, shape, dt=f32):
            return ctx.enter_context(nc.sbuf_tensor("h_" + name, shape, dt))

        names = ["const", "loaded", "resid", "tanh", "zero", "full", "act_empty", "dve_empty", "scores", "negmax", "probs",
                 "scaled", "pturn", "pcopy", "outT", "outTcopy", "step", "out", "weights", "nullp"]
        sem = open_phase(nc, keep, ["h_" + n for n in names])
        sem = {n: sem["h_" + n] for n in names}
        emptied = {"act": sem["act_empty"], "dve": sem["dve_empty"]}
        WQ, WK, WV, WO = (sb(n, [P, CT, D]) for n in ("wq", "wk", "wv", "wo"))
        GA, NKB, NVB, NQB = sb("ga", [P, CT]), sb("nkb", [P, J, 2]), sb("nvb", [P, J, P]), sb("nqb", [P, D])
        SEL, TSEL = sb("sel", [P, TT, 3 * B]), sb("tsel", [P, TT, 3 * B])
        IDF = sb("idf", [P, P])
        GT, TG = sb("gt", [P, 4]), sb("tg", [P, 4])
        X, XL = sb("x", [P, TT, D]), sb("xl", [P, TT, D])
        XT = sb("xT", [P, CT, S])
        QT, KT, V = sb("qT", [P, J, S]), sb("kT", [P, J, 2, S]), sb("v", [P, TT, D])
        WCOL = sb("wcol", [P, TT, 3])
        NS = sb("ns", [P, TT, H])
        PR, PT = sb("pr", [P, 2, S]), sb("pT", [P, 2, TT, S])
        SC = sb("sc", [P, 2, 8])
        PN, PNT = sb("pn", [P, 2, TT, P]), sb("pnT", [P, S])
        OT, Y = sb("oT", [P, J, S]), sb("y", [P, TT, D])
        bank = [ctx.enter_context(nc.psum_tensor(f"h_ps{i}", [P, 512], f32)) for i in range(8)]
        pW, pS, pP, pO = bank[0:2], bank[2:4], bank[4:6], bank[6:8]

        with nc.Block() as block:
            @block.sync
            def _(sp):
                for dst, src in ((WQ[:, :, :], a["hwqT"]), (WK[:, :, :], a["hwkT"]), (WV[:, :, :], a["hwvT"]), (WO[:, :, :], a["hwoT"]),
                                 (GA[:, :], a["gamma"]), (NKB[:, :, :], a["null_k"]), (NVB[:, :, :], a["null_v"]), (NQB[:, :], a["null_q"]),
                                 (SEL[:, :, :], sel), (IDF[:, :], a["idf"]), (GT[:, :], a["gates"])):
                    sp.dma_start(dst, src).then_inc(sem["const"], 16)
                with sp.Fori(0, B) as i:
                    row = lambda t: t[bass.ds(i, 1), :, :].rearrange("o (t p) d -> p (o t) d", p=P)
                    sp.wait_ge(sem["full"], after(i, len(jobs), NX[-1] - len(jobs)))
                    sp.dma_start(X[:, :, :], row(xr)).then_inc(sem["loaded"], 16)
                    sp.wait_ge(sem["dve_empty"], banks.emptied(i, -1, "dve"))
                    sp.dma_start(XL[:, :, :], row(x1l)).then_inc(sem["resid"], 16)
                    sp.wait_ge(sem["dve_empty"], banks.emptied(i, NO[-1], "dve"))
                    sp.dma_start(row(x2), Y[:, :, :]).then_inc(sem["out"], 16)
                sp.wait_ge(sem["out"], SEED + 16 * B)

            @block.scalar
            def _(act):
                act.wait_ge(sem["const"], SEED + 16 * 11)
                act.activation(TG[:, :], GT[:, :], ACT.Tanh).then_inc(sem["tanh"], 1)
                with act.Fori(0, B) as i:
                    def empty(m):
                        kind, k = jobs[m]
                        w = pW[m % 2]
                        act.wait_ge(sem["full"], after(i, len(jobs), m))
                        if kind == "x":
                            act.mul(XT[:, k, :], w[:, :], GA[:, k:k + 1]).then_inc(sem["act_empty"], 1)
                        if kind == "q":
                            act.mul(QT[:, k, :], w[:, :], SCALE).then_inc(sem["act_empty"], 1)
                        if kind == "k":
                            act.copy(KT[0:64, k, 0, :], w[0:64, :])
                            act.copy(KT[64:128, k, 1, :], w[64:128, :]).then_inc(sem["act_empty"], 1)
                        if kind == "v":
                            act.wait_ge(sem["weights"], after(i, 1, 0))
                            act.mul(V[:, k, :], w[:, :], WCOL[:, k, 1:2]).then_inc(sem["act_empty"], 1)
                        if kind == "z":
                            act.copy(PNT[:, :], w[:, :]).then_inc(sem["act_empty"], 1)

                    for m in range(NN[0]):
                        if banks.engine[m] == "act":
                            empty(m)
                    n = lambda k: after(i, U, k)
                    for r in range(U + 3):
                        if r < U:
                            h, t = r // TT, r % TT
                            act.wait_ge(sem["negmax"], n(r))
                            act.wait_ge(sem["pturn"], n(r - 2))
                            act.activation(PR[:, r % 2, :], pS[r % 2][:, :], ACT.Exp, bias=SC[:, r % 2, 0:1], accum_out=SC[:, r % 2, 1:2])
                            act.activation(SC[:, r % 2, 2:3], NS[:, t, h:h + 1], ACT.Exp, bias=SC[:, r % 2, 0:1]).then_inc(sem["probs"], 1)
                        if 1 <= r <= U:
                            h, t = (r - 1) // TT, (r - 1) % TT
                            act.wait_ge(sem["pturn"], n(r - 1))
                            act.wait_ge(sem["outT"], after(i, H, h - 2))
                            act.copy(PT[:, h % 2, :, P * t:P * t + P], pP[(r - 1) % 2][:, :].rearrange("p (k q) -> p k q", k=TT)).then_inc(sem["pcopy"], 1)
                        if r >= 3 and (r - 3) % (2 * TT) == 2 * TT - 1:
                            j = (r - 3) // (2 * TT)
                            empty(NZ[j])
                            act.wait_ge(sem["outT"], after(i, H, 2 * j + 1))
                            act.copy(OT[:, j, :], pO[j % 2][:, :]).then_inc(sem["outTcopy"], 1)

            @block.vector
            def _(dve):
                dve.memset(PN[:, :, :, :], 0.0).then_inc(sem["zero"], 1)
                dve.memset(KT[:, :, :, :], 0.0).then_inc(sem["zero"], 1)
                dve.wait_ge(sem["const"], SEED + 16 * 11)
                dve.wait_ge(sem["tanh"], SEED + 1)
                dve.wait_ge(sem["zero"], SEED + 2)
                dve.tensor_scalar(TSEL[:, :, :], SEL[:, :, :], TG[:, 2:3], None, ALU.mult).then_inc(sem["zero"], 1)
                dve.wait_ge(sem["zero"], SEED + 3)
                PER = 3 * U + TT
                with dve.Fori(0, B) as i:
                    steps = Steps(i, PER)
                    dve.wait_ge(sem["dve_empty"], banks.emptied(i, -1, "dve"))
                    dve.tensor_copy(WCOL[:, :, 0], TSEL[:, :, bass.ds(i, 1)].rearrange("p t o -> p (t o)"))
                    dve.tensor_copy(WCOL[:, :, 1], SEL[:, :, bass.ds(i + B, 1)].rearrange("p t o -> p (t o)"))
                    dve.tensor_copy(WCOL[:, :, 2], TSEL[:, :, bass.ds(i + 2 * B, 1)].rearrange("p t o -> p (t o)")).then_inc(sem["weights"], 1)
                    dve.wait_ge(sem["weights"], after(i, 1, 0))

                    def empty(m):
                        kind, k = jobs[m]
                        w = pW[m % 2]
                        dve.wait_ge(sem["full"], after(i, len(jobs), m))
                        if kind == "x":
                            dve.tensor_scalar(XT[:, k, :], w[:, :], GA[:, k:k + 1], None, ALU.mult).then_inc(sem["dve_empty"], 1)
                        if kind == "q":
                            dve.tensor_scalar(QT[:, k, :], w[:, :], SCALE, None, ALU.mult).then_inc(sem["dve_empty"], 1)
                        if kind == "k":
                            dve.tensor_copy(KT[0:64, k, 0, :], w[0:64, :])
                            dve.tensor_copy(KT[64:128, k, 1, :], w[64:128, :]).then_inc(sem["dve_empty"], 1)
                        if kind == "v":
                            dve.tensor_scalar(V[:, k, :], w[:, :], WCOL[:, k, 1:2], None, ALU.mult).then_inc(sem["dve_empty"], 1)
                        if kind == "n":
                            dve.tensor_copy(NS[:, :, :], w[:, 0:TT * H].rearrange("p (t h) -> p t h", h=H)).then_inc(sem["dve_empty"], 1)
                        if kind == "o":
                            dve.scalar_tensor_tensor(out=Y[:, k, :], in0=w[:, :], scalar=WCOL[:, k, 0:1], in1=XL[:, k, :],
                                                     op0=ALU.mult, op1=ALU.add).then_inc(sem["step"], 1)
                            dve.wait_ge(sem["step"], steps.next())
                            dve.scalar_tensor_tensor(out=Y[:, k, :], in0=NQB[:, :], scalar=WCOL[:, k, 2:3], in1=Y[:, k, :],
                                                     op0=ALU.mult, op1=ALU.add).then_inc(sem["dve_empty"], 1)

                    for m in range(NZ[0]):
                        if banks.engine[m] == "dve":
                            empty(m)
                    dve.wait_ge(sem["dve_empty"], banks.emptied(i, NN[0], "dve"))
                    n = lambda k: after(i, U, k)
                    for r in range(U + 1):
                        if r < U:
                            h, t = r // TT, r % TT
                            dve.wait_ge(sem["scores"], n(r))
                            dve.wait_ge(sem["scaled"], n(r - 2))
                            dve.reduce_max(SC[:, r % 2, 4:5], pS[r % 2][:, :], axis=AX.X).then_inc(sem["step"], 1)
                            dve.wait_ge(sem["step"], steps.next())
                            dve.tensor_scalar(SC[:, r % 2, 0:1], SC[:, r % 2, 4:5], NS[:, t, h:h + 1], -1.0, ALU.max, ALU.mult).then_inc(sem["negmax"], 1)
                        if r >= 1:
                            q = (r - 1) % 2
                            h, t = (r - 1) // TT, (r - 1) % TT
                            dve.wait_ge(sem["probs"], n(r - 1))
                            dve.tensor_scalar(SC[:, q, 5:6], SC[:, q, 1:2], SC[:, q, 2:3], None, ALU.add).then_inc(sem["step"], 1)
                            dve.wait_ge(sem["step"], steps.next())
                            dve.reciprocal(SC[:, q, 3:4], SC[:, q, 5:6]).then_inc(sem["step"], 1)
                            dve.wait_ge(sem["step"], steps.next())
                            if t == 0 and h % 2 == 0:
                                dve.wait_ge(sem["full"], after(i, len(jobs), (NZ[h // 2 - 2] if h >= 4 else NZ[h // 2 + 2] - len(jobs))))
                            dve.tensor_scalar(PN[:, h // 2 % 2, t, h:h + 1], SC[:, q, 2:3], SC[:, q, 3:4], None, ALU.mult)
                            dve.tensor_scalar(PR[:, q, :], PR[:, q, :], SC[:, q, 3:4], None, ALU.mult).then_inc(sem["scaled"], 1)
                    dve.wait_ge(sem["resid"], i * 16 + (SEED + 16))
                    dve.wait_ge(sem["out"], i * 16 + SEED)
                    for m in NO:
                        empty(m)
                    steps.close()

            @block.tensor
            def _(pe):
                pe.wait_ge(sem["const"], SEED + 16 * 11)
                pe.wait_ge(sem["zero"], SEED + 2)
                with pe.Fori(0, B) as i:
                    def ready(m):
                        for e in ("act", "dve"):
                            pe.wait_ge(emptied[e], banks.emptied(i, m, e))

                    def free(m):
                        before = banks.engine[(m - 2) % len(jobs)]
                        pe.wait_ge(emptied[before], banks.emptied(i, m - 2, before))

                    for m in range(NZ[0]):
                        kind, k = jobs[m]
                        if kind == "x" and k == 0:
                            pe.wait_ge(sem["loaded"], i * 16 + (SEED + 16))
                        if kind == "q" and k == 0:
                            ready(NX[-1])
                        if kind == "n":
                            ready(NQ[-1])
                        free(m)
                        w = pW[m % 2]
                        for c in range(4):
                            if kind == "x":
                                last = pe.transpose(w[:, P * c:P * c + P], X[:, c, P * k:P * k + P], IDF[:, :])
                            if kind in "qk":
                                last = pe.matmul(w[:, :], (WQ if kind == "q" else WK)[:, c, P * k:P * k + P], XT[:, c, :], start=c == 0, stop=c == 3)
                            if kind == "v":
                                last = pe.matmul(w[:, :], XT[:, c, P * k:P * k + P], WV[:, c, :], start=c == 0, stop=c == 3)
                            if kind == "n":
                                for j in range(J):
                                    last = pe.matmul(w[:, H * c + 2 * j:H * c + 2 * j + 2], QT[:, j, P * c:P * c + P], NKB[:, j, :], start=True, stop=True)
                        last.then_inc(sem["full"], 1)
                    ready(NVV[-1])
                    n = lambda k: after(i, U, k)
                    for r in range(U + 3):
                        if r < U:
                            h, t = r // TT, r % TT
                            pe.wait_ge(sem["probs"], n(r - 2))
                            pe.matmul(pS[r % 2][:, :], QT[:, h // 2, P * t:P * t + P], KT[:, h // 2, h % 2, :], start=True, stop=True).then_inc(sem["scores"], 1)
                        if 1 <= r <= U:
                            q = (r - 1) % 2
                            pe.wait_ge(sem["scaled"], n(r - 1))
                            pe.wait_ge(sem["pcopy"], n(r - 3))
                            for k in range(TT):
                                last = pe.transpose(pP[q][:, P * k:P * k + P], PR[:, q, P * k:P * k + P], IDF[:, :])
                            last.then_inc(sem["pturn"], 1)
                        if r >= 3 and (r - 3) % TT == TT - 1:
                            h = (r - 3) // TT
                            j, v = h // 2, h % 2
                            if v == 1:
                                free(NZ[j])
                                for t in range(TT):
                                    last = pe.transpose(pW[NZ[j] % 2][:, P * t:P * t + P], PN[:, j % 2, t, :], IDF[:, :])
                                last.then_inc(sem["full"], 1)
                            pe.wait_ge(sem["pcopy"], n(TT * h + TT - 1))
                            if v == 0:
                                pe.wait_ge(sem["outTcopy"], after(i, J, j - 2))
                            for k in range(TT):
                                last = pe.matmul(pO[j % 2][64 * v:64 * v + 64, :], V[:, k, 64 * h:64 * h + 64], PT[:, h % 2, k, :],
                                                 start=k == 0, stop=False, skip_group_check=True)
                            if v == 1:
                                pe.wait_ge(emptied["act"], banks.emptied(i, NZ[j], "act"))
                                last = pe.matmul(pO[j % 2][:, :], NVB[:, j, :], PNT[:, :], start=False, stop=True, skip_group_check=True)
                            last.then_inc(sem["outT"], 1)
                    pe.wait_ge(sem["outTcopy"], after(i, J, J - 1))
                    for m in NO:
                        k = jobs[m][1]
                        free(m)
                        for c in range(4):
                            last = pe.matmul(pW[m % 2][:, :], OT[:, c, P * k:P * k + P], WO[:, c, :], start=c == 0, stop=c == 3)
                        last.then_inc(sem["full"], 1)


def phase_window(nc, keep, a, x2, x3):
    H, DH = 16, 32
    SCALE = DH ** -0.5
    J = 4
    U = H * TT
    jobs = [("x", c) for c in range(4)] + [("q", j) for j in range(4)] + [("k", j) for j in range(4)] + \
           [("v", t) for t in range(4)] + [("o", t) for t in range(4)]
    banks = Banks(jobs, lambda m, job: "dve" if job[0] in "vo" else "act")
    NX, NQ, NK, NVV, NO = (banks.of(k) for k in "xqkvo")

    def tiles(t):
        return min(t + 1, 3)
    with ExitStack() as ctx:
        def sb(name, shape, dt=f32):
            return ctx.enter_context(nc.sbuf_tensor("c_" + name, shape, dt))

        names = ["const", "loaded", "resid", "ctx", "tanh", "zero", "read", "stats", "rstd", "norm", "full", "act_empty", "dve_empty",
                 "scores", "negmax", "probs", "scaled", "pturn", "pcopy", "outT", "outTcopy", "step", "out", "biased", "once"]
        sem = open_phase(nc, keep, ["c_" + n for n in names])
        sem = {n: sem["c_" + n] for n in names}
        emptied = {"act": sem["act_empty"], "dve": sem["dve_empty"]}
        WQ, WK, WV, WO = (sb(n, [P, CT, D]) for n in ("wq", "wk", "wv", "wo"))
        BQ, BK, BQS, BV, BO = sb("bq", [P, CT]), sb("bk", [P, CT]), sb("bqs", [P, CT]), sb("bv", [P, D]), sb("bo", [P, D])
        IDF, IDB, MASK = sb("idf", [P, P]), sb("idb", [P, P], bf16), sb("mask", [P, 3 * P], bf16)
        GT, TG = sb("gt", [P, 4]), sb("tg", [P, 4])
        X, XL, XB, C = (sb(n, [P, TT, D]) for n in ("x", "xl", "xb", "cT"))
        XT, QT, V = sb("xT", [P, CT, S]), sb("qT", [P, J, S]), sb("v", [P, TT, D])
        KT = sb("kT", [P, J, 4, S])
        BN, MV, VE, RD, POWT = sb("bn", [P, TT, 6]), sb("mv", [P, TT, 2]), sb("ve", [P, TT]), sb("rd", [P, TT]), sb("pow", [P, TT])
        PR, PT = sb("pr", [P, 4, 3 * P]), sb("pT", [P, 2, 3 * P])
        NM, SM, RI = sb("nm", [P, 4]), sb("sm", [P, 4]), sb("ri", [P, 4])
        OT, Y = sb("oT", [P, J, S]), sb("y", [P, TT, D])
        bank = [ctx.enter_context(nc.psum_tensor(f"c_ps{i}", [P, 512], f32)) for i in range(8)]
        pW, pS, pP, pO = bank[0:2], bank[2:4], bank[4:6], bank[6:8]
        with nc.Block() as block:
            @block.sync
            def _(sp):
                for dst, src in ((WQ[:, :, :], a["xwqT"]), (WK[:, :, :], a["xwkT"]), (WV[:, :, :], a["xwvT"]), (WO[:, :, :], a["xwoT"]),
                                 (BQ[:, :], a["xbq"]), (BK[:, :], a["xbk"]), (BV[:, :], a["xbv"]), (BO[:, :], a["xbo"]),
                                 (IDF[:, :], a["idf"]), (IDB[:, :], a["idb"]), (MASK[:, :], a["mask_w"]), (GT[:, :], a["gates"])):
                    sp.dma_start(dst, src).then_inc(sem["const"], 16)
                with sp.Fori(0, B) as i:
                    row = lambda t: t[bass.ds(i, 1), :, :].rearrange("o (t p) d -> p (o t) d", p=P)
                    sp.wait_ge(sem["read"], after(i, 1, -1))
                    sp.dma_start(X[:, :, :], row(x2)).then_inc(sem["loaded"], 16)
                    sp.wait_ge(sem["full"], after(i, len(jobs), NVV[-1] - len(jobs)))
                    sp.dma_start(C[:, :, :], a["ctxT"][bass.ds(i, 1), :, :, :].rearrange("o p c n -> (o p) c n")).then_inc(sem["ctx"], 16)
                    sp.wait_ge(sem["dve_empty"], banks.emptied(i, -1, "dve"))
                    sp.dma_start(XL[:, :, :], row(x2)).then_inc(sem["resid"], 16)
                    sp.wait_ge(sem["dve_empty"], banks.emptied(i, NO[-1], "dve"))
                    sp.dma_start(row(x3), Y[:, :, :]).then_inc(sem["out"], 16)
                sp.wait_ge(sem["out"], SEED + 16 * B)

            @block.gpsimd
            def _(pool):
                pool.wait_ge(sem["once"], SEED + 1)
                with pool.Fori(0, B) as i:
                    pool.wait_ge(sem["stats"], after(i, 1, 0))
                    pool.tensor_tensor(RD[:, :], VE[:, :], POWT[:, :], ALU.pow).then_inc(sem["rstd"], 1)
                    pool.wait_ge(sem["resid"], i * 16 + (SEED + 16))
                    for t in range(TT):
                        last = pool.tensor_tensor(XL[:, t, :], XL[:, t, :], BO[:, :], ALU.add)
                    last.then_inc(sem["biased"], 1)

            @block.scalar
            def _(act):
                act.wait_ge(sem["const"], SEED + 16 * 12)
                act.activation(TG[:, :], GT[:, :], ACT.Tanh).then_inc(sem["tanh"], 1)
                act.mul(BQS[:, :], BQ[:, :], SCALE).then_inc(sem["tanh"], 1)
                act.wait_ge(sem["tanh"], SEED + 2)
                with act.Fori(0, B) as i:
                    for m in range(NVV[0]):
                        kind, k = jobs[m]
                        w = pW[m % 2]
                        act.wait_ge(sem["full"], after(i, len(jobs), m))
                        if kind == "x":
                            last = act.copy(XT[:, k, :], w[:, :])
                        if kind == "q":
                            last = act.activation(QT[:, k, :], w[:, :], ACT.Identity, bias=BQS[:, k:k + 1], scale=SCALE)
                        if kind == "k":
                            for n in range(4):
                                rows = slice(DH * n, DH * n + DH)
                                last = act.activation(KT[rows, k, n, :], w[rows, :], ACT.Identity, bias=BK[rows, k:k + 1])
                        last.then_inc(sem["act_empty"], 1)
                    n = lambda k: after(i, U, k)
                    for r in range(U + 3):
                        if r < U:
                            w = P * tiles(r % TT)
                            act.wait_ge(sem["negmax"], n(r))
                            act.wait_ge(sem["pturn"], n(r - 4))
                            act.activation(PR[:, r % 4, 0:w], pS[r % 2][:, 0:w], ACT.Exp, bias=NM[:, r % 4:r % 4 + 1],
                                           accum_out=SM[:, r % 4:r % 4 + 1]).then_inc(sem["probs"], 1)
                        if 2 <= r < U + 2:
                            w = P * tiles((r - 2) % TT)
                            act.wait_ge(sem["pturn"], n(r - 2))
                            act.wait_ge(sem["outT"], n(r - 4))
                            act.copy(PT[:, r % 2, 0:w], pP[r % 2][:, 0:w]).then_inc(sem["pcopy"], 1)
                        if r >= 3 and (r - 3) % (4 * TT) == 4 * TT - 1:
                            j = (r - 3) // (4 * TT)
                            act.wait_ge(sem["outT"], n(r - 3))
                            act.copy(OT[:, j, :], pO[j % 2][:, :]).then_inc(sem["outTcopy"], 1)

            @block.vector
            def _(dve):
                dve.memset(POWT[:, :], -0.5).then_inc(sem["zero"], 1)
                dve.memset(KT[:, :, :, :], 0.0).then_inc(sem["zero"], 1)
                dve.wait_ge(sem["const"], SEED + 16 * 12)
                dve.wait_ge(sem["tanh"], SEED + 2)
                dve.wait_ge(sem["zero"], SEED + 2)
                dve.tensor_scalar(BO[:, :], BO[:, :], TG[:, 1:2], None, ALU.mult).then_inc(sem["once"], 1)
                PER = 2 + U
                with dve.Fori(0, B) as i:
                    steps = Steps(i, PER)
                    dve.wait_ge(sem["loaded"], i * 16 + (SEED + 16))
                    for t in range(TT):
                        last = dve.bn_stats(BN[:, t, :], X[:, t, :])
                    last.then_inc(sem["step"], 1)
                    dve.wait_ge(sem["step"], steps.next())
                    dve.memset(VE[:, 0:1], 0.0)
                    for t in range(TT):
                        last = dve.bn_aggr(MV[:, t, :], BN[:, t, :])
                    last.then_inc(sem["step"], 1)
                    dve.wait_ge(sem["step"], steps.next())
                    dve.tensor_scalar(VE[:, :], MV[:, :, 1], EPS, None, ALU.add).then_inc(sem["stats"], 1)
                    dve.wait_ge(sem["rstd"], after(i, 1, 0))
                    dve.wait_ge(sem["full"], after(i, len(jobs), NX[-1] - len(jobs)))
                    for t in range(TT):
                        last = dve.tensor_scalar(XB[:, t, :], X[:, t, :], MV[:, t, 0:1], RD[:, t:t + 1], ALU.subtract, ALU.mult)
                        if t == TT - 1:
                            last.then_inc(sem["norm"], 1)
                    dve.wait_ge(sem["norm"], after(i, 1, 0))
                    dve.sem_inc(sem["read"], 1)
                    for m in NVV:
                        k = jobs[m][1]
                        dve.wait_ge(sem["full"], after(i, len(jobs), m))
                        dve.tensor_tensor(V[:, k, :], pW[m % 2][:, :], BV[:, :], ALU.add).then_inc(sem["dve_empty"], 1)
                    n = lambda k: after(i, U, k)
                    for r in range(U + 1):
                        if r < U:
                            w = P * tiles(r % TT)
                            dve.wait_ge(sem["scores"], n(r))
                            dve.wait_ge(sem["probs"], n(r - 4))
                            dve.tensor_reduce(NM[:, r % 4:r % 4 + 1], pS[r % 2][:, 0:w], axis=AX.X, op=ALU.max, negate=True).then_inc(sem["negmax"], 1)
                        if r >= 1:
                            q = (r - 1) % 4
                            w = P * tiles((r - 1) % TT)
                            dve.wait_ge(sem["probs"], n(r - 1))
                            dve.reciprocal(RI[:, q:q + 1], SM[:, q:q + 1]).then_inc(sem["step"], 1)
                            dve.wait_ge(sem["step"], steps.next())
                            dve.tensor_scalar(PR[:, q, 0:w], PR[:, q, 0:w], RI[:, q:q + 1], None, ALU.mult).then_inc(sem["scaled"], 1)
                    steps.close()
                    dve.wait_ge(sem["biased"], after(i, 1, 0))
                    dve.wait_ge(sem["out"], i * 16 + SEED)
                    for m in NO:
                        k = jobs[m][1]
                        dve.wait_ge(sem["full"], after(i, len(jobs), m))
                        dve.scalar_tensor_tensor(out=Y[:, k, :], in0=pW[m % 2][:, :], scalar=TG[:, 1:2], in1=XL[:, k, :],
                                                 op0=ALU.mult, op1=ALU.add).then_inc(sem["dve_empty"], 1)

            @block.tensor
            def _(pe):
                pe.wait_ge(sem["const"], SEED + 16 * 12)
                pe.wait_ge(sem["zero"], SEED + 2)
                with pe.Fori(0, B) as i:
                    def ready(m):
                        for e in ("act", "dve"):
                            pe.wait_ge(emptied[e], banks.emptied(i, m, e))

                    def free(m):
                        before = banks.engine[(m - 2) % len(jobs)]
                        pe.wait_ge(emptied[before], banks.emptied(i, m - 2, before))

                    for m in range(NO[0]):
                        kind, k = jobs[m]
                        if kind == "x" and k == 0:
                            pe.wait_ge(sem["norm"], after(i, 1, 0))
                        if kind == "q" and k == 0:
                            ready(NX[-1])
                        if kind == "k" and k == 0:
                            pe.wait_ge(sem["ctx"], i * 16 + (SEED + 16))
                        free(m)
                        w = pW[m % 2]
                        for c in range(4):
                            if kind == "x":
                                last = pe.transpose(w[:, P * c:P * c + P], XB[:, c, P * k:P * k + P], IDF[:, :])
                            if kind == "q":
                                last = pe.matmul(w[:, :], WQ[:, c, P * k:P * k + P], XT[:, c, :], start=c == 0, stop=c == 3)
                            if kind == "k":
                                last = pe.matmul(w[:, :], WK[:, c, P * k:P * k + P], C[:, c, :], start=c == 0, stop=c == 3)
                            if kind == "v":
                                last = pe.matmul(w[:, :], C[:, c, P * k:P * k + P], WV[:, c, :], start=c == 0, stop=c == 3)
                        last.then_inc(sem["full"], 1)
                    ready(NVV[-1])
                    n = lambda k: after(i, U, k)
                    for r in range(U + 3):
                        if r < U:
                            h, t = r // TT, r % TT
                            w = P * tiles(t)
                            j, v = h // 4, h % 4
                            pe.wait_ge(sem["probs"], n(r - 2))
                            pe.matmul(pS[r % 2][:, 0:w], IDB[:, :], MASK[:, 3 * P - w:3 * P], start=True, stop=False)
                            pe.matmul(pS[r % 2][:, 0:w], QT[:, j, P * t:P * t + P], KT[:, j, v, P * (t + 1) - w:P * (t + 1)],
                                      start=False, stop=True).then_inc(sem["scores"], 1)
                        if 2 <= r < U + 2:
                            q = (r - 2) % 4
                            pe.wait_ge(sem["scaled"], n(r - 2))
                            pe.wait_ge(sem["pcopy"], n(r - 4))
                            for k in range(tiles((r - 2) % TT)):
                                last = pe.transpose(pP[r % 2][:, P * k:P * k + P], PR[:, q, P * k:P * k + P], IDF[:, :])
                            last.then_inc(sem["pturn"], 1)
                        if r >= 3:
                            h, t = (r - 3) // TT, (r - 3) % TT
                            j, v = h // 4, h % 4
                            pe.wait_ge(sem["pcopy"], n(r - 3))
                            if v == 0 and t == 0:
                                pe.wait_ge(sem["outTcopy"], after(i, J, j - 2))
                            nk = tiles(t)
                            for k in range(nk):
                                last = pe.matmul(pO[j % 2][DH * v:DH * v + DH, P * t:P * t + P], V[:, t + 1 - nk + k, DH * h:DH * h + DH],
                                                 PT[:, (r - 3) % 2, P * k:P * k + P], start=k == 0, stop=k == nk - 1, skip_group_check=True)
                            last.then_inc(sem["outT"], 1)
                    pe.wait_ge(sem["outTcopy"], after(i, J, J - 1))
                    for m in NO:
                        k = jobs[m][1]
                        free(m)
                        for c in range(4):
                            last = pe.matmul(pW[m % 2][:, :], OT[:, c, P * k:P * k + P], WO[:, c, :], start=c == 0, stop=c == 3)
                        last.then_inc(sem["full"], 1)


def phase_ffn(nc, keep, a, x3, out):
    F, RANK = 2048, 16
    FT = F // P
    QMAX = 127.0
    MAGIC = 1.5 * 2.0 ** 23
    with ExitStack() as ctx:
        def sb(name, shape, dt=f32):
            return ctx.enter_context(nc.sbuf_tensor("d_" + name, shape, dt))

        names = ["const", "wfc", "wproj", "loaded", "resid", "tanh", "zero", "read", "stats", "rstd", "norm", "xfull", "xempty", "wstep", "wmax", "wall",
                 "ab", "abdone", "weights", "hfull", "hempty", "ofull", "step", "out", "biased", "done"]
        sem = open_phase(nc, keep, ["d_" + n for n in names])
        sem = {n: sem["d_" + n] for n in names}
        WF, WP, WT = sb("wf", [P, CT, F]), sb("wp", [P, FT, D]), sb("wt", [P, CT * F])
        AF, BF, AP_, BP = sb("af", [RANK, D]), sb("bf", [RANK, F]), sb("ap", [RANK, F]), sb("bp", [RANK, D])
        MXW, ALLM, SCL = sb("mxw", [P, 2]), sb("allm", [P, 2]), sb("scl", [P, 4])
        BFC, BPR = sb("bfc", [P, FT]), sb("bpr", [P, D])
        IDF = sb("idf", [P, P])
        GT, TG = sb("gt", [P, 4]), sb("tg", [P, 4])
        X, XL, XB, XT = (sb(n, [P, TT, D]) for n in ("x", "xl", "xb", "xT"))
        HT, Y = sb("hT", [P, 4, S]), sb("y", [P, TT, D])
        BN, MV, VE, RD, POWT = sb("bn", [P, TT, 6]), sb("mv", [P, TT, 2]), sb("ve", [P, TT]), sb("rd", [P, TT]), sb("pow", [P, TT])
        bank = [ctx.enter_context(nc.psum_tensor(f"d_ps{i}", [P, 512], f32)) for i in range(8)]
        pW, pO = bank[0:4], bank[4:8]
        with nc.Block() as block:
            @block.sync
            def _(sp):
                sp.dma_start(WF[:, :, :], a["wfcT"]).then_inc(sem["wfc"], 16)
                for dst, src in ((AF[:, :], a["afc"]), (BF[:, :], a["bfcT"]), (AP_[:, :], a["aproj"]), (BP[:, :], a["bprojT"]),
                                 (BFC[:, :], a["b_fc"]), (BPR[:, :], a["b_proj"]), (IDF[:, :], a["idf"]), (GT[:, :], a["gates"])):
                    sp.dma_start(dst, src).then_inc(sem["const"], 16)
                sp.dma_start(WP[:, :, :], a["wprojT"]).then_inc(sem["wproj"], 16)
                with sp.Fori(0, B) as i:
                    row = lambda t: t[bass.ds(i, 1), :, :].rearrange("o (t p) d -> p (o t) d", p=P)
                    sp.wait_ge(sem["read"], after(i, 1, -1))
                    sp.dma_start(X[:, :, :], row(x3)).then_inc(sem["loaded"], 16)
                    sp.wait_ge(sem["done"], after(i, 1, -1))
                    sp.dma_start(XL[:, :, :], row(x3)).then_inc(sem["resid"], 16)
                    sp.wait_ge(sem["done"], after(i, 1, 0))
                    sp.dma_start(row(out), Y[:, :, :]).then_inc(sem["out"], 16)
                sp.wait_ge(sem["out"], SEED + 16 * B)

            @block.gpsimd
            def _(pool):
                for n in range(2):
                    pool.wait_ge(sem["wmax"], SEED + n + 1)
                    pool.partition_all_reduce(ALLM[:, n:n + 1], MXW[:, n:n + 1], P, bass.bass_isa.ReduceOp.max).then_inc(sem["wall"], 1)
                pool.wait_ge(sem["zero"], SEED + 2)
                with pool.Fori(0, B) as i:
                    pool.wait_ge(sem["stats"], after(i, 1, 0))
                    pool.tensor_tensor(RD[:, :], VE[:, :], POWT[:, :], ALU.pow).then_inc(sem["rstd"], 1)
                    pool.wait_ge(sem["resid"], i * 16 + (SEED + 16))
                    for t in range(TT):
                        last = pool.tensor_tensor(XL[:, t, :], XL[:, t, :], BPR[:, :], ALU.add)
                    last.then_inc(sem["biased"], 1)

            @block.scalar
            def _(act):
                act.wait_ge(sem["const"], SEED + 16 * 8)
                act.activation(TG[:, :], GT[:, :], ACT.Tanh).then_inc(sem["tanh"], 1)
                with act.Fori(0, B) as i:
                    for c in range(CT):
                        act.wait_ge(sem["xfull"], after(i, CT, c))
                        act.copy(XT[:, c, :], pW[c][:, :]).then_inc(sem["xempty"], 1)
                    for f in range(FT):
                        act.wait_ge(sem["hfull"], after(i, FT, f))
                        act.wait_ge(sem["ofull"], after(i, FT, f - 4))
                        act.activation(HT[:, f % 4, :], pW[f % 4][:, :], ACT.Gelu, bias=BFC[:, f:f + 1]).then_inc(sem["hempty"], 1)

            @block.vector
            def _(dve):
                dve.memset(POWT[:, :], -0.5).then_inc(sem["zero"], 1)
                dve.wait_ge(sem["tanh"], SEED + 1)
                dve.tensor_scalar(BPR[:, :], BPR[:, :], TG[:, 3:4], None, ALU.mult).then_inc(sem["zero"], 1)
                k = 0
                for n, (W, w) in enumerate(((WF, "wfc"), (WP, "wproj"))):
                    flat = W[:, :, :].rearrange("p c f -> p (c f)")
                    dve.wait_ge(sem[w], SEED + 16)
                    dve.tensor_reduce(MXW[:, n:n + 1], flat, axis=AX.X, op=ALU.max, apply_absolute_value=True).then_inc(sem["wmax"], 1)
                for n, W in enumerate((WF, WP)):
                    flat = W[:, :, :].rearrange("p c f -> p (c f)")
                    dve.wait_ge(sem["wall"], SEED + n + 1)
                    dve.tensor_scalar(SCL[:, 2 * n:2 * n + 1], ALLM[:, n:n + 1], 1.0 / QMAX, None, ALU.mult).then_inc(sem["wstep"], 1)
                    dve.wait_ge(sem["wstep"], SEED + k + 1)
                    dve.reciprocal(SCL[:, 2 * n + 1:2 * n + 2], SCL[:, 2 * n:2 * n + 1]).then_inc(sem["wstep"], 1)
                    dve.wait_ge(sem["wstep"], SEED + k + 2)
                    dve.tensor_scalar(WT[:, :], flat, SCL[:, 2 * n + 1:2 * n + 2], MAGIC, ALU.mult, ALU.add).then_inc(sem["wstep"], 1)
                    dve.wait_ge(sem["wstep"], SEED + k + 3)
                    dve.tensor_scalar(WT[:, :], WT[:, :], MAGIC, QMAX, ALU.subtract, ALU.min).then_inc(sem["wstep"], 1)
                    dve.wait_ge(sem["wstep"], SEED + k + 4)
                    dve.tensor_scalar(flat, WT[:, :], -QMAX - 1, SCL[:, 2 * n:2 * n + 1], ALU.max, ALU.mult).then_inc(sem["wstep"], 1)
                    k += 5
                    dve.wait_ge(sem["wstep"], SEED + k)
                for m in range(2 * FT):
                    part = WF[:, m // 4, 512 * (m % 4):512 * (m % 4) + 512] if m < FT else WP[:, m - FT, :]
                    dve.wait_ge(sem["ab"], SEED + m + 1)
                    dve.scalar_tensor_tensor(out=part, in0=pW[m % 4][:, :], scalar=2.0, in1=part, op0=ALU.mult, op1=ALU.add).then_inc(sem["abdone"], 1)
                with dve.Fori(0, B) as i:
                    steps = Steps(i, 2)
                    dve.wait_ge(sem["loaded"], i * 16 + (SEED + 16))
                    for t in range(TT):
                        last = dve.bn_stats(BN[:, t, :], X[:, t, :])
                    last.then_inc(sem["step"], 1)
                    dve.wait_ge(sem["step"], steps.next())
                    dve.memset(VE[:, 0:1], 0.0)
                    for t in range(TT):
                        last = dve.bn_aggr(MV[:, t, :], BN[:, t, :])
                    last.then_inc(sem["step"], 1)
                    dve.wait_ge(sem["step"], steps.next())
                    steps.close()
                    dve.tensor_scalar(VE[:, :], MV[:, :, 1], EPS, None, ALU.add).then_inc(sem["stats"], 1)
                    dve.wait_ge(sem["rstd"], after(i, 1, 0))
                    dve.wait_ge(sem["xfull"], after(i, CT, -1))
                    for t in range(TT):
                        last = dve.tensor_scalar(XB[:, t, :], X[:, t, :], MV[:, t, 0:1], RD[:, t:t + 1], ALU.subtract, ALU.mult)
                    last.then_inc(sem["norm"], 1)
                    dve.wait_ge(sem["norm"], after(i, 1, 0))
                    dve.sem_inc(sem["read"], 1)
                    dve.wait_ge(sem["biased"], after(i, 1, 0))
                    dve.wait_ge(sem["out"], i * 16 + SEED)
                    dve.wait_ge(sem["ofull"], after(i, FT, FT - 1))
                    for t in range(TT):
                        last = dve.scalar_tensor_tensor(out=Y[:, t, :], in0=pO[t][:, :], scalar=TG[:, 3:4], in1=XL[:, t, :], op0=ALU.mult, op1=ALU.add)
                    last.then_inc(sem["done"], 1)

            @block.tensor
            def _(pe):
                pe.wait_ge(sem["const"], SEED + 16 * 8)
                for m in range(2 * FT):
                    if m >= 4:
                        pe.wait_ge(sem["abdone"], SEED + m - 3)
                    if m < FT:
                        c, f = m // 4, m % 4
                        last = pe.matmul(pW[m % 4][:, :], AF[:, P * c:P * c + P], BF[:, 512 * f:512 * f + 512], start=True, stop=True)
                    else:
                        f = m - FT
                        last = pe.matmul(pW[m % 4][:, :], AP_[:, P * f:P * f + P], BP[:, :], start=True, stop=True)
                    last.then_inc(sem["ab"], 1)
                pe.wait_ge(sem["abdone"], SEED + 2 * FT)
                with pe.Fori(0, B) as i:
                    pe.wait_ge(sem["norm"], after(i, 1, 0))
                    for c in range(CT):
                        pe.wait_ge(sem["hempty"], after(i, FT, c - 4))
                        for t in range(TT):
                            last = pe.transpose(pW[c][:, P * t:P * t + P], XB[:, t, P * c:P * c + P], IDF[:, :])
                        last.then_inc(sem["xfull"], 1)
                    pe.wait_ge(sem["xempty"], after(i, CT, CT - 1))
                    for f in range(FT + 2):
                        if f < FT:
                            pe.wait_ge(sem["hempty"], after(i, FT, f - 4))
                            for c in range(CT):
                                last = pe.matmul(pW[f % 4][:, :], WF[:, c, P * f:P * f + P], XT[:, c, :], start=c == 0, stop=c == CT - 1)
                            last.then_inc(sem["hfull"], 1)
                        if f >= 2:
                            g = f - 2
                            pe.wait_ge(sem["hempty"], after(i, FT, g))
                            if g == 0:
                                pe.wait_ge(sem["done"], after(i, 1, -1))
                            for t in range(TT):
                                last = pe.matmul(pO[t][:, :], HT[:, g % 4, P * t:P * t + P], WP[:, g, :], start=g == 0, stop=g == FT - 1)
                            last.then_inc(sem["ofull"], 1)


def program(nc, a, out, x1, x1l, xr, s_route, sel, x2, x3):
    with ExitStack() as keep:
        phase_token_heads(nc, keep, a["x_th"], a["v_th"], a["kT_th"], a, a["gates"], x1)
        phase_local(nc, keep, a, x1, x1l, xr, s_route)
        phase_route(nc, keep, a, s_route, sel)
        phase_heavy(nc, keep, a, xr, x1l, sel, x2)
        phase_window(nc, keep, a, x2, x3)
        phase_ffn(nc, keep, a, x3, out)


BF16_CONSTANTS = ("idb", "mask_th", "neg64", "mask_w")


def bf16_bits(constant):
    return (constant.astype(np.float32).view(np.uint32) >> 16).astype(np.uint16)


def dram_inputs(nc, arrays):
    a = {k: nc.dram_tensor(f"in_{k}", v.shape, mybir.dt.from_np(v.dtype), kind="ExternalInput").ap() for k, v in arrays.items()}
    return {k: v.bitcast(bf16) if k in BF16_CONSTANTS else v for k, v in a.items()}


def layouts(inputs):
    f = {k: np.asarray(v) for k, v in inputs.items()}
    x, c = f["x"], f["ctx_1024"]
    a = {}
    a["x_th"] = x.reshape(B, S // 8, P, 32).transpose(0, 2, 1, 3).reshape(B, P, S * 4)
    a["v_th"] = c.reshape(B, S // 8, P, 32).transpose(0, 2, 1, 3).reshape(B, P, S * 4)
    a["kT_th"] = c.reshape(B, S // 32, 4, P, 32).transpose(0, 2, 4, 1, 3).reshape(B, P, S // 32, P)
    a["gates"] = np.tile(np.concatenate([f["g_xattn"], f["g_ffn"]]), (P, 1))
    p = np.arange(P)
    a["idf"] = np.eye(P, dtype=np.float32)
    a["idb"] = bf16_bits(np.eye(P))
    same = p[:, None] // 16 == p[None, :] // 16
    a["blockmean"] = (same / D).astype(np.float32)
    a["mask_th"] = bf16_bits(np.tile(np.where(same & (p[None, :] <= p[:, None]), 0, NEG), (1, 4)))
    def wT(w):
        return w.T.reshape(w.shape[1] // P, P, w.shape[0]).transpose(1, 0, 2)

    def col(v):
        return v.reshape(-1, P).T

    a["wqkvT"], a["woutlT"] = wT(f["L0_ffn_Wqkv"]), wT(f["L0_ffn_Wout_l"])
    a["rt"] = np.tile(np.stack([f["L0_ffn_rt_q"][0], f["L0_ffn_rt_kv"][0]])[None], (P, 1, 1))
    a["ln_w"], a["ln_b"] = col(f["L0_ffn_ln_w"]), col(f["L0_ffn_ln_b"])
    a["neg64"] = bf16_bits(np.full((P, 64), -1e9))
    k_of = [min(256 * 9.0 / 8.0, float(S)), min(512 * 9.0 / 8.0, float(S))]
    a["logk"] = np.repeat([[np.log(k), np.log(S) - np.log(k)] for k in k_of], B, axis=0).astype(np.float32)
    wkv = f["L0_ffn_Wkv"].reshape(8, 2, 64, D)
    a["hwqT"], a["hwoT"] = wT(f["L0_ffn_Wq"]), wT(f["L0_ffn_Wout_h"])
    a["hwkT"], a["hwvT"] = wT(wkv[:, 0].reshape(D, D)), wT(wkv[:, 1].reshape(D, D))
    a["gamma"] = col(f["L0_ffn_gamma"])
    nk, nv = f["L0_ffn_null_kv"]
    nkb, nvb = np.zeros((P, 4, 2), np.float32), np.zeros((P, 4, P), np.float32)
    for h in range(8):
        o = 64 * (h % 2)
        nkb[o:o + 64, h // 2, h % 2] = nk[h]
        nvb[h, h // 2, o:o + 64] = nv[h]
    a["null_k"], a["null_v"] = nkb, nvb
    a["null_q"] = np.tile(f["L0_ffn_null_q"][None], (P, 1))
    a["ctxT"] = c.transpose(0, 2, 1).reshape(B, CT, P, S).transpose(0, 2, 1, 3)
    for n in "qkvo":
        a[f"xw{n}T"] = wT(f[f"L1_xattn_w{n}"])
    a["xbq"], a["xbk"] = col(f["L1_xattn_bq"]), col(f["L1_xattn_bk"])
    a["xbv"], a["xbo"] = (np.tile(f[k][None], (P, 1)) for k in ("L1_xattn_bv", "L1_xattn_bo"))
    r, k = p[:, None], p[None, :]
    a["mask_w"] = bf16_bits(np.concatenate([np.where(k >= r, 0, NEG), 0.0 * (k + r), np.where(k <= r, 0, NEG)], 1))
    a["wfcT"], a["wprojT"] = wT(f["L1_ffn_W_fc"]), wT(f["L1_ffn_W_proj"])
    a["afc"], a["aproj"] = f["L1_ffn_A_fc"], f["L1_ffn_A_proj"]
    a["bfcT"], a["bprojT"] = f["L1_ffn_B_fc"].T, f["L1_ffn_B_proj"].T
    a["b_fc"], a["b_proj"] = col(f["L1_ffn_b_fc"]), np.tile(f["L1_ffn_b_proj"][None], (P, 1))
    return {k: np.ascontiguousarray(v) for k, v in a.items()}


def kernel(**inputs):
    import concourse.bacc as _bacc
    from concourse.bass_utils import run_bass_kernel_spmd as _run

    nc = _bacc.Bacc("TRN2", target_bir_lowering=False, num_devices=1)
    arrays = layouts(inputs)
    a = dram_inputs(nc, arrays)
    out = nc.dram_tensor("out_0", (B, S, D), f32, kind="ExternalOutput").ap()
    scratch = {k: nc.dram_tensor(f"s_{k}", shape, f32).ap() for k, shape in SCRATCH.items()}
    program(nc, a, out, **scratch)
    r = _run(nc, [{f"in_{k}": v for k, v in arrays.items()}], core_ids=[0])
    return r.results[0]["out_0"]


SCRATCH = {"x1": (B, S, D), "x1l": (B, S, D), "xr": (B, S, D), "s_route": (B, P, 2 * TT), "sel": (P, TT, 3 * B), "x2": (B, S, D), "x3": (B, S, D)}
```

```python
import concourse.bass as bass
from concourse import mybir
from contextlib import ExitStack
import numpy as np

f32 = mybir.dt.float32
bf16 = mybir.dt.bfloat16
ALU = mybir.AluOpType
ACT = mybir.ActivationFunctionType
AX = mybir.AxisListType

B, S, D = 8, 512, 512
P = 128
TT = S // P
CT = D // P
EPS = 1e-5
NEG = -1e30

SEED = 48


def after(i, per, k):
    return i * per + (SEED + k + 1)


class Steps:

    def __init__(self, i, per):
        self.i, self.per, self.k = i, per, 0

    def next(self):
        self.k += 1
        return after(self.i, self.per, self.k - 1)

    def close(self):
        assert self.k == self.per, (self.k, self.per)


def open_phase(nc, keep, names):
    sems = {n: keep.enter_context(nc.semaphore(n)) for n in names}
    with nc.Block() as block:
        @block.gpsimd
        def _(pool):
            for s in sems.values():
                pool.sem_inc(s, SEED)
    return sems


def phase_token_heads(nc, keep, x_th, v_th, kT_th, consts, gates, x1):
    H, DH = 16, 32
    G = S // 8
    R = G // 4
    W = G * DH
    SCALE = DH ** -0.5
    with ExitStack() as ctx:
        def sb(name, shape, dt=f32):
            return ctx.enter_context(nc.sbuf_tensor(name, shape, dt))

        a_stored = keep.enter_context(nc.semaphore("a_stored"))
        names = ["a_const", "a_loaded0", "a_loaded1", "a_kv0", "a_kv1", "a_tanh", "a_sums", "a_mean", "a_sqsums", "a_var", "a_vareps", "a_rstd",
                 "a_q", "a_qturn", "a_qcopy", "a_scores", "a_shift", "a_probs", "a_psum", "a_pturn", "a_pcopy",
                 "a_outT", "a_outTcopy", "a_outrow", "a_done", "a_vstep", "a_xfree", "a_zeroed"]
        sem = open_phase(nc, keep, names)
        X = sb("a_x", [P, 2, W])
        V = sb("a_v", [P, 2, W])
        KH = sb("a_kh", [P, 2, R, 4 * P])
        XC = sb("a_xc", [P, W])
        SQ = sb("a_sq", [P, W])
        Q = sb("a_qn", [P, W])
        ST = sb("a_st", [P, 4, G])
        POWT = sb("a_pow", [P, G])
        QT = sb("a_qT", [P, 2, P])
        Z = sb("a_z", [P, 2, 4, P])
        PR = sb("a_pr", [P, 2, 4, P])
        PT = sb("a_pT", [P, 2, 4 * P])
        OT = sb("a_oT", [P, 2, P])
        MX = sb("a_mx", [P, 2, 4])
        SM = sb("a_sm", [P, 2, 16])
        RS = sb("a_rs", [P, 16])
        TO = sb("a_to", [P, 16, DH])
        IDF, IDB, BM, MASK = (sb("a_idf", [P, P]), sb("a_idb", [P, P], bf16), sb("a_bm", [P, P]), sb("a_mask", [P, 4 * P], bf16))
        GT = sb("a_gt", [P, 4])
        TG = sb("a_tg", [P, 4])
        bank = [ctx.enter_context(nc.psum_tensor(f"a_ps{i}", [P, 512], f32)) for i in range(8)]
        pS, pP, pQ, pOT, pO, pL = bank[0:2], bank[2:4], bank[4], bank[5], bank[6], bank[7]
        NV = 2 + R + 3 * (R // 4)

        with nc.Block() as block:
            @block.sync
            def _(sp):
                sp.wait_ge(sem["a_zeroed"], SEED + 2)
                sp.dma_start(IDF[:, :], consts["idf"]).then_inc(sem["a_const"], 16)
                sp.dma_start(IDB[:, :], consts["idb"]).then_inc(sem["a_const"], 16)
                sp.dma_start(BM[:, :], consts["blockmean"]).then_inc(sem["a_const"], 16)
                sp.dma_start(MASK[:, :], consts["mask_th"]).then_inc(sem["a_const"], 16)
                sp.dma_start(GT[:, :], gates).then_inc(sem["a_const"], 16)
                with sp.Fori(0, B // 2) as i:
                    for u in range(2):
                        b = i * 2 + u
                        sp.wait_ge(sem["a_xfree"], after(i, 2, u - 2))
                        sp.dma_start(X[:, u, :], x_th[bass.ds(b, 1), :, :].rearrange("o p w -> (o p) w")).then_inc(sem[f"a_loaded{u}"], 16)
                        sp.wait_ge(sem["a_outT"], after(i, 2 * R, (u - 2) * R + R - 1))
                        sp.dma_start(V[:, u, :], v_th[bass.ds(b, 1), :, :].rearrange("o p w -> (o p) w")).then_inc(sem[f"a_kv{u}"], 16)
                        for g in range(4):
                            sp.dma_start(KH[32 * g:32 * g + 32, u, :, P * g:P * g + P],
                                         kT_th[bass.ds(b, 1), 32 * g:32 * g + 32, :, :].rearrange("o p r n -> (o p) r n")).then_inc(sem[f"a_kv{u}"], 16)

            @block.gpsimd
            def _(pool):
                with pool.Fori(0, B // 2) as i:
                    for u in range(2):
                        b = i * 2 + u
                        pool.wait_ge(sem["a_vareps"], after(i, 2, u))
                        pool.tensor_tensor(ST[:, 3, :], ST[:, 2, :], POWT[:, :], ALU.pow).then_inc(sem["a_rstd"], 1)
                        pool.wait_ge(sem["a_done"], after(i, 2 * (R // 4), u * (R // 4) + R // 4 - 1))
                        pool.dma_start(x1[bass.ds(b, 1), :, :].rearrange("o (g t) (h d) -> (o t h) g d", t=8, d=DH),
                                       X[:, u, :].rearrange("p (g d) -> p g d", d=DH)).then_inc(a_stored, 16)
                        pool.wait_ge(a_stored, b * 16 + 16)
                        pool.sem_inc(sem["a_xfree"], 1)

            @block.scalar
            def _(act):
                act.wait_ge(sem["a_const"], SEED + 80)
                act.activation(TG[:, :], GT[:, :], ACT.Tanh).then_inc(sem["a_tanh"], 1)
                with act.Fori(0, B // 2) as i:
                    for u in range(2):
                        n = lambda k: after(i, 2 * R, u * R + k)

                        def copy_q(r):
                            act.wait_ge(sem["a_qturn"], n(r))
                            act.wait_ge(sem["a_scores"], n(r - 2))
                            act.copy(QT[:, r % 2, :], pQ[:, 0:P]).then_inc(sem["a_qcopy"], 1)

                        copy_q(0)
                        for r in range(R + 2):
                            if r + 1 < R:
                                copy_q(r + 1)
                            if r < R:
                                act.wait_ge(sem["a_shift"], n(r))
                                act.wait_ge(sem["a_pturn"], n(r - 2))
                                act.wait_ge(sem["a_psum"], n(r - 2))
                                act.activation(PR[:, r % 2, :, :], Z[:, r % 2, :, :], ACT.Exp, scale=SCALE).then_inc(sem["a_probs"], 1)
                            if 1 <= r <= R:
                                act.wait_ge(sem["a_pturn"], n(r - 1))
                                act.wait_ge(sem["a_outT"], n(r - 3))
                                act.copy(PT[:, (r - 1) % 2, :], pP[(r - 1) % 2][:, :]).then_inc(sem["a_pcopy"], 1)
                            if r >= 2:
                                act.wait_ge(sem["a_outT"], n(r - 2))
                                act.wait_ge(sem["a_outrow"], n(r - 4))
                                act.copy(OT[:, r % 2, :], pOT[:, 0:P]).then_inc(sem["a_outTcopy"], 1)

            @block.vector
            def _(dve):
                dve.memset(POWT[:, :], -0.5).then_inc(sem["a_zeroed"], 1)
                dve.memset(KH[:, :, :, :], 0.0).then_inc(sem["a_zeroed"], 1)
                with dve.Fori(0, B // 2) as i:
                    for u in range(2):
                        steps = Steps(i * 2 + u, NV)
                        n = lambda k: after(i, 2 * R, u * R + k)
                        x3 = X[:, u, :].rearrange("p (g d) -> p g d", d=DH)
                        xc3, sq3, q3 = (t[:, :].rearrange("p (g d) -> p g d", d=DH) for t in (XC, SQ, Q))
                        dve.wait_ge(sem[f"a_loaded{u}"], i * 16 + (SEED + 16))
                        dve.wait_ge(sem["a_mean"], after(i, 2, u - 1))
                        dve.reduce_sum(ST[:, 0, :], x3, axis=AX.X).then_inc(sem["a_sums"], 1)
                        dve.wait_ge(sem["a_mean"], after(i, 2, u))
                        dve.tensor_tensor(xc3, x3, pL[:, 0:G].unsqueeze(2).broadcast_to([P, G, DH]), ALU.subtract).then_inc(sem["a_vstep"], 1)
                        dve.wait_ge(sem["a_vstep"], steps.next())
                        dve.tensor_tensor(SQ[:, :], XC[:, :], XC[:, :], ALU.mult).then_inc(sem["a_vstep"], 1)
                        dve.wait_ge(sem["a_vstep"], steps.next())
                        dve.reduce_sum(ST[:, 1, :], sq3, axis=AX.X).then_inc(sem["a_sqsums"], 1)
                        dve.wait_ge(sem["a_var"], after(i, 2, u))
                        dve.tensor_scalar(ST[:, 2, :], pL[:, G:2 * G], EPS, None, ALU.add).then_inc(sem["a_vareps"], 1)
                        dve.wait_ge(sem["a_rstd"], after(i, 2, u))
                        dve.wait_ge(sem["a_qturn"], n(-1))
                        dve.tensor_tensor(q3, xc3, ST[:, 3, :].unsqueeze(2).broadcast_to([P, G, DH]), ALU.mult).then_inc(sem["a_q"], 1)

                        def finish(j):
                            rs = RS[:, :]
                            dve.wait_ge(sem["a_psum"], n(4 * j + 3))
                            dve.reciprocal(rs, SM[:, j % 2, :]).then_inc(sem["a_vstep"], 1)
                            dve.wait_ge(sem["a_vstep"], steps.next())
                            dve.tensor_scalar(rs, rs, TG[:, 0:1], None, ALU.mult).then_inc(sem["a_vstep"], 1)
                            dve.wait_ge(sem["a_vstep"], steps.next())
                            dve.wait_ge(sem["a_outrow"], n(4 * j + 3))
                            dve.tensor_tensor(TO[:, :, :], pO[:, :].rearrange("p (g d) -> p g d", d=DH),
                                              rs.unsqueeze(2).broadcast_to([P, 16, DH]), ALU.mult).then_inc(sem["a_vstep"], 1)
                            dve.wait_ge(sem["a_vstep"], steps.next())
                            xs = x3[:, 16 * j:16 * j + 16, :]
                            dve.tensor_tensor(xs, xs, TO[:, :, :], ALU.add).then_inc(sem["a_done"], 1)

                        dve.wait_ge(sem["a_tanh"], SEED + 1)
                        for r in range(R + 4):
                            if r < R:
                                dve.wait_ge(sem["a_scores"], n(r))
                                dve.reduce_max(MX[:, r % 2, :], pS[r % 2][:, :].rearrange("p (g n) -> p g n", n=P), axis=AX.X).then_inc(sem["a_vstep"], 1)
                                dve.wait_ge(sem["a_vstep"], steps.next())
                                dve.wait_ge(sem["a_probs"], n(r - 2))
                                dve.tensor_tensor(Z[:, r % 2, :, :], pS[r % 2][:, :].rearrange("p (g n) -> p g n", n=P),
                                                  MX[:, r % 2, :].unsqueeze(2).broadcast_to([P, 4, P]), ALU.subtract).then_inc(sem["a_shift"], 1)
                            if 1 <= r <= R:
                                dve.wait_ge(sem["a_probs"], n(r - 1))
                                dve.reduce_sum(SM[:, (r - 1) // 4 % 2, 4 * ((r - 1) % 4):4 * ((r - 1) % 4) + 4], PR[:, (r - 1) % 2, :, :], axis=AX.X).then_inc(sem["a_psum"], 1)
                            if r >= 7 and (r - 7) % 4 == 0:
                                finish((r - 7) // 4)
                        steps.close()

            @block.tensor
            def _(pe):
                pe.wait_ge(sem["a_const"], SEED + 80)
                with pe.Fori(0, B // 2) as i:
                    for u in range(2):
                        n = lambda k: after(i, 2 * R, u * R + k)
                        pe.wait_ge(sem["a_sums"], after(i, 2, u))
                        pe.wait_ge(sem["a_vareps"], after(i, 2, u - 1))
                        pe.matmul(pL[:, 0:G], BM[:, :], ST[:, 0, :], start=True, stop=True).then_inc(sem["a_mean"], 1)
                        pe.wait_ge(sem["a_sqsums"], after(i, 2, u))
                        pe.matmul(pL[:, G:2 * G], BM[:, :], ST[:, 1, :], start=True, stop=True).then_inc(sem["a_var"], 1)
                        pe.wait_ge(sem[f"a_kv{u}"], i * 80 + (SEED + 80))

                        def turn_q(r):
                            pe.wait_ge(sem["a_qcopy"], n(r - 1))
                            pe.transpose(pQ[:, 0:P], Q[:, P * r:P * r + P], IDF[:, :]).then_inc(sem["a_qturn"], 1)

                        pe.wait_ge(sem["a_q"], after(i, 2, u))
                        turn_q(0)
                        for r in range(R + 3):
                            if r + 1 < R:
                                turn_q(r + 1)
                            if r < R:
                                pe.wait_ge(sem["a_qcopy"], n(r))
                                pe.wait_ge(sem["a_shift"], n(r - 2))
                                pe.matmul(pS[r % 2][:, :], IDB[:, :], MASK[:, :], start=True, stop=False)
                                pe.matmul(pS[r % 2][:, :], QT[:, r % 2, :], KH[:, u, r, :], start=False, stop=True).then_inc(sem["a_scores"], 1)
                            if 1 <= r <= R:
                                pe.wait_ge(sem["a_probs"], n(r - 1))
                                pe.wait_ge(sem["a_pcopy"], n(r - 3))
                                for g in range(4):
                                    last = pe.transpose(pP[(r - 1) % 2][:, P * g:P * g + P], PR[:, (r - 1) % 2, g, :], IDF[:, :])
                                last.then_inc(sem["a_pturn"], 1)
                            if 2 <= r <= R + 1:
                                pe.wait_ge(sem["a_pcopy"], n(r - 2))
                                pe.wait_ge(sem["a_outTcopy"], n(r - 3))
                                for g in range(4):
                                    gg = 4 * (r - 2) + g
                                    last = pe.matmul(pOT[32 * g:32 * g + 32, 0:P], V[:, u, 32 * gg:32 * gg + 32],
                                                     PT[:, r % 2, P * g:P * g + P], start=True, stop=True)
                                last.then_inc(sem["a_outT"], 1)
                            if r >= 3:
                                pe.wait_ge(sem["a_outTcopy"], n(r - 3))
                                if (r - 3) % 4 == 0:
                                    pe.wait_ge(sem["a_done"], after(i, 2 * (R // 4), u * (R // 4) + (r - 3) // 4 - 1))
                                c = (r - 3) % 4
                                pe.transpose(pO[:, P * c:P * c + P], OT[:, (r - 3) % 2, :], IDF[:, :]).then_inc(sem["a_outrow"], 1)


class Banks:

    def __init__(self, jobs, engine_of):
        self.jobs = jobs
        self.engine = [engine_of(m, job) for m, job in enumerate(jobs)]
        self.per = {e: self.engine.count(e) for e in ("act", "dve")}

    def of(self, kind):
        return [m for m, job in enumerate(self.jobs) if job[0] == kind]

    def emptied(self, i, m, e):
        back = 0
        while m < 0:
            m, back = m + len(self.jobs), back + 1
        return after(i, self.per[e], self.engine[:m + 1].count(e) - 1 - back * self.per[e])


def phase_local(nc, keep, a, x1, x1l, xr, s_route):
    H, DH, WIN = 8, 64, 64
    SCALE = DH ** -0.5
    J = 4
    U = J * TT
    jobs = [("x", c) for c in range(4)] + [("q", j) for j in range(4)] + [("k", j) for j in range(4)] + \
           [("v", t) for t in range(4)] + [("o", t) for t in range(4)]
    banks = Banks(jobs, lambda m, job: "dve" if job[0] == "o" else ("act", "dve")[m % 2])
    NX, NQ, NK, NVV, NO = (banks.of(k) for k in "xqkvo")
    with ExitStack() as ctx:
        def sb(name, shape, dt=f32):
            return ctx.enter_context(nc.sbuf_tensor("b_" + name, shape, dt))

        names = ["const", "loaded", "resid", "read", "nstep", "stats", "rstd", "xr", "s", "route_out", "xr_out", "norm",
                 "full", "act_empty", "dve_empty", "scores", "negmax", "probs", "scaled", "pturn", "pmain", "pextra",
                 "outT", "outTcopy", "tanh", "step", "out", "rows", "zero"]
        sem = open_phase(nc, keep, ["b_" + n for n in names])
        sem = {n: sem["b_" + n] for n in names}
        emptied = {"act": sem["act_empty"], "dve": sem["dve_empty"]}
        WQKV = sb("wqkv", [P, CT, 3 * D])
        WO = sb("wo", [P, CT, D])
        RT = sb("rt", [P, 2, D])
        LNW, LNB = sb("lnw", [P, CT]), sb("lnb", [P, CT])
        IDF, IDB, NEGB = sb("idf", [P, P]), sb("idb", [P, P], bf16), sb("negb", [P, WIN], bf16)
        GT, TG = sb("gt", [P, 4]), sb("tg", [P, 4])
        X, XL, XA, XB, XR = (sb(n, [P, TT, D]) for n in ("x", "xl", "xa", "xb", "xr"))
        XBT = sb("xbT", [P, CT, S])
        QT, KT, V = sb("qT", [P, J, S]), sb("kT", [P, J, 2, S]), sb("v", [P, TT, D])
        VL = sb("vlo", [WIN, TT, D])
        BN, MV, RD, POWT = sb("bn", [P, TT, 6]), sb("mv", [P, 3 * TT, 2]), sb("rd", [P, 3 * TT]), sb("pow", [P, 2 * TT])
        VE = sb("ve", [P, 3 * TT])
        SS, SCR = sb("ss", [P, 2, TT]), sb("scr", [P, D])
        PR, NM, SM, RI = sb("pr", [P, 4, 2, 192]), sb("nm", [P, 4, 2]), sb("sm", [P, 4, 2]), sb("ri", [P, 4, 2])
        PTM, PTE = sb("pTm", [P, 2, 2, P]), sb("pTe", [WIN, 2, 2, P])
        OT, Y = sb("oT", [P, J, S]), sb("y", [P, TT, D])
        bank = [ctx.enter_context(nc.psum_tensor(f"b_ps{i}", [P, 512], f32)) for i in range(8)]
        pW, pS, pP, pO = bank[0:2], bank[2:5], bank[5:7], bank[7]

        with nc.Block() as block:
            @block.sync
            def _(sp):
                for dst, src in ((WQKV[:, :, :], a["wqkvT"]), (WO[:, :, :], a["woutlT"]), (RT[:, :, :], a["rt"]), (LNW[:, :], a["ln_w"]),
                                 (LNB[:, :], a["ln_b"]), (IDF[:, :], a["idf"]), (IDB[:, :], a["idb"]), (NEGB[:, :], a["neg64"]),
                                 (GT[:, :], a["gates"])):
                    sp.dma_start(dst, src).then_inc(sem["const"], 16)
                sp.dma_start(X[:, :, :], x1[0, :, :].rearrange("(t p) d -> p t d", p=P)).then_inc(sem["loaded"], 16)
                with sp.Fori(0, B) as i:
                    row = lambda t, b=i: t[bass.ds(b, 1), :, :].rearrange("o (t p) d -> p (o t) d", p=P)
                    ahead = sp.snap((i + 1) % B)
                    sp.wait_ge(sem["read"], after(i, 1, 0))
                    sp.dma_start(X[:, :, :], row(x1, ahead)).then_inc(sem["loaded"], 16)
                    sp.wait_ge(sem["dve_empty"], banks.emptied(i, -1, "dve"))
                    sp.dma_start(XL[:, :, :], row(x1)).then_inc(sem["resid"], 16)
                    sp.wait_ge(sem["xr"], after(i, 1, 0))
                    sp.dma_start(row(xr), XR[:, :, :]).then_inc(sem["xr_out"], 16)
                    sp.wait_ge(sem["s"], after(i, 1, 0))
                    sp.dma_start(s_route[bass.ds(i, 1), :, :].rearrange("o p n -> (o p) n"), SS[:, :, :].rearrange("p r t -> p (r t)")).then_inc(sem["route_out"], 16)
                    sp.wait_ge(sem["dve_empty"], banks.emptied(i, NO[-1], "dve"))
                    sp.dma_start(row(x1l), Y[:, :, :]).then_inc(sem["out"], 16)
                sp.wait_ge(sem["xr_out"], SEED + 16 * B)
                sp.wait_ge(sem["route_out"], SEED + 16 * B)
                sp.wait_ge(sem["out"], SEED + 16 * B)

            @block.gpsimd
            def _(pool):
                with pool.Fori(0, B + 1) as i:
                    pool.wait_ge(sem["stats"], after(i, 2, 0))
                    pool.tensor_tensor(RD[:, 0:TT], VE[:, 0:TT], POWT[:, 0:TT], ALU.pow).then_inc(sem["rstd"], 1)
                    pool.wait_ge(sem["stats"], after(i, 2, 1))
                    pool.tensor_tensor(RD[:, TT:3 * TT], VE[:, TT:3 * TT], POWT[:, :], ALU.pow).then_inc(sem["rstd"], 1)

            @block.scalar
            def _(act):
                act.wait_ge(sem["const"], SEED + 16 * 9)
                act.activation(TG[:, :], GT[:, :], ACT.Tanh).then_inc(sem["tanh"], 1)
                with act.Fori(0, B) as i:
                    for m, (kind, k) in enumerate(jobs):
                        if banks.engine[m] != "act":
                            continue
                        w = pW[m % 2]
                        act.wait_ge(sem["full"], after(i, len(jobs), m))
                        if kind == "x":
                            act.activation(XBT[:, k, :], w[:, :], ACT.Identity, bias=LNB[:, k:k + 1], scale=LNW[:, k:k + 1]).then_inc(sem["act_empty"], 1)
                        if kind == "q":
                            act.mul(QT[:, k, :], w[:, :], SCALE).then_inc(sem["act_empty"], 1)
                        if kind == "k":
                            act.copy(KT[0:64, k, 0, :], w[0:64, :])
                            act.copy(KT[64:128, k, 1, :], w[64:128, :]).then_inc(sem["act_empty"], 1)
                        if kind == "v":
                            act.copy(V[:, k, :], w[:, :])
                            act.copy(VL[:, k, :], w[64:128, :]).then_inc(sem["act_empty"], 1)
                    n = lambda k: after(i, U, k)
                    for r in range(U + 3):
                        if r < U:
                            act.wait_ge(sem["negmax"], n(r))
                            act.wait_ge(sem["pturn"], n(r - 4))
                            for v in range(2):
                                last = act.activation(PR[:, r % 4, v, :], pS[r % 3][:, 256 * v:256 * v + 192], ACT.Exp,
                                                      bias=NM[:, r % 4, v:v + 1], accum_out=SM[:, r % 4, v:v + 1])
                            last.then_inc(sem["probs"], 1)
                        if 2 <= r < U + 2:
                            q = r % 2
                            act.wait_ge(sem["pturn"], n(r - 2))
                            act.wait_ge(sem["outT"], n(r - 4))
                            act.copy(PTM[:, q, :, :], pP[0][:, 0:256].rearrange("p (v n) -> p v n", v=2)).then_inc(sem["pmain"], 1)
                        if r >= 3 and (r - 3) % TT == TT - 1:
                            j = (r - 3) // TT
                            act.wait_ge(sem["outT"], n(r - 3))
                            act.copy(OT[:, j, :], pO[:, :]).then_inc(sem["outTcopy"], 1)

            @block.vector
            def _(dve):
                dve.memset(POWT[:, :], -0.5).then_inc(sem["zero"], 1)
                dve.memset(KT[:, :, :, :], 0.0).then_inc(sem["zero"], 1)
                dve.wait_ge(sem["const"], SEED + 16 * 9)
                dve.wait_ge(sem["zero"], SEED + 2)
                def moments(b, src, at, t0):
                    for t in (t0, t0 + 1):
                        last = dve.bn_stats(BN[:, t, :], src[:, t, :])
                    if t0:
                        last.then_inc(sem["nstep"], 1)

                def variance(b, at, e):
                    steps = Steps(b, 6)
                    steps.k = 2 * e
                    dve.wait_ge(sem["nstep"], steps.next())
                    dve.memset(VE[:, 0:1], 0.0)
                    for t in range(TT):
                        last = dve.bn_aggr(MV[:, at + t, :], BN[:, t, :])
                    last.then_inc(sem["nstep"], 1)
                    dve.wait_ge(sem["nstep"], steps.next())
                    if e:
                        dve.tensor_tensor(MV[:, 2 * TT:3 * TT, 0], MV[:, at:at + TT, 0], MV[:, at:at + TT, 0], ALU.mult).then_inc(sem["nstep"], 1)
                        dve.wait_ge(sem["nstep"], steps.next())
                        dve.tensor_tensor(MV[:, 2 * TT:3 * TT, 1], MV[:, 2 * TT:3 * TT, 0], MV[:, at:at + TT, 1], ALU.add).then_inc(sem["nstep"], 1)
                        dve.wait_ge(sem["nstep"], steps.next())
                        dve.tensor_scalar(VE[:, 2 * TT:3 * TT], MV[:, 2 * TT:3 * TT, 1], 1e-24 / D, None, ALU.max)
                    dve.tensor_scalar(VE[:, at:at + TT], MV[:, at:at + TT, 1], EPS, None, ALU.add).then_inc(sem["stats"], 1)

                def normed(b, src, dst, at, e):
                    dve.wait_ge(sem["rstd"], after(b, 2, e))
                    for t in range(TT):
                        last = dve.tensor_scalar(dst[:, t, :], src[:, t, :], MV[:, at + t, 0:1], RD[:, at + t:at + t + 1], ALU.subtract, ALU.mult)
                    return last

                def rms_rows(b):
                    dve.wait_ge(sem["xr_out"], b * 16 + SEED)
                    for t in range(TT):
                        last = dve.tensor_scalar(XR[:, t, :], XA[:, t, :], RD[:, 2 * TT + t:2 * TT + t + 1], None, ALU.mult)
                    last.then_inc(sem["xr"], 1)

                def routing(b, t):
                    if t == 0:
                        dve.wait_ge(sem["route_out"], b * 16 + SEED)
                        dve.wait_ge(sem["s"], after(b, 1, -1))
                    for r in range(2):
                        last = dve.tensor_tensor_reduce(out=SCR[:, :].unsqueeze(1), in0=XA[:, t, :].unsqueeze(1), in1=RT[:, r, :].unsqueeze(1), scale=1.0, scalar=0.0,
                                                        op0=ALU.mult, op1=ALU.add, accum_out=SS[:, r, t:t + 1])
                        if not (t == TT - 1 and r == 1):
                            last.then_inc(sem["rows"], 1)
                            dve.wait_ge(sem["rows"], after(b, 7, t * 2 + r))
                    if t == TT - 1:
                        last.then_inc(sem["s"], 1)

                def prepare(b, k):
                    if k == 0:
                        dve.wait_ge(sem["loaded"], b * 16 + (SEED + 16))
                    if k in (0, 1):
                        moments(b, X, 0, 2 * k)
                    if k == 2:
                        variance(b, 0, 0)
                    if k == 4:
                        normed(b, X, XA, 0, 0).then_inc(sem["read"], 1)
                        dve.wait_ge(sem["read"], after(b, 1, 0))
                    if k in (5, 6):
                        moments(b, XA, TT, 2 * (k - 5))
                    if k == 7:
                        variance(b, TT, 1)
                    if k == 9:
                        dve.wait_ge(sem["full"], after(b, len(jobs), NX[-1] - len(jobs)))
                        normed(b, XA, XB, TT, 1).then_inc(sem["norm"], 1)
                    if k == 10:
                        rms_rows(b)
                    if k >= 12:
                        routing(b, k - 12)

                for k in range(16):
                    prepare(0, k)
                with dve.Fori(0, B) as i:
                    steps = Steps(i, U)

                    def empty(m):
                        kind, k = jobs[m]
                        w = pW[m % 2]
                        dve.wait_ge(sem["full"], after(i, len(jobs), m))
                        if kind == "x":
                            dve.tensor_scalar(XBT[:, k, :], w[:, :], LNW[:, k:k + 1], LNB[:, k:k + 1], ALU.mult, ALU.add).then_inc(sem["dve_empty"], 1)
                        if kind == "q":
                            dve.tensor_scalar(QT[:, k, :], w[:, :], SCALE, None, ALU.mult).then_inc(sem["dve_empty"], 1)
                        if kind == "k":
                            dve.tensor_copy(KT[0:64, k, 0, :], w[0:64, :])
                            dve.tensor_copy(KT[64:128, k, 1, :], w[64:128, :]).then_inc(sem["dve_empty"], 1)
                        if kind == "v":
                            dve.tensor_copy(V[:, k, :], w[:, :])
                            dve.tensor_copy(VL[:, k, :], w[64:128, :]).then_inc(sem["dve_empty"], 1)
                        if kind == "o":
                            dve.scalar_tensor_tensor(out=Y[:, k, :], in0=w[:, :], scalar=TG[:, 2:3], in1=XL[:, k, :],
                                                     op0=ALU.mult, op1=ALU.add).then_inc(sem["dve_empty"], 1)

                    for m in range(NO[0]):
                        if banks.engine[m] == "dve":
                            empty(m)
                    n = lambda k: after(i, U, k)
                    for r in range(U + 2):
                        if r < U:
                            dve.wait_ge(sem["scores"], n(r))
                            dve.wait_ge(sem["probs"], n(r - 4))
                            dve.tensor_reduce(NM[:, r % 4, :], pS[r % 3][:, :].rearrange("p (v n) -> p v n", v=2)[:, :, 0:192],
                                              axis=AX.X, op=ALU.max, negate=True).then_inc(sem["negmax"], 1)
                        if 1 <= r <= U:
                            q = (r - 1) % 4
                            dve.wait_ge(sem["probs"], n(r - 1))
                            dve.reciprocal(RI[:, q, :], SM[:, q, :]).then_inc(sem["step"], 1)
                            dve.wait_ge(sem["step"], steps.next())
                            for v in range(2):
                                last = dve.tensor_scalar(PR[:, q, v, :], PR[:, q, v, :], RI[:, q, v:v + 1], None, ALU.mult)
                            last.then_inc(sem["scaled"], 1)
                        if r < U:
                            prepare(i + 1, r)
                        if r >= 2:
                            dve.wait_ge(sem["pturn"], n(r - 2))
                            dve.wait_ge(sem["outT"], n(r - 4))
                            dve.tensor_copy(PTE[:, r % 2, :, :], pP[1][0:64, 0:256].rearrange("p (v n) -> p v n", v=2)).then_inc(sem["pextra"], 1)
                    steps.close()
                    dve.wait_ge(sem["tanh"], SEED + 1)
                    dve.wait_ge(sem["resid"], i * 16 + (SEED + 16))
                    dve.wait_ge(sem["out"], i * 16 + SEED)
                    for m in NO:
                        empty(m)

            @block.tensor
            def _(pe):
                pe.wait_ge(sem["const"], SEED + 16 * 9)
                pe.wait_ge(sem["zero"], SEED + 2)
                with pe.Fori(0, B) as i:
                    def ready(m):
                        for e in ("act", "dve"):
                            pe.wait_ge(emptied[e], banks.emptied(i, m, e))

                    def free(m):
                        before = banks.engine[(m - 2) % len(jobs)]
                        pe.wait_ge(emptied[before], banks.emptied(i, m - 2, before))

                    for m, (kind, k) in enumerate(jobs):
                        if kind == "o":
                            continue
                        if kind == "x" and k == 0:
                            pe.wait_ge(sem["norm"], after(i, 1, 0))
                        if kind == "q" and k == 0:
                            ready(NX[-1])
                        free(m)
                        w = pW[m % 2]
                        for c in range(4):
                            if kind == "x":
                                last = pe.transpose(w[:, P * c:P * c + P], XB[:, c, P * k:P * k + P], IDF[:, :])
                            if kind in "qk":
                                o = (kind == "k") * D + P * k
                                last = pe.matmul(w[:, :], WQKV[:, c, o:o + P], XBT[:, c, :], start=c == 0, stop=c == 3)
                            if kind == "v":
                                last = pe.matmul(w[:, :], XBT[:, c, P * k:P * k + P], WQKV[:, c, 2 * D:3 * D], start=c == 0, stop=c == 3)
                        last.then_inc(sem["full"], 1)
                    ready(NVV[-1])
                    n = lambda k: after(i, U, k)
                    for r in range(U + 3):
                        if r < U:
                            j, t = r // TT, r % TT
                            pe.wait_ge(sem["probs"], n(r - 3 if r >= 3 else -1))
                            for v in range(2):
                                o = 256 * v
                                pe.matmul(pS[r % 3][:, o:o + P], QT[:, j, P * t:P * t + P], KT[:, j, v, P * t:P * t + P], start=True, stop=True)
                                if t == 0:
                                    pe.matmul(pS[r % 3][0:64, o + P:o + 192], IDB[:, 0:64], NEGB[:, :], start=True, stop=True)
                                else:
                                    pe.matmul(pS[r % 3][0:64, o + P:o + 192], QT[:, j, P * t:P * t + 64], KT[:, j, v, P * t - 64:P * t], start=True, stop=True)
                                if t == TT - 1:
                                    last = pe.matmul(pS[r % 3][64:128, o + P:o + 192], IDB[:, 64:128], NEGB[:, :], start=True, stop=True)
                                else:
                                    last = pe.matmul(pS[r % 3][64:128, o + P:o + 192], QT[:, j, P * t + 64:P * t + P],
                                                     KT[:, j, v, P * t + P:P * t + 192], start=True, stop=True)
                            last.then_inc(sem["scores"], 1)
                        if 2 <= r < U + 2:
                            q = (r - 2) % 4
                            pe.wait_ge(sem["scaled"], n(r - 2))
                            pe.wait_ge(sem["pmain"], n(r - 3))
                            pe.wait_ge(sem["pextra"], n(r - 3))
                            for v in range(2):
                                pe.transpose(pP[0][:, P * v:P * v + P], PR[:, q, v, 0:P], IDF[:, :])
                                last = pe.transpose(pP[1][0:64, P * v:P * v + P], PR[:, q, v, P:192], IDF[:, :])
                            last.then_inc(sem["pturn"], 1)
                        if r >= 3:
                            q = (r - 3) % 2
                            j, t = (r - 3) // TT, (r - 3) % TT
                            pe.wait_ge(sem["pmain"], n(r - 3))
                            pe.wait_ge(sem["pextra"], n(r - 3))
                            if t == 0:
                                pe.wait_ge(sem["outTcopy"], after(i, J, j - 1))
                            for v in range(2):
                                h = 2 * j + v
                                vc = slice(64 * h, 64 * h + 64)
                                dst = pO[64 * v:64 * v + 64, P * t:P * t + P]
                                last = pe.matmul(dst, V[:, t, vc], PTM[:, q, v, :], start=True, stop=False, skip_group_check=True)
                                if t > 0:
                                    last = pe.matmul(dst[:, 0:64], VL[:, t - 1, vc], PTE[:, q, v, 0:64], start=False, stop=t == TT - 1, skip_group_check=True)
                                if t < TT - 1:
                                    last = pe.matmul(dst[:, 64:P], V[0:64, t + 1, vc], PTE[:, q, v, 64:P], start=False, stop=True, skip_group_check=True)
                            last.then_inc(sem["outT"], 1)
                    pe.wait_ge(sem["outTcopy"], after(i, J, J - 1))
                    for m in NO:
                        k = jobs[m][1]
                        free(m)
                        for c in range(4):
                            last = pe.matmul(pW[m % 2][:, :], OT[:, c, P * k:P * k + P], WO[:, c, :], start=c == 0, stop=c == 3)
                        last.then_inc(sem["full"], 1)


def phase_route(nc, keep, a, s_route, sel, qsel, qidx):
    NQ, ITERS, LAPS, RISE = 256, 50, 7, 6.0
    WINDOWS = (ITERS - 1) // LAPS
    assert WINDOWS * LAPS == ITERS - 1
    R2, QT2 = 2 * B, NQ // P
    with ExitStack() as ctx:
        def sb(name, shape, dt=f32):
            return ctx.enter_context(nc.sbuf_tensor("r_" + name, shape, dt))

        names = ["const", "loaded", "turned", "copied", "step", "low", "start", "window", "log", "kth", "expd", "rows", "turned2", "out", "stored", "top"]
        sem = open_phase(nc, keep, ["r_" + n for n in names])
        sem = {n: sem["r_" + n] for n in names}
        u32 = mybir.dt.uint32
        SA = sb("sa", [P, B, 2, TT])
        SG = sb("sg", [P, TT, R2])
        IDF, LK, BASE = sb("idf", [P, P]), sb("lk", [R2, 2]), sb("base", [P, B])
        SR, T, E, MN = sb("sr", [R2, S]), sb("t", [R2, S]), sb("e", [R2, S]), sb("mn", [R2, S])
        SMX, NA, ML, NB, NBC, SU, C, LG = (sb(n, [R2, 1]) for n in ("smx", "na", "ml", "nb", "nbc", "su", "c", "lg"))
        WK, M8, I8, IF = sb("wk", [B, S]), sb("m8", [B, NQ]), sb("i8", [B, NQ], u32), sb("if", [B, NQ])
        OUTW, OUTN, QW = sb("outw", [R2, S]), sb("outn", [B, S]), sb("qw", [B, NQ])
        SEL, QSEL, QIDX = sb("sel", [P, TT, 3 * B]), sb("qsel", [P, QT2, B]), sb("qidx", [P, QT2, B], u32)
        ps = [ctx.enter_context(nc.psum_tensor(f"r_ps{i}", [P, 512], f32)) for i in range(2)]
        with nc.Block() as block:
            @block.sync
            def _(sp):
                sp.dma_start(IDF[:, :], a["idf"]).then_inc(sem["const"], 16)
                sp.dma_start(LK[:, :], a["router_k"]).then_inc(sem["const"], 16)
                sp.dma_start(BASE[:, :], a["batch_base"]).then_inc(sem["const"], 16)
                sp.dma_start(SA[:, :, :, :].rearrange("p b r t -> p b (r t)"), s_route.rearrange("b p n -> p b n")).then_inc(sem["loaded"], 16)
                sp.wait_ge(sem["out"], SEED + 1)
                sp.dma_start(sel, SEL[:, :, :]).then_inc(sem["stored"], 16)
                sp.dma_start(qsel, QSEL[:, :, :]).then_inc(sem["stored"], 16)
                sp.dma_start(qidx, QIDX[:, :, :]).then_inc(sem["stored"], 16)
                sp.wait_ge(sem["stored"], SEED + 48)

            @block.tensor
            def _(pe):
                pe.wait_ge(sem["const"], SEED + 48)
                pe.wait_ge(sem["copied"], SEED + 1)
                for t in range(TT):
                    last = pe.transpose(ps[0][0:R2, P * t:P * t + P], SG[:, t, :], IDF[:, :])
                last.then_inc(sem["turned"], 1)
                pe.wait_ge(sem["rows"], SEED + 1)
                pe.wait_ge(sem["copied"], SEED + 2)
                for t in range(TT):
                    pe.transpose(ps[1][:, 24 * t:24 * t + R2], OUTW[:, P * t:P * t + P], IDF[0:R2, 0:R2])
                    pe.transpose(ps[1][:, 24 * t + R2:24 * t + 24], OUTN[:, P * t:P * t + P], IDF[0:B, 0:B])
                for t in range(QT2):
                    pe.transpose(ps[1][:, 128 + B * t:128 + B * t + B], QW[:, P * t:P * t + P], IDF[0:B, 0:B])
                    last = pe.transpose(ps[1][:, 192 + B * t:192 + B * t + B], IF[:, P * t:P * t + P], IDF[0:B, 0:B])
                last.then_inc(sem["turned2"], 1)

            @block.scalar
            def _(act):
                with act.Fori(0, WINDOWS) as i:
                    act.wait_ge(sem["low"], after(i, 1, 0))
                    act.activation(E[:, :], T[:, :], ACT.Exp, bias=NB[:, 0:1])
                    act.activation(C[:, :], NBC[:, :], ACT.Exp).then_inc(sem["start"], 1)
                    act.wait_ge(sem["window"], after(i, 1, 0))
                    act.activation(LG[:, :], C[:, :], ACT.Ln).then_inc(sem["log"], 1)
                act.wait_ge(sem["kth"], SEED + 1)
                act.activation(E[:, :], T[:, :], ACT.Exp).then_inc(sem["expd"], 1)

            @block.vector
            def _(dve):
                dve.wait_ge(sem["loaded"], SEED + 16)
                dve.tensor_copy(SG[:, :, :].rearrange("p t (r b) -> p t r b", r=2), SA[:, :, :, :].rearrange("p b r t -> p t r b")).then_inc(sem["copied"], 1)
                dve.wait_ge(sem["turned"], SEED + 1)
                dve.tensor_copy(SR[:, :], ps[0][0:R2, :]).then_inc(sem["copied"], 1)
                dve.wait_ge(sem["copied"], SEED + 2)
                dve.reduce_max(SMX[:, :], SR[:, :], axis=AX.X)
                dve.wait_ge(sem["const"], SEED + 48)
                dve.tensor_copy(NA[:, :], LK[:, 0:1]).then_inc(sem["top"], 1)
                dve.wait_ge(sem["top"], SEED + 1)
                with dve.Fori(0, WINDOWS) as i:
                    steps = Steps(i, 2 * LAPS + 1)
                    dve.tensor_scalar(ML[:, :], SMX[:, :], NA[:, 0:1], -1.0, ALU.min, ALU.mult)
                    dve.tensor_scalar(T[:, :], SR[:, :], NA[:, 0:1], RISE, ALU.subtract, ALU.min).then_inc(sem["step"], 1)
                    dve.wait_ge(sem["step"], steps.next())
                    dve.tensor_scalar(NB[:, :], NA[:, :], ML[:, 0:1], None, ALU.add)
                    dve.tensor_scalar(NBC[:, :], NA[:, :], ML[:, 0:1], 80.0, ALU.add, ALU.min).then_inc(sem["low"], 1)
                    dve.wait_ge(sem["start"], after(i, 1, 0))
                    for lap in range(LAPS):
                        dve.tensor_scalar(MN[:, :], E[:, :], C[:, 0:1], None, ALU.min, ALU.add, accum_out=SU[:, 0:1]).then_inc(sem["step"], 1)
                        dve.wait_ge(sem["step"], steps.next())
                        last = dve.tensor_scalar(C[:, :], SU[:, :], LK[:, 1:2], None, ALU.mult)
                        if lap < LAPS - 1:
                            last.then_inc(sem["step"], 1)
                            dve.wait_ge(sem["step"], steps.next())
                    last.then_inc(sem["window"], 1)
                    dve.wait_ge(sem["log"], after(i, 1, 0))
                    dve.tensor_scalar(NA[:, :], LG[:, :], ML[:, 0:1], None, ALU.subtract).then_inc(sem["step"], 1)
                    dve.wait_ge(sem["step"], steps.next())
                    steps.close()
                dve.tensor_scalar(T[:, :], SR[:, :], NA[:, 0:1], 0.0, ALU.subtract, ALU.min).then_inc(sem["kth"], 1)
                dve.wait_ge(sem["expd"], SEED + 1)
                dve.tensor_scalar(OUTW[:, :], E[:, :], -1.0, 1.0, ALU.mult, ALU.add)
                dve.tensor_copy(WK[:, :], E[0:B, :]).then_inc(sem["top"], 1)
                dve.wait_ge(sem["top"], SEED + 2)
                dve.tensor_tensor(OUTW[:, :], OUTW[:, :], E[:, :], ALU.add)
                k = 2
                for r in range(NQ // 8):
                    eight = slice(8 * r, 8 * r + 8)
                    dve.max(M8[:, eight], WK[:, :]).then_inc(sem["top"], 1)
                    dve.wait_ge(sem["top"], SEED + k + 1)
                    dve.max_index(I8[:, eight], M8[:, eight], WK[:, :])
                    dve.match_replace(WK[:, :], M8[:, eight], WK[:, :], -1.0).then_inc(sem["top"], 1)
                    dve.wait_ge(sem["top"], SEED + k + 2)
                    k += 2
                dve.tensor_scalar(OUTN[:, :], WK[:, :], 0.0, None, ALU.is_ge)
                dve.tensor_copy(IF[:, :], I8[:, :])
                dve.tensor_scalar(QW[:, :], M8[:, :], -1.0, 1.0, ALU.mult, ALU.add).then_inc(sem["top"], 1)
                dve.wait_ge(sem["top"], SEED + k + 1)
                dve.tensor_tensor(QW[:, :], QW[:, :], M8[:, :], ALU.add).then_inc(sem["rows"], 1)
                dve.wait_ge(sem["turned2"], SEED + 1)
                dve.tensor_copy(SEL[:, :, :], ps[1][:, 0:24 * TT].rearrange("p (t n) -> p t n", n=24))
                dve.tensor_copy(QSEL[:, :, :], ps[1][:, 128:128 + QT2 * B].rearrange("p (t b) -> p t b", b=B))
                dve.tensor_tensor(QIDX[:, :, :], ps[1][:, 192:192 + QT2 * B].rearrange("p (t b) -> p t b", b=B),
                                  BASE[:, :].unsqueeze(1).broadcast_to([P, QT2, B]), ALU.add).then_inc(sem["out"], 1)

def phase_heavy(nc, keep, a, xr, x1l, sel, qsel, qidx, x2):
    H, DH = 8, 64
    SCALE = DH ** -0.5
    J = 4
    QT2 = 2
    NQ_ = QT2 * P
    U = H * QT2
    LP, LV = 2, 3
    jobs = [("x", c) for c in range(4)] + [("k", j) for j in range(4)] + [("v", t) for t in range(4)] + \
           [("g", c) for c in (0, 2)] + [("q", j) for j in (0, 2)] + \
           [("n", t) for t in range(QT2)] + [("z", j) for j in range(4)] + [("o", t) for t in range(QT2)]
    banks = Banks(jobs, lambda m, job: "dve" if job[0] in "on" else "act" if job[0] == "z" else ("act", "dve")[m % 2])
    NX, NK, NVV, NG, NQ, NN, NZ, NO = (banks.of(k) for k in "xkvgqnzo")
    with ExitStack() as ctx:
        def sb(name, shape, dt=f32):
            return ctx.enter_context(nc.sbuf_tensor("h_" + name, shape, dt))

        names = ["const", "loaded", "resid", "tanh", "zero", "full", "act_empty", "dve_empty", "scores", "negmax", "probs",
                 "scaled", "pturn", "pcopy", "outT", "outTcopy", "step", "base_out", "base", "weights", "nullp", "idx", "qloaded", "go", "qnext"]
        h_gather = keep.enter_context(nc.semaphore("h_gather"))
        h_scatter = keep.enter_context(nc.semaphore("h_scatter"))
        sem = open_phase(nc, keep, ["h_" + n for n in names])
        sem = {n: sem["h_" + n] for n in names}
        emptied = {"act": sem["act_empty"], "dve": sem["dve_empty"]}
        WQ, WK, WV, WO = (sb(n, [P, CT, D]) for n in ("wq", "wk", "wv", "wo"))
        GA, NKB, NVB, NQB = sb("ga", [P, CT]), sb("nkb", [P, J, 2]), sb("nvb", [P, J, P]), sb("nqb", [P, D])
        SEL, TSEL = sb("sel", [P, TT, 3 * B]), sb("tsel", [P, TT, 3 * B])
        QSEL, QIDX = sb("qsel", [P, QT2, B]), sb("qidx", [P, QT2, B], mybir.dt.uint32)
        QROW = sb("qrow", [P, 2, QT2], mybir.dt.uint32)
        IDF = sb("idf", [P, P])
        GT, TG = sb("gt", [P, 4]), sb("tg", [P, 4])
        X, XL = sb("x", [P, TT, D]), sb("xl", [P, TT, D])
        XG, XLG, YG = (sb(n, [P, QT2, D]) for n in ("xg", "xlg", "yg"))
        XGT = sb("xgT", [P, CT, NQ_])
        XT = sb("xT", [P, CT, S])
        QT, KT, V = sb("qT", [P, J, NQ_]), sb("kT", [P, J, 2, S]), sb("v", [P, TT, D])
        WCOL, QCOL = sb("wcol", [P, TT, 3]), sb("qcol", [P, QT2])
        NS = sb("ns", [P, QT2, H])
        PR, PT = sb("pr", [P, 4, S]), sb("pT", [P, 2, TT, NQ_])
        SC = sb("sc", [P, 4, 8])
        PN, PNT = sb("pn", [P, 2, QT2, P]), sb("pnT", [P, NQ_])
        OT, Y = sb("oT", [P, J, NQ_]), sb("y", [P, TT, D])
        bank = [ctx.enter_context(nc.psum_tensor(f"h_ps{i}", [P, 512], f32)) for i in range(8)]
        pW, pS, pP, pO = bank[0:2], bank[2:5], bank[5:7], bank[7]

        with nc.Block() as block:
            @block.sync
            def _(sp):
                for dst, src in ((WQ[:, :, :], a["hwqT"]), (WK[:, :, :], a["hwkT"]), (WV[:, :, :], a["hwvT"]), (WO[:, :, :], a["hwoT"]),
                                 (GA[:, :], a["gamma"]), (NKB[:, :, :], a["null_k"]), (NVB[:, :, :], a["null_v"]), (NQB[:, :], a["null_q"]),
                                 (SEL[:, :, :], sel), (QSEL[:, :, :], qsel), (QIDX[:, :, :], qidx), (IDF[:, :], a["idf"]), (GT[:, :], a["gates"])):
                    sp.dma_start(dst, src).then_inc(sem["const"], 16)
                with sp.Fori(0, B) as i:
                    row = lambda t: t[bass.ds(i, 1), :, :].rearrange("o (t p) d -> p (o t) d", p=P)
                    sp.wait_ge(sem["full"], after(i, len(jobs), NX[-1] - len(jobs)))
                    sp.dma_start(X[:, :, :], row(xr)).then_inc(sem["loaded"], 16)
                    sp.wait_ge(sem["base"], after(i, 1, -1))
                    sp.dma_start(XL[:, :, :], row(x1l)).then_inc(sem["resid"], 16)
                    sp.wait_ge(sem["base"], after(i, 1, 0))
                    sp.dma_start(row(x2), Y[:, :, :]).then_inc(sem["base_out"], 16)
                sp.wait_ge(sem["base_out"], SEED + 16 * B)

            @block.gpsimd
            def _(pool):
                flat = lambda t: t.rearrange("b s d -> (b s) d")

                def gather(b, parity):
                    for t in range(QT2):
                        for dst, src in ((XG, xr), (XLG, x1l)):
                            pool.indirect_dma_start(out=dst[:, t, :], out_offset=None, in_=flat(src),
                                                    in_offset=bass.IndirectOffsetOnAxis(ap=QROW[:, parity, t:t + 1], axis=0)).then_inc(h_gather, 16)

                pool.wait_ge(sem["idx"], SEED + 1)
                gather(0, 0)
                with pool.Fori(0, B // 2) as i2:
                    for u in range(2):
                        i = i2 * 2 + u
                        pool.wait_ge(sem["dve_empty"], banks.emptied(i, NO[-1], "dve"))
                        pool.wait_ge(sem["base_out"], i * 16 + (SEED + 16))
                        pool.sem_inc(sem["go"], 1)
                        for t in range(QT2):
                            pool.indirect_dma_start(out=flat(x2), out_offset=bass.IndirectOffsetOnAxis(ap=QROW[:, u, t:t + 1], axis=0),
                                                    in_=YG[:, t, :], in_offset=None).then_inc(h_scatter, 16)
                        pool.wait_ge(sem["idx"], after(i, 1, 1))
                        pool.sem_inc(sem["go"], 1)
                        gather(i + 1, 1 - u)
                        pool.wait_ge(h_scatter, i * 32 + 32)
                        pool.sem_inc(sem["qnext"], 1)
                pool.wait_ge(h_gather, 64 * (B + 1))

            @block.scalar
            def _(act):
                act.wait_ge(sem["const"], SEED + 16 * 13)
                act.activation(TG[:, :], GT[:, :], ACT.Tanh).then_inc(sem["tanh"], 1)
                with act.Fori(0, B) as i:
                    def empty(m):
                        kind, k = jobs[m]
                        w = pW[m % 2]
                        act.wait_ge(sem["full"], after(i, len(jobs), m))
                        if kind == "x":
                            act.mul(XT[:, k, :], w[:, :], GA[:, k:k + 1]).then_inc(sem["act_empty"], 1)
                        if kind == "g":
                            act.mul(XGT[:, k, :], w[:, 0:NQ_], GA[:, k:k + 1])
                            act.mul(XGT[:, k + 1, :], w[:, NQ_:], GA[:, k + 1:k + 2]).then_inc(sem["act_empty"], 1)
                        if kind == "q":
                            act.mul(QT[:, k:k + 2, :], w[:, :].rearrange("p (j q) -> p j q", j=2), SCALE).then_inc(sem["act_empty"], 1)
                        if kind == "k":
                            act.copy(KT[0:64, k, 0, :], w[0:64, :])
                            act.copy(KT[64:128, k, 1, :], w[64:128, :]).then_inc(sem["act_empty"], 1)
                        if kind == "v":
                            act.wait_ge(sem["weights"], after(i, 1, 0))
                            act.mul(V[:, k, :], w[:, :], WCOL[:, k, 1:2]).then_inc(sem["act_empty"], 1)
                        if kind == "z":
                            act.copy(PNT[:, :], w[:, 0:NQ_]).then_inc(sem["act_empty"], 1)

                    for m in range(NN[0]):
                        if banks.engine[m] == "act":
                            empty(m)
                    n = lambda k: after(i, U, k)
                    for r in range(U + LV + 1):
                        if r < U:
                            h, t = r // QT2, r % QT2
                            act.wait_ge(sem["negmax"], n(r))
                            act.wait_ge(sem["pturn"], n(r - 4))
                            act.activation(PR[:, r % 4, :], pS[r % 3][:, :], ACT.Exp, bias=SC[:, r % 4, 0:1], accum_out=SC[:, r % 4, 1:2])
                            act.activation(SC[:, r % 4, 2:3], NS[:, t, h:h + 1], ACT.Exp, bias=SC[:, r % 4, 0:1]).then_inc(sem["probs"], 1)
                        if LP <= r < U + LP:
                            h, t = (r - LP) // QT2, (r - LP) % QT2
                            act.wait_ge(sem["pturn"], n(r - LP))
                            act.wait_ge(sem["outT"], after(i, H, h - 2))
                            act.copy(PT[:, h % 2, :, P * t:P * t + P], pP[r % 2][:, :].rearrange("p (k q) -> p k q", k=TT)).then_inc(sem["pcopy"], 1)
                        if r >= LV and (r - LV) % (2 * QT2) == 2 * QT2 - 1:
                            empty(NZ[(r - LV) // (2 * QT2)])
                        if r > LV and (r - LV - 1) % (2 * QT2) == 2 * QT2 - 1:
                            j = (r - LV - 1) // (2 * QT2)
                            act.wait_ge(sem["outT"], after(i, H, 2 * j + 1))
                            act.copy(OT[:, j, :], pO[:, 0:NQ_]).then_inc(sem["outTcopy"], 1)

            @block.vector
            def _(dve):
                dve.memset(PN[:, :, :, :], 0.0).then_inc(sem["zero"], 1)
                dve.memset(KT[:, :, :, :], 0.0).then_inc(sem["zero"], 1)
                dve.wait_ge(sem["const"], SEED + 16 * 13)
                dve.wait_ge(sem["tanh"], SEED + 1)
                dve.wait_ge(sem["zero"], SEED + 2)
                dve.tensor_scalar(TSEL[:, :, :], SEL[:, :, :], TG[:, 2:3], None, ALU.mult).then_inc(sem["zero"], 1)
                dve.wait_ge(sem["zero"], SEED + 3)
                dve.tensor_scalar(QSEL[:, :, :], QSEL[:, :, :], TG[:, 2:3], None, ALU.mult).then_inc(sem["zero"], 1)
                dve.tensor_copy(QROW[:, 0, :], QIDX[:, :, 0]).then_inc(sem["idx"], 1)
                dve.wait_ge(sem["zero"], SEED + 4)
                with dve.Fori(0, B) as i:
                    ahead = dve.snap((i + 1) % B)
                    parity = dve.snap((i + 1) % 2)
                    steps = Steps(i, 3 * U)
                    dve.wait_ge(sem["dve_empty"], banks.emptied(i, -1, "dve"))
                    dve.tensor_copy(QCOL[:, :], QSEL[:, :, bass.ds(i, 1)].rearrange("p t o -> p (t o)"))
                    dve.wait_ge(sem["qnext"], after(i, 1, -1))
                    dve.tensor_copy(QROW[:, bass.ds(parity, 1), :].rearrange("p o t -> p (o t)"), QIDX[:, :, bass.ds(ahead, 1)].rearrange("p t o -> p (t o)")).then_inc(sem["idx"], 1)
                    dve.tensor_copy(WCOL[:, :, 1], SEL[:, :, bass.ds(i + B, 1)].rearrange("p t o -> p (t o)"))
                    dve.tensor_copy(WCOL[:, :, 2], TSEL[:, :, bass.ds(i + 2 * B, 1)].rearrange("p t o -> p (t o)")).then_inc(sem["weights"], 1)
                    dve.wait_ge(sem["weights"], after(i, 1, 0))

                    def empty(m):
                        kind, k = jobs[m]
                        w = pW[m % 2]
                        dve.wait_ge(sem["full"], after(i, len(jobs), m))
                        if kind == "x":
                            dve.tensor_scalar(XT[:, k, :], w[:, :], GA[:, k:k + 1], None, ALU.mult).then_inc(sem["dve_empty"], 1)
                        if kind == "g":
                            dve.tensor_scalar(XGT[:, k, :], w[:, 0:NQ_], GA[:, k:k + 1], None, ALU.mult)
                            dve.tensor_scalar(XGT[:, k + 1, :], w[:, NQ_:], GA[:, k + 1:k + 2], None, ALU.mult).then_inc(sem["dve_empty"], 1)
                        if kind == "q":
                            dve.tensor_scalar(QT[:, k:k + 2, :], w[:, :].rearrange("p (j q) -> p j q", j=2), SCALE, None, ALU.mult).then_inc(sem["dve_empty"], 1)
                        if kind == "k":
                            dve.tensor_copy(KT[0:64, k, 0, :], w[0:64, :])
                            dve.tensor_copy(KT[64:128, k, 1, :], w[64:128, :]).then_inc(sem["dve_empty"], 1)
                        if kind == "v":
                            dve.tensor_scalar(V[:, k, :], w[:, :], WCOL[:, k, 1:2], None, ALU.mult).then_inc(sem["dve_empty"], 1)
                        if kind == "n":
                            dve.tensor_copy(NS[:, k, :], w[:, 0:H]).then_inc(sem["dve_empty"], 1)
                        if kind == "o":
                            dve.scalar_tensor_tensor(out=YG[:, k, :], in0=w[:, :], scalar=QCOL[:, k:k + 1], in1=XLG[:, k, :],
                                                     op0=ALU.mult, op1=ALU.add).then_inc(sem["dve_empty"], 1)

                    for m in range(NZ[0]):
                        if banks.engine[m] == "dve":
                            empty(m)
                    dve.wait_ge(sem["dve_empty"], banks.emptied(i, NN[-1], "dve"))
                    n = lambda k: after(i, U, k)
                    for r in range(U + 1):
                        if r < U:
                            h, t = r // QT2, r % QT2
                            dve.wait_ge(sem["scores"], n(r))
                            dve.wait_ge(sem["scaled"], n(r - 4))
                            dve.reduce_max(SC[:, r % 4, 4:5], pS[r % 3][:, :], axis=AX.X).then_inc(sem["step"], 1)
                            dve.wait_ge(sem["step"], steps.next())
                            dve.tensor_scalar(SC[:, r % 4, 0:1], SC[:, r % 4, 4:5], NS[:, t, h:h + 1], -1.0, ALU.max, ALU.mult).then_inc(sem["negmax"], 1)
                        if r >= 1:
                            q = (r - 1) % 4
                            h, t = (r - 1) // QT2, (r - 1) % QT2
                            dve.wait_ge(sem["probs"], n(r - 1))
                            dve.tensor_scalar(SC[:, q, 5:6], SC[:, q, 1:2], SC[:, q, 2:3], None, ALU.add).then_inc(sem["step"], 1)
                            dve.wait_ge(sem["step"], steps.next())
                            dve.reciprocal(SC[:, q, 3:4], SC[:, q, 5:6]).then_inc(sem["step"], 1)
                            dve.wait_ge(sem["step"], steps.next())
                            if t == 0 and h % 2 == 0:
                                dve.wait_ge(sem["full"], after(i, len(jobs), (NZ[h // 2 - 2] if h >= 4 else NZ[h // 2 + 2] - len(jobs))))
                            dve.tensor_scalar(PN[:, h // 2 % 2, t, h:h + 1], SC[:, q, 2:3], SC[:, q, 3:4], None, ALU.mult)
                            dve.tensor_scalar(PR[:, q, :], PR[:, q, :], SC[:, q, 3:4], None, ALU.mult).then_inc(sem["scaled"], 1)
                        if r in (4, 6, 8, 10):
                            t = (r - 4) // 2
                            if t == 0:
                                dve.wait_ge(sem["resid"], i * 16 + (SEED + 16))
                                dve.wait_ge(sem["base_out"], i * 16 + SEED)
                            last = dve.scalar_tensor_tensor(out=Y[:, t, :], in0=NQB[:, :], scalar=WCOL[:, t, 2:3], in1=XL[:, t, :], op0=ALU.mult, op1=ALU.add)
                            if t == TT - 1:
                                last.then_inc(sem["base"], 1)
                    dve.wait_ge(h_gather, i * 64 + 64)
                    dve.wait_ge(sem["qnext"], after(i, 1, -1))
                    for m in NO:
                        empty(m)
                    steps.close()

            @block.tensor
            def _(pe):
                pe.wait_ge(sem["const"], SEED + 16 * 13)
                pe.wait_ge(sem["zero"], SEED + 2)
                with pe.Fori(0, B) as i:
                    def ready(m):
                        for e in ("act", "dve"):
                            pe.wait_ge(emptied[e], banks.emptied(i, m, e))

                    def free(m):
                        before = banks.engine[(m - 2) % len(jobs)]
                        pe.wait_ge(emptied[before], banks.emptied(i, m - 2, before))

                    for m in range(NZ[0]):
                        kind, k = jobs[m]
                        if kind == "x" and k == 0:
                            pe.wait_ge(sem["loaded"], i * 16 + (SEED + 16))
                        if kind == "k" and k == 0:
                            ready(NX[-1])
                        if kind == "g" and k == 0:
                            pe.wait_ge(h_gather, i * 64 + 64)
                        if kind == "q" and k == 0:
                            ready(NG[-1])
                        if kind == "n":
                            ready(NQ[-1])
                        free(m)
                        w = pW[m % 2]
                        for c in range(4):
                            if kind == "x":
                                last = pe.transpose(w[:, P * c:P * c + P], X[:, c, P * k:P * k + P], IDF[:, :])
                            if kind == "g":
                                g, t = k + c // 2, c % 2
                                last = pe.transpose(w[:, P * c:P * c + P], XG[:, t, P * g:P * g + P], IDF[:, :])
                            if kind == "q":
                                for n in range(2):
                                    last = pe.matmul(w[:, NQ_ * (c // 2):NQ_ * (c // 2) + NQ_], WQ[:, 2 * (c % 2) + n, P * (k + c // 2):P * (k + c // 2) + P],
                                                     XGT[:, 2 * (c % 2) + n, :], start=c % 2 + n == 0, stop=c % 2 + n == 2)
                            if kind == "k":
                                last = pe.matmul(w[:, :], WK[:, c, P * k:P * k + P], XT[:, c, :], start=c == 0, stop=c == 3)
                            if kind == "v":
                                last = pe.matmul(w[:, :], XT[:, c, P * k:P * k + P], WV[:, c, :], start=c == 0, stop=c == 3)
                            if kind == "n":
                                last = pe.matmul(w[:, 2 * c:2 * c + 2], QT[:, c, P * k:P * k + P], NKB[:, c, :], start=True, stop=True)
                        last.then_inc(sem["full"], 1)
                    ready(NVV[-1])
                    n = lambda k: after(i, U, k)
                    for r in range(U + LV):
                        if r < U:
                            h, t = r // QT2, r % QT2
                            pe.wait_ge(sem["probs"], n(r - 3 if r >= 3 else -1))
                            pe.matmul(pS[r % 3][:, :], QT[:, h // 2, P * t:P * t + P], KT[:, h // 2, h % 2, :], start=True, stop=True).then_inc(sem["scores"], 1)
                        if LP <= r < U + LP:
                            q = (r - LP) % 4
                            pe.wait_ge(sem["scaled"], n(r - LP))
                            pe.wait_ge(sem["pcopy"], n(r - LP - 2))
                            for k in range(TT):
                                last = pe.transpose(pP[r % 2][:, P * k:P * k + P], PR[:, q, P * k:P * k + P], IDF[:, :])
                            last.then_inc(sem["pturn"], 1)
                        if r >= LV and (r - LV) % QT2 == QT2 - 1:
                            h = (r - LV) // QT2
                            j, v = h // 2, h % 2
                            if v == 1:
                                free(NZ[j])
                                for t in range(QT2):
                                    last = pe.transpose(pW[NZ[j] % 2][:, P * t:P * t + P], PN[:, j % 2, t, :], IDF[:, :])
                                last.then_inc(sem["full"], 1)
                            pe.wait_ge(sem["pcopy"], n(QT2 * h + QT2 - 1))
                            if v == 0:
                                pe.wait_ge(sem["outTcopy"], after(i, J, j - 1))
                            for k in range(TT):
                                last = pe.matmul(pO[64 * v:64 * v + 64, 0:NQ_], V[:, k, 64 * h:64 * h + 64], PT[:, h % 2, k, :],
                                                 start=k == 0, stop=False, skip_group_check=True)
                            if v == 1:
                                pe.wait_ge(emptied["act"], banks.emptied(i, NZ[j], "act"))
                                last = pe.matmul(pO[:, 0:NQ_], NVB[:, j, :], PNT[:, :], start=False, stop=True, skip_group_check=True)
                            last.then_inc(sem["outT"], 1)
                    pe.wait_ge(sem["outTcopy"], after(i, J, J - 1))
                    for m in NO:
                        k = jobs[m][1]
                        free(m)
                        for c in range(4):
                            last = pe.matmul(pW[m % 2][:, :], OT[:, c, P * k:P * k + P], WO[:, c, :], start=c == 0, stop=c == 3)
                        last.then_inc(sem["full"], 1)


def phase_window(nc, keep, a, x2, x3):
    H, DH = 16, 32
    SCALE = DH ** -0.5
    J = 4
    U = H * TT
    LP, LV = 3, 4
    jobs = [("x", c) for c in range(4)] + [("q", j) for j in range(4)] + [("k", j) for j in range(4)] + \
           [("v", t) for t in range(4)] + [("o", t) for t in range(4)]
    banks = Banks(jobs, lambda m, job: "dve" if job[0] in "vo" else "act")
    NX, NQ, NK, NVV, NO = (banks.of(k) for k in "xqkvo")

    def tiles(t):
        return min(t + 1, 3)
    with ExitStack() as ctx:
        def sb(name, shape, dt=f32):
            return ctx.enter_context(nc.sbuf_tensor("c_" + name, shape, dt))

        names = ["const", "loaded", "resid", "ctx", "tanh", "zero", "read", "nstep", "stats", "rstd", "norm", "full", "act_empty", "dve_empty",
                 "scores", "negmax", "probs", "scaled", "pturn", "pcopy", "outT", "outTcopy", "step", "out", "biased", "once"]
        sem = open_phase(nc, keep, ["c_" + n for n in names])
        sem = {n: sem["c_" + n] for n in names}
        emptied = {"act": sem["act_empty"], "dve": sem["dve_empty"]}
        WQ, WK, WV, WO = (sb(n, [P, CT, D]) for n in ("wq", "wk", "wv", "wo"))
        BQ, BK, BQS, BV, BO = sb("bq", [P, CT]), sb("bk", [P, CT]), sb("bqs", [P, CT]), sb("bv", [P, D]), sb("bo", [P, D])
        IDF, IDB, MASK = sb("idf", [P, P]), sb("idb", [P, P], bf16), sb("mask", [P, 3 * P], bf16)
        GT, TG = sb("gt", [P, 4]), sb("tg", [P, 4])
        X, XL, XB, C = (sb(n, [P, TT, D]) for n in ("x", "xl", "xb", "cT"))
        XT, QT, V = sb("xT", [P, CT, S]), sb("qT", [P, J, S]), sb("v", [P, TT, D])
        KT = sb("kT", [P, J, 4, S])
        BN, MV, VE, RD, POWT = sb("bn", [P, TT, 6]), sb("mv", [P, TT, 2]), sb("ve", [P, TT]), sb("rd", [P, TT]), sb("pow", [P, TT])
        PR, PT = sb("pr", [P, 4, 3 * P]), sb("pT", [P, 2, 3 * P])
        NM, SM, RI = sb("nm", [P, 4]), sb("sm", [P, 4]), sb("ri", [P, 4])
        OT, Y = sb("oT", [P, J, S]), sb("y", [P, TT, D])
        bank = [ctx.enter_context(nc.psum_tensor(f"c_ps{i}", [P, 512], f32)) for i in range(8)]
        pW, pS, pP, pO = bank[0:2], bank[2:5], bank[5:7], bank[7]
        with nc.Block() as block:
            @block.sync
            def _(sp):
                for dst, src in ((WQ[:, :, :], a["xwqT"]), (WK[:, :, :], a["xwkT"]), (WV[:, :, :], a["xwvT"]), (WO[:, :, :], a["xwoT"]),
                                 (BQ[:, :], a["xbq"]), (BK[:, :], a["xbk"]), (BV[:, :], a["xbv"]), (BO[:, :], a["xbo"]),
                                 (IDF[:, :], a["idf"]), (IDB[:, :], a["idb"]), (MASK[:, :], a["mask_w"]), (GT[:, :], a["gates"])):
                    sp.dma_start(dst, src).then_inc(sem["const"], 16)
                sp.dma_start(X[:, :, :], x2[0, :, :].rearrange("(t p) d -> p t d", p=P)).then_inc(sem["loaded"], 16)
                with sp.Fori(0, B) as i:
                    row = lambda t, b=i: t[bass.ds(b, 1), :, :].rearrange("o (t p) d -> p (o t) d", p=P)
                    ahead = sp.snap((i + 1) % B)
                    sp.wait_ge(sem["read"], after(i, 1, 0))
                    sp.dma_start(X[:, :, :], row(x2, ahead)).then_inc(sem["loaded"], 16)
                    sp.wait_ge(sem["full"], after(i, len(jobs), NVV[-1] - len(jobs)))
                    sp.dma_start(C[:, :, :], a["ctxT"][bass.ds(i, 1), :, :, :].rearrange("o p c n -> (o p) c n")).then_inc(sem["ctx"], 16)
                    sp.wait_ge(sem["dve_empty"], banks.emptied(i, -1, "dve"))
                    sp.dma_start(XL[:, :, :], row(x2)).then_inc(sem["resid"], 16)
                    sp.wait_ge(sem["dve_empty"], banks.emptied(i, NO[-1], "dve"))
                    sp.dma_start(row(x3), Y[:, :, :]).then_inc(sem["out"], 16)
                sp.wait_ge(sem["out"], SEED + 16 * B)

            @block.gpsimd
            def _(pool):
                pool.wait_ge(sem["once"], SEED + 1)
                pool.wait_ge(sem["stats"], SEED + 1)
                pool.tensor_tensor(RD[:, :], VE[:, :], POWT[:, :], ALU.pow).then_inc(sem["rstd"], 1)
                with pool.Fori(0, B) as i:
                    pool.wait_ge(sem["resid"], i * 16 + (SEED + 16))
                    for t in range(TT):
                        last = pool.tensor_tensor(XL[:, t, :], XL[:, t, :], BO[:, :], ALU.add)
                    last.then_inc(sem["biased"], 1)
                    pool.wait_ge(sem["stats"], after(i, 1, 1))
                    pool.tensor_tensor(RD[:, :], VE[:, :], POWT[:, :], ALU.pow).then_inc(sem["rstd"], 1)

            @block.scalar
            def _(act):
                act.wait_ge(sem["const"], SEED + 16 * 12)
                act.activation(TG[:, :], GT[:, :], ACT.Tanh).then_inc(sem["tanh"], 1)
                act.mul(BQS[:, :], BQ[:, :], SCALE).then_inc(sem["tanh"], 1)
                act.wait_ge(sem["tanh"], SEED + 2)
                with act.Fori(0, B) as i:
                    for m in range(NVV[0]):
                        kind, k = jobs[m]
                        w = pW[m % 2]
                        act.wait_ge(sem["full"], after(i, len(jobs), m))
                        if kind == "x":
                            last = act.copy(XT[:, k, :], w[:, :])
                        if kind == "q":
                            last = act.activation(QT[:, k, :], w[:, :], ACT.Identity, bias=BQS[:, k:k + 1], scale=SCALE)
                        if kind == "k":
                            for n in range(4):
                                rows = slice(DH * n, DH * n + DH)
                                last = act.activation(KT[rows, k, n, :], w[rows, :], ACT.Identity, bias=BK[rows, k:k + 1])
                        last.then_inc(sem["act_empty"], 1)
                    n = lambda k: after(i, U, k)
                    for r in range(U + LV + 1):
                        if r < U:
                            w = P * tiles(r % TT)
                            act.wait_ge(sem["negmax"], n(r))
                            act.wait_ge(sem["pturn"], n(r - 4))
                            act.activation(PR[:, r % 4, 0:w], pS[r % 3][:, 0:w], ACT.Exp, bias=NM[:, r % 4:r % 4 + 1],
                                           accum_out=SM[:, r % 4:r % 4 + 1]).then_inc(sem["probs"], 1)
                        if LP <= r < U + LP:
                            w, q = P * tiles((r - LP) % TT), (r - LP) % 2
                            act.wait_ge(sem["pturn"], n(r - LP))
                            act.wait_ge(sem["outT"], n(r - LP - 2))
                            act.copy(PT[:, q, 0:w], pP[q][:, 0:w]).then_inc(sem["pcopy"], 1)
                        if r > LV and (r - LV - 1) % (4 * TT) == 4 * TT - 1:
                            j = (r - LV - 1) // (4 * TT)
                            act.wait_ge(sem["outT"], n(r - LV - 1))
                            act.copy(OT[:, j, :], pO[:, :]).then_inc(sem["outTcopy"], 1)

            @block.vector
            def _(dve):
                dve.memset(POWT[:, :], -0.5).then_inc(sem["zero"], 1)
                dve.memset(KT[:, :, :, :], 0.0).then_inc(sem["zero"], 1)
                dve.wait_ge(sem["const"], SEED + 16 * 12)
                dve.wait_ge(sem["tanh"], SEED + 2)
                dve.wait_ge(sem["zero"], SEED + 2)
                dve.tensor_scalar(BO[:, :], BO[:, :], TG[:, 1:2], None, ALU.mult).then_inc(sem["once"], 1)

                def prepare(b, k):
                    steps = Steps(b, 2)
                    if k == 0:
                        dve.wait_ge(sem["loaded"], b * 16 + (SEED + 16))
                    if k < 4:
                        last = dve.bn_stats(BN[:, k, :], X[:, k, :])
                        if k == 3:
                            last.then_inc(sem["nstep"], 1)
                    if k == 4:
                        dve.wait_ge(sem["nstep"], steps.next())
                        dve.memset(VE[:, 0:1], 0.0)
                        for t in range(TT):
                            last = dve.bn_aggr(MV[:, t, :], BN[:, t, :])
                        last.then_inc(sem["nstep"], 1)
                        dve.wait_ge(sem["nstep"], steps.next())
                        dve.tensor_scalar(VE[:, :], MV[:, :, 1], EPS, None, ALU.add).then_inc(sem["stats"], 1)
                    if k == 8:
                        dve.wait_ge(sem["rstd"], after(b, 1, 0))
                        dve.wait_ge(sem["full"], after(b, len(jobs), NX[-1] - len(jobs)))
                    if k >= 8:
                        t = k - 8
                        last = dve.tensor_scalar(XB[:, t, :], X[:, t, :], MV[:, t, 0:1], RD[:, t:t + 1], ALU.subtract, ALU.mult)
                        if k == 11:
                            last.then_inc(sem["norm"], 1)
                            dve.wait_ge(sem["norm"], after(b, 1, 0))
                            dve.sem_inc(sem["read"], 1)

                for k in (0, 1, 2, 3, 4, 8, 9, 10, 11):
                    prepare(0, k)
                with dve.Fori(0, B) as i:
                    steps = Steps(i, U)
                    for m in NVV:
                        k = jobs[m][1]
                        dve.wait_ge(sem["full"], after(i, len(jobs), m))
                        dve.tensor_tensor(V[:, k, :], pW[m % 2][:, :], BV[:, :], ALU.add).then_inc(sem["dve_empty"], 1)
                    n = lambda k: after(i, U, k)
                    for r in range(U + 1):
                        if r < U:
                            w = P * tiles(r % TT)
                            dve.wait_ge(sem["scores"], n(r))
                            dve.wait_ge(sem["probs"], n(r - 4))
                            dve.tensor_reduce(NM[:, r % 4:r % 4 + 1], pS[r % 3][:, 0:w], axis=AX.X, op=ALU.max, negate=True).then_inc(sem["negmax"], 1)
                        if 20 <= r < 40 and r % 2 == 0 and (r < 30 or r >= 32):
                            prepare(i + 1, {20: 0, 22: 1, 24: 2, 26: 3, 28: 4, 32: 8, 34: 9, 36: 10, 38: 11}[r])
                        if r >= 1:
                            q = (r - 1) % 4
                            w = P * tiles((r - 1) % TT)
                            dve.wait_ge(sem["probs"], n(r - 1))
                            dve.reciprocal(RI[:, q:q + 1], SM[:, q:q + 1]).then_inc(sem["step"], 1)
                            dve.wait_ge(sem["step"], steps.next())
                            dve.tensor_scalar(PR[:, q, 0:w], PR[:, q, 0:w], RI[:, q:q + 1], None, ALU.mult).then_inc(sem["scaled"], 1)
                    steps.close()
                    dve.wait_ge(sem["biased"], after(i, 1, 0))
                    dve.wait_ge(sem["out"], i * 16 + SEED)
                    for m in NO:
                        k = jobs[m][1]
                        dve.wait_ge(sem["full"], after(i, len(jobs), m))
                        dve.scalar_tensor_tensor(out=Y[:, k, :], in0=pW[m % 2][:, :], scalar=TG[:, 1:2], in1=XL[:, k, :],
                                                 op0=ALU.mult, op1=ALU.add).then_inc(sem["dve_empty"], 1)

            @block.tensor
            def _(pe):
                pe.wait_ge(sem["const"], SEED + 16 * 12)
                pe.wait_ge(sem["zero"], SEED + 2)
                with pe.Fori(0, B) as i:
                    def ready(m):
                        for e in ("act", "dve"):
                            pe.wait_ge(emptied[e], banks.emptied(i, m, e))

                    def free(m):
                        before = banks.engine[(m - 2) % len(jobs)]
                        pe.wait_ge(emptied[before], banks.emptied(i, m - 2, before))

                    for m in range(NO[0]):
                        kind, k = jobs[m]
                        if kind == "x" and k == 0:
                            pe.wait_ge(sem["norm"], after(i, 1, 0))
                        if kind == "q" and k == 0:
                            ready(NX[-1])
                        if kind == "k" and k == 0:
                            pe.wait_ge(sem["ctx"], i * 16 + (SEED + 16))
                        free(m)
                        w = pW[m % 2]
                        for c in range(4):
                            if kind == "x":
                                last = pe.transpose(w[:, P * c:P * c + P], XB[:, c, P * k:P * k + P], IDF[:, :])
                            if kind == "q":
                                last = pe.matmul(w[:, :], WQ[:, c, P * k:P * k + P], XT[:, c, :], start=c == 0, stop=c == 3)
                            if kind == "k":
                                last = pe.matmul(w[:, :], WK[:, c, P * k:P * k + P], C[:, c, :], start=c == 0, stop=c == 3)
                            if kind == "v":
                                last = pe.matmul(w[:, :], C[:, c, P * k:P * k + P], WV[:, c, :], start=c == 0, stop=c == 3)
                        last.then_inc(sem["full"], 1)
                    ready(NVV[-1])
                    n = lambda k: after(i, U, k)
                    for r in range(U + LV):
                        if r < U:
                            h, t = r // TT, r % TT
                            w = P * tiles(t)
                            j, v = h // 4, h % 4
                            pe.wait_ge(sem["probs"], n(r - 3 if r >= 3 else -1))
                            pe.matmul(pS[r % 3][:, 0:w], IDB[:, :], MASK[:, 3 * P - w:3 * P], start=True, stop=False)
                            pe.matmul(pS[r % 3][:, 0:w], QT[:, j, P * t:P * t + P], KT[:, j, v, P * (t + 1) - w:P * (t + 1)],
                                      start=False, stop=True).then_inc(sem["scores"], 1)
                        if LP <= r < U + LP:
                            q = (r - LP) % 4
                            pe.wait_ge(sem["scaled"], n(r - LP))
                            pe.wait_ge(sem["pcopy"], n(r - LP - 2))
                            for k in range(tiles((r - LP) % TT)):
                                last = pe.transpose(pP[(r - LP) % 2][:, P * k:P * k + P], PR[:, q, P * k:P * k + P], IDF[:, :])
                            last.then_inc(sem["pturn"], 1)
                        if r >= LV:
                            h, t = (r - LV) // TT, (r - LV) % TT
                            j, v = h // 4, h % 4
                            pe.wait_ge(sem["pcopy"], n(r - LV))
                            if v == 0 and t == 0:
                                pe.wait_ge(sem["outTcopy"], after(i, J, j - 1))
                            nk = tiles(t)
                            for k in range(nk):
                                last = pe.matmul(pO[DH * v:DH * v + DH, P * t:P * t + P], V[:, t + 1 - nk + k, DH * h:DH * h + DH],
                                                 PT[:, (r - LV) % 2, P * k:P * k + P], start=k == 0, stop=k == nk - 1, skip_group_check=True)
                            last.then_inc(sem["outT"], 1)
                    pe.wait_ge(sem["outTcopy"], after(i, J, J - 1))
                    for m in NO:
                        k = jobs[m][1]
                        free(m)
                        for c in range(4):
                            last = pe.matmul(pW[m % 2][:, :], OT[:, c, P * k:P * k + P], WO[:, c, :], start=c == 0, stop=c == 3)
                        last.then_inc(sem["full"], 1)


def phase_ffn(nc, keep, a, x3, out):
    F, RANK = 2048, 16
    FT = F // P
    QMAX = 127.0
    MAGIC = 1.5 * 2.0 ** 23
    with ExitStack() as ctx:
        def sb(name, shape, dt=f32):
            return ctx.enter_context(nc.sbuf_tensor("d_" + name, shape, dt))

        names = ["const", "wfc", "wproj", "loaded", "resid", "tanh", "zero", "read", "stats", "rstd", "norm", "xfull", "xempty", "wstep", "wmax", "wall",
                 "ab", "abdone", "weights", "hfull", "hempty", "ofull", "step", "out", "biased", "done"]
        sem = open_phase(nc, keep, ["d_" + n for n in names])
        sem = {n: sem["d_" + n] for n in names}
        WF, WP, WT = sb("wf", [P, CT, F]), sb("wp", [P, FT, D]), sb("wt", [P, CT * F])
        AF, BF, AP_, BP = sb("af", [RANK, D]), sb("bf", [RANK, F]), sb("ap", [RANK, F]), sb("bp", [RANK, D])
        MXW, ALLM, SCL = sb("mxw", [P, 2]), sb("allm", [P, 2]), sb("scl", [P, 4])
        BFC, BPR = sb("bfc", [P, FT]), sb("bpr", [P, D])
        IDF = sb("idf", [P, P])
        GT, TG = sb("gt", [P, 4]), sb("tg", [P, 4])
        X, XL, XB, XT = (sb(n, [P, TT, D]) for n in ("x", "xl", "xb", "xT"))
        HT, Y = sb("hT", [P, 4, S]), sb("y", [P, TT, D])
        BN, MV, VE, RD, POWT = sb("bn", [P, TT, 6]), sb("mv", [P, TT, 2]), sb("ve", [P, TT]), sb("rd", [P, TT]), sb("pow", [P, TT])
        bank = [ctx.enter_context(nc.psum_tensor(f"d_ps{i}", [P, 512], f32)) for i in range(8)]
        pW, pO = bank[0:4], bank[4:8]
        with nc.Block() as block:
            @block.sync
            def _(sp):
                sp.dma_start(WF[:, :, :], a["wfcT"]).then_inc(sem["wfc"], 16)
                for dst, src in ((AF[:, :], a["afc"]), (BF[:, :], a["bfcT"]), (AP_[:, :], a["aproj"]), (BP[:, :], a["bprojT"]),
                                 (BFC[:, :], a["b_fc"]), (BPR[:, :], a["b_proj"]), (IDF[:, :], a["idf"]), (GT[:, :], a["gates"])):
                    sp.dma_start(dst, src).then_inc(sem["const"], 16)
                sp.dma_start(WP[:, :, :], a["wprojT"]).then_inc(sem["wproj"], 16)
                with sp.Fori(0, B) as i:
                    row = lambda t: t[bass.ds(i, 1), :, :].rearrange("o (t p) d -> p (o t) d", p=P)
                    sp.wait_ge(sem["read"], after(i, 1, -1))
                    sp.dma_start(X[:, :, :], row(x3)).then_inc(sem["loaded"], 16)
                    sp.wait_ge(sem["done"], after(i, 1, -1))
                    sp.dma_start(XL[:, :, :], row(x3)).then_inc(sem["resid"], 16)
                    sp.wait_ge(sem["done"], after(i, 1, 0))
                    sp.dma_start(row(out), Y[:, :, :]).then_inc(sem["out"], 16)
                sp.wait_ge(sem["out"], SEED + 16 * B)

            @block.gpsimd
            def _(pool):
                for n in range(2):
                    pool.wait_ge(sem["wmax"], SEED + n + 1)
                    pool.partition_all_reduce(ALLM[:, n:n + 1], MXW[:, n:n + 1], P, bass.bass_isa.ReduceOp.max).then_inc(sem["wall"], 1)
                pool.wait_ge(sem["zero"], SEED + 2)
                with pool.Fori(0, B) as i:
                    pool.wait_ge(sem["stats"], after(i, 1, 0))
                    pool.tensor_tensor(RD[:, :], VE[:, :], POWT[:, :], ALU.pow).then_inc(sem["rstd"], 1)
                    pool.wait_ge(sem["resid"], i * 16 + (SEED + 16))
                    for t in range(TT):
                        last = pool.tensor_tensor(XL[:, t, :], XL[:, t, :], BPR[:, :], ALU.add)
                    last.then_inc(sem["biased"], 1)

            @block.scalar
            def _(act):
                act.wait_ge(sem["const"], SEED + 16 * 8)
                act.activation(TG[:, :], GT[:, :], ACT.Tanh).then_inc(sem["tanh"], 1)
                with act.Fori(0, B) as i:
                    for c in range(CT):
                        act.wait_ge(sem["xfull"], after(i, CT, c))
                        act.copy(XT[:, c, :], pW[c][:, :]).then_inc(sem["xempty"], 1)
                    for f in range(FT):
                        act.wait_ge(sem["hfull"], after(i, FT, f))
                        act.wait_ge(sem["ofull"], after(i, FT, f - 4))
                        act.activation(HT[:, f % 4, :], pW[f % 4][:, :], ACT.Gelu, bias=BFC[:, f:f + 1]).then_inc(sem["hempty"], 1)

            @block.vector
            def _(dve):
                dve.memset(POWT[:, :], -0.5).then_inc(sem["zero"], 1)
                dve.wait_ge(sem["tanh"], SEED + 1)
                dve.tensor_scalar(BPR[:, :], BPR[:, :], TG[:, 3:4], None, ALU.mult).then_inc(sem["zero"], 1)
                k = 0
                for n, (W, w) in enumerate(((WF, "wfc"), (WP, "wproj"))):
                    flat = W[:, :, :].rearrange("p c f -> p (c f)")
                    dve.wait_ge(sem[w], SEED + 16)
                    dve.tensor_reduce(MXW[:, n:n + 1], flat, axis=AX.X, op=ALU.max, apply_absolute_value=True).then_inc(sem["wmax"], 1)
                for n, W in enumerate((WF, WP)):
                    flat = W[:, :, :].rearrange("p c f -> p (c f)")
                    dve.wait_ge(sem["wall"], SEED + n + 1)
                    dve.tensor_scalar(SCL[:, 2 * n:2 * n + 1], ALLM[:, n:n + 1], 1.0 / QMAX, None, ALU.mult).then_inc(sem["wstep"], 1)
                    dve.wait_ge(sem["wstep"], SEED + k + 1)
                    dve.reciprocal(SCL[:, 2 * n + 1:2 * n + 2], SCL[:, 2 * n:2 * n + 1]).then_inc(sem["wstep"], 1)
                    dve.wait_ge(sem["wstep"], SEED + k + 2)
                    dve.tensor_scalar(WT[:, :], flat, SCL[:, 2 * n + 1:2 * n + 2], MAGIC, ALU.mult, ALU.add).then_inc(sem["wstep"], 1)
                    dve.wait_ge(sem["wstep"], SEED + k + 3)
                    dve.tensor_scalar(WT[:, :], WT[:, :], MAGIC, QMAX, ALU.subtract, ALU.min).then_inc(sem["wstep"], 1)
                    dve.wait_ge(sem["wstep"], SEED + k + 4)
                    dve.tensor_scalar(flat, WT[:, :], -QMAX - 1, SCL[:, 2 * n:2 * n + 1], ALU.max, ALU.mult).then_inc(sem["wstep"], 1)
                    k += 5
                    dve.wait_ge(sem["wstep"], SEED + k)
                for m in range(2 * FT):
                    part = WF[:, m // 4, 512 * (m % 4):512 * (m % 4) + 512] if m < FT else WP[:, m - FT, :]
                    dve.wait_ge(sem["ab"], SEED + m + 1)
                    dve.scalar_tensor_tensor(out=part, in0=pW[m % 4][:, :], scalar=2.0, in1=part, op0=ALU.mult, op1=ALU.add).then_inc(sem["abdone"], 1)
                with dve.Fori(0, B) as i:
                    steps = Steps(i, 2)
                    dve.wait_ge(sem["loaded"], i * 16 + (SEED + 16))
                    for t in range(TT):
                        last = dve.bn_stats(BN[:, t, :], X[:, t, :])
                    last.then_inc(sem["step"], 1)
                    dve.wait_ge(sem["step"], steps.next())
                    dve.memset(VE[:, 0:1], 0.0)
                    for t in range(TT):
                        last = dve.bn_aggr(MV[:, t, :], BN[:, t, :])
                    last.then_inc(sem["step"], 1)
                    dve.wait_ge(sem["step"], steps.next())
                    steps.close()
                    dve.tensor_scalar(VE[:, :], MV[:, :, 1], EPS, None, ALU.add).then_inc(sem["stats"], 1)
                    dve.wait_ge(sem["rstd"], after(i, 1, 0))
                    dve.wait_ge(sem["xfull"], after(i, CT, -1))
                    for t in range(TT):
                        last = dve.tensor_scalar(XB[:, t, :], X[:, t, :], MV[:, t, 0:1], RD[:, t:t + 1], ALU.subtract, ALU.mult)
                    last.then_inc(sem["norm"], 1)
                    dve.wait_ge(sem["norm"], after(i, 1, 0))
                    dve.sem_inc(sem["read"], 1)
                    dve.wait_ge(sem["biased"], after(i, 1, 0))
                    dve.wait_ge(sem["out"], i * 16 + SEED)
                    dve.wait_ge(sem["ofull"], after(i, FT, FT - 1))
                    for t in range(TT):
                        last = dve.scalar_tensor_tensor(out=Y[:, t, :], in0=pO[t][:, :], scalar=TG[:, 3:4], in1=XL[:, t, :], op0=ALU.mult, op1=ALU.add)
                    last.then_inc(sem["done"], 1)

            @block.tensor
            def _(pe):
                pe.wait_ge(sem["const"], SEED + 16 * 8)
                for m in range(2 * FT):
                    if m >= 4:
                        pe.wait_ge(sem["abdone"], SEED + m - 3)
                    if m < FT:
                        c, f = m // 4, m % 4
                        last = pe.matmul(pW[m % 4][:, :], AF[:, P * c:P * c + P], BF[:, 512 * f:512 * f + 512], start=True, stop=True)
                    else:
                        f = m - FT
                        last = pe.matmul(pW[m % 4][:, :], AP_[:, P * f:P * f + P], BP[:, :], start=True, stop=True)
                    last.then_inc(sem["ab"], 1)
                pe.wait_ge(sem["abdone"], SEED + 2 * FT)
                with pe.Fori(0, B) as i:
                    pe.wait_ge(sem["norm"], after(i, 1, 0))
                    for c in range(CT):
                        pe.wait_ge(sem["hempty"], after(i, FT, c - 4))
                        for t in range(TT):
                            last = pe.transpose(pW[c][:, P * t:P * t + P], XB[:, t, P * c:P * c + P], IDF[:, :])
                        last.then_inc(sem["xfull"], 1)
                    pe.wait_ge(sem["xempty"], after(i, CT, CT - 1))
                    for f in range(FT + 2):
                        if f < FT:
                            pe.wait_ge(sem["hempty"], after(i, FT, f - 4))
                            for c in range(CT):
                                last = pe.matmul(pW[f % 4][:, :], WF[:, c, P * f:P * f + P], XT[:, c, :], start=c == 0, stop=c == CT - 1)
                            last.then_inc(sem["hfull"], 1)
                        if f >= 2:
                            g = f - 2
                            pe.wait_ge(sem["hempty"], after(i, FT, g))
                            if g == 0:
                                pe.wait_ge(sem["done"], after(i, 1, -1))
                            for t in range(TT):
                                last = pe.matmul(pO[t][:, :], HT[:, g % 4, P * t:P * t + P], WP[:, g, :], start=g == 0, stop=g == FT - 1)
                            last.then_inc(sem["ofull"], 1)


def program(nc, a, out, x1, x1l, xr, s_route, sel, qsel, qidx, x2, x3):
    with ExitStack() as keep:
        phase_token_heads(nc, keep, a["x_th"], a["v_th"], a["kT_th"], a, a["gates"], x1)
        phase_local(nc, keep, a, x1, x1l, xr, s_route)
        phase_route(nc, keep, a, s_route, sel, qsel, qidx)
        phase_heavy(nc, keep, a, xr, x1l, sel, qsel, qidx, x2)
        phase_window(nc, keep, a, x2, x3)
        phase_ffn(nc, keep, a, x3, out)


BF16_CONSTANTS = ("idb", "mask_th", "neg64", "mask_w")


def bf16_bits(constant):
    return (constant.astype(np.float32).view(np.uint32) >> 16).astype(np.uint16)


def dram_inputs(nc, arrays):
    a = {k: nc.dram_tensor(f"in_{k}", v.shape, mybir.dt.from_np(v.dtype), kind="ExternalInput").ap() for k, v in arrays.items()}
    return {k: v.bitcast(bf16) if k in BF16_CONSTANTS else v for k, v in a.items()}


def layouts(inputs):
    f = {k: np.asarray(v) for k, v in inputs.items()}
    x, c = f["x"], f["ctx_1024"]
    a = {}
    a["x_th"] = x.reshape(B, S // 8, P, 32).transpose(0, 2, 1, 3).reshape(B, P, S * 4)
    a["v_th"] = c.reshape(B, S // 8, P, 32).transpose(0, 2, 1, 3).reshape(B, P, S * 4)
    a["kT_th"] = c.reshape(B, S // 32, 4, P, 32).transpose(0, 2, 4, 1, 3).reshape(B, P, S // 32, P)
    a["gates"] = np.tile(np.concatenate([f["g_xattn"], f["g_ffn"]]), (P, 1))
    p = np.arange(P)
    a["idf"] = np.eye(P, dtype=np.float32)
    a["idb"] = bf16_bits(np.eye(P))
    same = p[:, None] // 16 == p[None, :] // 16
    a["blockmean"] = (same / D).astype(np.float32)
    a["mask_th"] = bf16_bits(np.tile(np.where(same & (p[None, :] <= p[:, None]), 0, NEG), (1, 4)))
    def wT(w):
        return w.T.reshape(w.shape[1] // P, P, w.shape[0]).transpose(1, 0, 2)

    def col(v):
        return v.reshape(-1, P).T

    a["wqkvT"], a["woutlT"] = wT(f["L0_ffn_Wqkv"]), wT(f["L0_ffn_Wout_l"])
    a["rt"] = np.tile(np.stack([f["L0_ffn_rt_q"][0], f["L0_ffn_rt_kv"][0]])[None], (P, 1, 1))
    a["ln_w"], a["ln_b"] = col(f["L0_ffn_ln_w"]), col(f["L0_ffn_ln_b"])
    a["neg64"] = bf16_bits(np.full((P, 64), -1e9))
    k_of = [min(256 * 9.0 / 8.0, float(S)), min(512 * 9.0 / 8.0, float(S))]
    a["router_k"] = np.repeat([[np.log(S) - np.log(k), 1 / k] for k in k_of], B, axis=0).astype(np.float32)
    a["batch_base"] = np.tile(S * np.arange(B, dtype=np.float32)[None], (P, 1))
    wkv = f["L0_ffn_Wkv"].reshape(8, 2, 64, D)
    a["hwqT"], a["hwoT"] = wT(f["L0_ffn_Wq"]), wT(f["L0_ffn_Wout_h"])
    a["hwkT"], a["hwvT"] = wT(wkv[:, 0].reshape(D, D)), wT(wkv[:, 1].reshape(D, D))
    a["gamma"] = col(f["L0_ffn_gamma"])
    nk, nv = f["L0_ffn_null_kv"]
    nkb, nvb = np.zeros((P, 4, 2), np.float32), np.zeros((P, 4, P), np.float32)
    for h in range(8):
        o = 64 * (h % 2)
        nkb[o:o + 64, h // 2, h % 2] = nk[h]
        nvb[h, h // 2, o:o + 64] = nv[h]
    a["null_k"], a["null_v"] = nkb, nvb
    a["null_q"] = np.tile(f["L0_ffn_null_q"][None], (P, 1))
    a["ctxT"] = c.transpose(0, 2, 1).reshape(B, CT, P, S).transpose(0, 2, 1, 3)
    for n in "qkvo":
        a[f"xw{n}T"] = wT(f[f"L1_xattn_w{n}"])
    a["xbq"], a["xbk"] = col(f["L1_xattn_bq"]), col(f["L1_xattn_bk"])
    a["xbv"], a["xbo"] = (np.tile(f[k][None], (P, 1)) for k in ("L1_xattn_bv", "L1_xattn_bo"))
    r, k = p[:, None], p[None, :]
    a["mask_w"] = bf16_bits(np.concatenate([np.where(k >= r, 0, NEG), 0.0 * (k + r), np.where(k <= r, 0, NEG)], 1))
    a["wfcT"], a["wprojT"] = wT(f["L1_ffn_W_fc"]), wT(f["L1_ffn_W_proj"])
    a["afc"], a["aproj"] = f["L1_ffn_A_fc"], f["L1_ffn_A_proj"]
    a["bfcT"], a["bprojT"] = f["L1_ffn_B_fc"].T, f["L1_ffn_B_proj"].T
    a["b_fc"], a["b_proj"] = col(f["L1_ffn_b_fc"]), np.tile(f["L1_ffn_b_proj"][None], (P, 1))
    return {k: np.ascontiguousarray(v) for k, v in a.items()}


def kernel(**inputs):
    import concourse.bacc as _bacc
    from concourse.bass_utils import run_bass_kernel_spmd as _run

    nc = _bacc.Bacc("TRN2", target_bir_lowering=False, num_devices=1)
    arrays = layouts(inputs)
    a = dram_inputs(nc, arrays)
    out = nc.dram_tensor("out_0", (B, S, D), f32, kind="ExternalOutput").ap()
    scratch = {k: nc.dram_tensor(f"s_{k}", shape, mybir.dt.uint32 if k == "qidx" else f32).ap() for k, shape in SCRATCH.items()}
    program(nc, a, out, **scratch)
    r = _run(nc, [{f"in_{k}": v for k, v in arrays.items()}], core_ids=[0])
    return r.results[0]["out_0"]


SCRATCH = {"x1": (B, S, D), "x1l": (B, S, D), "xr": (B, S, D), "s_route": (B, P, 2 * TT), "sel": (P, TT, 3 * B),
           "qsel": (P, 2, B), "qidx": (P, 2, B), "x2": (B, S, D), "x3": (B, S, D)}
```

```python
import concourse.bass as bass
from concourse import mybir
from contextlib import ExitStack
import numpy as np

f32 = mybir.dt.float32
bf16 = mybir.dt.bfloat16
f16 = mybir.dt.float16
ALU = mybir.AluOpType
ACT = mybir.ActivationFunctionType
AX = mybir.AxisListType

B, S, D = 8, 512, 512
P = 128
TT = S // P
CT = D // P
EPS = 1e-5
NEG = -1e30

THREE = ((0, 0), (0, 1), (1, 0))
TOP = 32768.0
XSCALE = 1024.0

SEED = 48


def after(i, per, k):
    return i * per + (SEED + k + 1)


class Steps:

    def __init__(self, i, per):
        self.i, self.per, self.k = i, per, 0

    def next(self):
        self.k += 1
        return after(self.i, self.per, self.k - 1)

    def close(self):
        assert self.k == self.per, (self.k, self.per)


def semaphore(nc, used, name):
    used.append(nc.alloc_semaphore(name=name))
    return used[-1]


def open_phase(nc, used, names):
    sems = {n: semaphore(nc, used, n) for n in names}
    with nc.Block() as block:
        @block.gpsimd
        def _(pool):
            for s in sems.values():
                pool.sem_inc(s, SEED)
    return sems


def close_phase(nc, used):
    nc.clear_and_free_semaphores(used)
    nc.all_engine_barrier()


def placed(room, a, names):
    pairs, o = [], 0
    for name in names:
        _, c, n = a[name].shape
        pairs.append((room[:, o:o + c * n].rearrange("p (c n) -> p c n", c=c), a[name]))
        o += c * n
    return pairs


def load_ahead(sp, ahead, sem):
    for dst, src in ahead:
        sp.dma_start(dst, src).then_inc(sem["ahead"], 16)


def loaded_ahead(sp, ahead, sem):
    if ahead:
        sp.wait_ge(sem["ahead"], SEED + 16 * len(ahead))


def phase_token_heads(nc, used, x_th, v_th, kT_th, consts, gates, x1, ahead):
    H, DH = 16, 32
    G = S // 8
    R = G // 4
    W = G * DH
    SCALE = DH ** -0.5
    with ExitStack() as ctx:
        def sb(name, shape, dt=f32):
            return ctx.enter_context(nc.sbuf_tensor("a_" + name, shape, dt))

        a_stored = semaphore(nc, used, "a_stored")
        names = ["const", "x0", "x1", "kv0", "kv1", "xc", "tanh", "zeroed0", "zeroed1", "exponent",
                 "sums", "mean", "meancopy", "centred", "squared", "sqsums", "var", "vareps", "rstd", "q",
                 "mturn", "mcopy", "scores", "step", "negmax", "probs", "pturn", "pcopy", "outrow",
                 "sumread", "scaled", "product", "added", "xfree", "ahead"]
        sem = open_phase(nc, used, ["a_" + n for n in names])
        sem = {n: sem["a_" + n] for n in names}
        X, V = sb("x", [P, 2, W]), sb("v", [P, 2, W])
        KH = sb("kh", [P, 2, R, 4 * P])
        XC, SQ, Q = sb("xc", [P, W]), sb("sq", [P, W]), sb("qn", [P, 2, W])
        SUMS, MEAN, SQSUMS, VE, RSTD, POWT = (sb(n, [P, G]) for n in ("sums", "mean", "sqsums", "ve", "rstd", "pow"))
        QO = sb("qo", [P, 4, 2 * P])
        PR, PT = sb("pr", [P, 3, 4, P]), sb("pT", [P, 2, 4 * P])
        MX, NM = sb("mx", [P, 4]), sb("nm", [P, 4, 4])
        SM, RS, TO = sb("sm", [P, 2, 16]), sb("rs", [P, 16]), sb("to", [P, 2, 16, DH])
        IDF, IDB, BM, MASK = sb("idf", [P, P]), sb("idb", [P, P], bf16), sb("bm", [P, P]), sb("mask", [P, 4 * P], bf16)
        GT, TG = sb("gt", [P, 4]), sb("tg", [P, 4])
        bank = [ctx.enter_context(nc.psum_tensor(f"a_ps{i}", [P, 512], f32)) for i in range(8)]
        pS, pP, pM, pO, pL = bank[0:3], bank[3:5], bank[5], bank[6], bank[7]
        M = R + 5
        F = R // 4

        def events(i, u):
            return tuple(lambda k, per=per: after(i, 2 * per, u * per + k) for per in (R, M, F))

        def grouped(t):
            return t.rearrange("p (g d) -> p g d", d=DH)

        with nc.Block() as block:
            @block.sync
            def _(sp):
                def load_xc(b):
                    sp.dma_start(XC[:, :], x_th[bass.ds(b, 1), :, :].rearrange("o p w -> (o p) w")).then_inc(sem["xc"], 16)

                load_xc(0)
                sp.dma_start(BM[:, :], consts["blockmean"]).then_inc(sem["const"], 16)
                sp.dma_start(IDF[:, :], consts["idf"]).then_inc(sem["const"], 16)
                sp.dma_start(IDB[:, :], consts["idb"]).then_inc(sem["const"], 16)
                sp.dma_start(MASK[:, :], consts["mask_th"]).then_inc(sem["const"], 16)
                sp.dma_start(GT[:, :], gates).then_inc(sem["const"], 16)
                load_ahead(sp, ahead, sem)
                with sp.Fori(0, B // 2) as i:
                    following = [sp.snap(i * 2 + 1), sp.snap((i * 2 + 2) % B)]
                    for u in range(2):
                        b = i * 2 + u
                        sp.wait_ge(sem[f"zeroed{u}"], SEED + 1)
                        sp.wait_ge(sem["mturn"], events(i, u - 1)[1](-1))
                        sp.dma_start(V[:, u, :], v_th[bass.ds(b, 1), :, :].rearrange("o p w -> (o p) w")).then_inc(sem[f"kv{u}"], 16)
                        for g in range(4):
                            sp.dma_start(KH[32 * g:32 * g + 32, u, :, P * g:P * g + P],
                                         kT_th[bass.ds(b, 1), 32 * g:32 * g + 32, :, :].rearrange("o p r n -> (o p) r n")).then_inc(sem[f"kv{u}"], 16)
                        sp.wait_ge(sem["xfree"], after(i, 2, u - 2))
                        sp.dma_start(X[:, u, :], x_th[bass.ds(b, 1), :, :].rearrange("o p w -> (o p) w")).then_inc(sem[f"x{u}"], 16)
                        sp.wait_ge(sem["q"], after(i, 2, u))
                        load_xc(following[u])
                loaded_ahead(sp, ahead, sem)

            @block.gpsimd
            def _(pool):
                def centre(i, k):
                    pool.wait_ge(sem["meancopy"], after(i, 2, k))
                    pool.tensor_tensor(grouped(XC[:, :]), grouped(XC[:, :]), MEAN[:, :].unsqueeze(2).broadcast_to([P, G, DH]), ALU.subtract).then_inc(sem["centred"], 1)

                def normalize(i, k):
                    pool.wait_ge(sem["vareps"], after(i, 2, k))
                    pool.tensor_tensor(RSTD[:, :], VE[:, :], POWT[:, :], ALU.pow).then_inc(sem["rstd"], 1)
                    pool.wait_ge(sem["rstd"], after(i, 2, k))
                    pool.wait_ge(sem["mturn"], after(i, 2 * M, (k - 1) * M - 1))
                    pool.tensor_tensor(grouped(Q[:, k % 2, :]), grouped(XC[:, :]), RSTD[:, :].unsqueeze(2).broadcast_to([P, G, DH]), ALU.mult).then_inc(sem["q"], 1)

                pool.memset(POWT[:, :], -0.5).then_inc(sem["exponent"], 1)
                centre(0, 0)
                pool.wait_ge(sem["exponent"], SEED + 1)
                normalize(0, 0)
                pool.memset(KH[:, 1, :, :], 0.0).then_inc(sem["zeroed1"], 1)
                with pool.Fori(0, B // 2) as i:
                    for u in range(2):
                        b = i * 2 + u
                        _, _, part = events(i, u)

                        def add(j):
                            pool.wait_ge(sem["product"], part(j))
                            xs = grouped(X[:, u, :])[:, 16 * j:16 * j + 16, :]
                            pool.tensor_tensor(xs, xs, TO[:, j % 2, :, :], ALU.add).then_inc(sem["added"], 1)

                        centre(i, u + 1)
                        pool.wait_ge(sem[f"x{u}"], i * 16 + (SEED + 16))
                        add(0)
                        normalize(i, u + 1)
                        for j in range(1, F):
                            add(j)
                        pool.wait_ge(sem["added"], part(F - 1))
                        pool.dma_start(x1[bass.ds(b, 1), :, :].rearrange("o (g t) (h d) -> (o t h) g d", t=8, d=DH), grouped(X[:, u, :])).then_inc(a_stored, 16)
                        pool.wait_ge(a_stored, b * 16 + 16)
                        pool.sem_inc(sem["xfree"], 1)

            @block.scalar
            def _(act):
                def square(i, k):
                    act.wait_ge(sem["centred"], after(i, 2, k))
                    act.wait_ge(sem["sqsums"], after(i, 2, k - 1))
                    act.activation(SQ[:, :], XC[:, :], ACT.Square).then_inc(sem["squared"], 1)

                square(0, 0)
                act.wait_ge(sem["const"], SEED + 80)
                act.activation(TG[:, :], GT[:, :], ACT.Tanh).then_inc(sem["tanh"], 1)
                with act.Fori(0, B // 2) as i:
                    for u in range(2):
                        n, turn, part = events(i, u)
                        for x in range(M + 1):
                            r = x - 2
                            if 0 <= r < R:
                                act.wait_ge(sem["negmax"], n(r))
                                act.wait_ge(sem["pturn"], n(r - 3))
                                if r % 4 == 0:
                                    act.wait_ge(sem["sumread"], part(r // 4 - 2))
                                for g in range(4):
                                    last = act.activation(PR[:, r % 3, g, :], pS[r % 3][:, P * g:P * g + P], ACT.Exp, bias=NM[:, r % 4, g:g + 1], scale=SCALE,
                                                          accum_out=SM[:, r // 4 % 2, 4 * (r % 4) + g:4 * (r % 4) + g + 1])
                                last.then_inc(sem["probs"], 1)
                            if x < M:
                                act.wait_ge(sem["mturn"], turn(x))
                                act.wait_ge(sem["scores"], n(min(x - 4, R - 1) if x >= 4 else -1))
                                if x < 4 or x >= 9:
                                    act.wait_ge(sem["outrow"], n(x - 9 if x >= 9 else -1))
                                lo, hi = (0 if x < R else P), (2 * P if x >= 5 else P)
                                act.copy(QO[:, x % 4, lo:hi], pM[:, lo:hi]).then_inc(sem["mcopy"], 1)
                            if x == 7:
                                square(i, u + 1)

            @block.vector
            def _(dve):
                def sums(i, k):
                    dve.wait_ge(sem["xc"], i * 32 + (SEED + 16 * k + 16))
                    dve.wait_ge(sem["mean"], after(i, 2, k - 1))
                    dve.reduce_sum(SUMS[:, :], grouped(XC[:, :]), axis=AX.X).then_inc(sem["sums"], 1)

                def mean(i, k):
                    dve.wait_ge(sem["mean"], after(i, 2, k))
                    dve.wait_ge(sem["centred"], after(i, 2, k - 1))
                    dve.tensor_copy(MEAN[:, :], pL[:, 0:G]).then_inc(sem["meancopy"], 1)

                def square_sums(i, k):
                    dve.wait_ge(sem["squared"], after(i, 2, k))
                    dve.wait_ge(sem["var"], after(i, 2, k - 1))
                    dve.reduce_sum(SQSUMS[:, :], grouped(SQ[:, :]), axis=AX.X).then_inc(sem["sqsums"], 1)

                def var(i, k):
                    dve.wait_ge(sem["var"], after(i, 2, k))
                    dve.wait_ge(sem["rstd"], after(i, 2, k - 1))
                    dve.tensor_scalar(VE[:, :], pL[:, G:2 * G], EPS, None, ALU.add).then_inc(sem["vareps"], 1)

                dve.memset(KH[:, 0, :, :], 0.0).then_inc(sem["zeroed0"], 1)
                sums(0, 0)
                mean(0, 0)
                square_sums(0, 0)
                var(0, 0)
                dve.wait_ge(sem["tanh"], SEED + 1)
                with dve.Fori(0, B // 2) as i:
                    for u in range(2):
                        steps = Steps(i * 2 + u, R)
                        n, turn, part = events(i, u)
                        for x in range(M + 2):
                            r = x - 2
                            if 0 <= r < R:
                                dve.wait_ge(sem["scores"], n(r))
                                dve.wait_ge(sem["negmax"], n(r - 1))
                                dve.reduce_max(MX[:, :], pS[r % 3][:, :].rearrange("p (g n) -> p g n", n=P), axis=AX.X).then_inc(sem["step"], 1)
                                dve.wait_ge(sem["step"], steps.next())
                                dve.wait_ge(sem["probs"], n(r - 4))
                                dve.tensor_scalar(NM[:, r % 4, :], MX[:, :], -SCALE, None, ALU.mult).then_inc(sem["negmax"], 1)
                            if x >= 10 and x % 4 == 2:
                                j = (x - 10) // 4
                                dve.wait_ge(sem["probs"], n(4 * j + 3))
                                dve.wait_ge(sem["product"], part(j - 1))
                                dve.reciprocal(RS[:, :], SM[:, j % 2, :]).then_inc(sem["sumread"], 1)
                                dve.wait_ge(sem["sumread"], part(j))
                                dve.tensor_scalar(RS[:, :], RS[:, :], TG[:, 0:1], None, ALU.mult).then_inc(sem["scaled"], 1)
                                dve.wait_ge(sem["scaled"], part(j))
                                dve.wait_ge(sem["added"], part(j - 2))
                                dve.wait_ge(sem["outrow"], n(4 * j + 3))
                                dve.tensor_tensor(TO[:, j % 2, :, :], grouped(pO[:, :]), RS[:, :].unsqueeze(2).broadcast_to([P, 16, DH]), ALU.mult).then_inc(sem["product"], 1)
                            if 0 <= x - 4 < R:
                                r = x - 4
                                dve.wait_ge(sem["pturn"], n(r))
                                dve.wait_ge(sem["mturn"], turn(r + 3 if r >= 2 else -1))
                                dve.tensor_copy(PT[:, r % 2, :], pP[r % 2][:, :]).then_inc(sem["pcopy"], 1)
                            if x == 2:
                                sums(i, u + 1)
                            if x == 4:
                                mean(i, u + 1)
                            if x == 9:
                                square_sums(i, u + 1)
                            if x == 11:
                                var(i, u + 1)
                        steps.close()

            @block.tensor
            def _(pe):
                def mean(i, k):
                    pe.wait_ge(sem["sums"], after(i, 2, k))
                    pe.wait_ge(sem["vareps"], after(i, 2, k - 1))
                    pe.matmul(pL[:, 0:G], BM[:, :], SUMS[:, :], start=True, stop=True).then_inc(sem["mean"], 1)

                def var(i, k):
                    pe.wait_ge(sem["sqsums"], after(i, 2, k))
                    pe.wait_ge(sem["meancopy"], after(i, 2, k))
                    pe.matmul(pL[:, G:2 * G], BM[:, :], SQSUMS[:, :], start=True, stop=True).then_inc(sem["var"], 1)

                pe.wait_ge(sem["const"], SEED + 80)
                mean(0, 0)
                var(0, 0)
                with pe.Fori(0, B // 2) as i:
                    for u in range(2):
                        n, turn, part = events(i, u)
                        pe.wait_ge(sem["q"], after(i, 2, u))
                        for x in range(M + 1):
                            r = x - 2
                            if r == 0:
                                pe.wait_ge(sem[f"kv{u}"], i * 80 + (SEED + 80))
                            if 0 <= r < R:
                                pe.wait_ge(sem["mcopy"], turn(r))
                                pe.wait_ge(sem["probs"], n(r - 3))
                                pe.matmul(pS[r % 3][:, :], IDB[:, :], MASK[:, :], start=True, stop=False)
                                pe.matmul(pS[r % 3][:, :], QO[:, r % 4, 0:P], KH[:, u, r, :], start=False, stop=True).then_inc(sem["scores"], 1)
                            r = x - 4
                            if 0 <= r < R:
                                pe.wait_ge(sem["probs"], n(r))
                                pe.wait_ge(sem["pcopy"], n(r - 2))
                                for g in range(4):
                                    last = pe.transpose(pP[r % 2][:, P * g:P * g + P], PR[:, r % 3, g, :], IDF[:, :])
                                last.then_inc(sem["pturn"], 1)
                            if x < M:
                                pe.wait_ge(sem["mcopy"], turn(x - 1))
                                r = x - 5
                                if r >= 0:
                                    pe.wait_ge(sem["pcopy"], n(r))
                                    for g in range(4):
                                        last = pe.matmul(pM[32 * g:32 * g + 32, P:2 * P], V[:, u, 32 * (4 * r + g):32 * (4 * r + g) + 32],
                                                         PT[:, r % 2, P * g:P * g + P], start=True, stop=True)
                                if x < R:
                                    last = pe.transpose(pM[:, 0:P], Q[:, u, P * x:P * x + P], IDF[:, :])
                                last.then_inc(sem["mturn"], 1)
                            r = x - 6
                            if r >= 0:
                                pe.wait_ge(sem["mcopy"], turn(r + 5))
                                if r % 4 == 0:
                                    pe.wait_ge(sem["product"], part(r // 4 - 1))
                                c = r % 4
                                pe.transpose(pO[:, P * c:P * c + P], QO[:, (r + 5) % 4, P:2 * P], IDF[:, :]).then_inc(sem["outrow"], 1)
                            if x == 3:
                                mean(i, u + 1)
                            if x == 10:
                                var(i, u + 1)


class Banks:

    def __init__(self, jobs, engine_of):
        self.jobs = jobs
        self.engine = [engine_of(m, job) for m, job in enumerate(jobs)]
        self.per = {e: self.engine.count(e) for e in ("act", "dve")}

    def of(self, kind):
        return [m for m, job in enumerate(self.jobs) if job[0] == kind]

    def emptied(self, i, m, e):
        back = 0
        while m < 0:
            m, back = m + len(self.jobs), back + 1
        return after(i, self.per[e], self.engine[:m + 1].count(e) - 1 - back * self.per[e])


def phase_local(nc, used, a, x1, x1l, xr, s_route, own, ahead):
    H, DH, WIN = 8, 64, 64
    SCALE = DH ** -0.5
    J = 4
    U = J * TT
    LP, LV = 3, 4
    jobs = [("x", c) for c in range(4)] + [("q", j) for j in range(4)] + [("k", j) for j in range(4)] + \
           [("v", t) for t in range(4)] + [("o", t) for t in range(4)]
    banks = Banks(jobs, lambda m, job: "dve" if job[0] == "o" else "act" if job[0] == "x" else ("act", "dve")[m % 2])
    NX, NQ, NK, NVV, NO = (banks.of(k) for k in "xqkvo")
    with ExitStack() as ctx:
        def sb(name, shape, dt=f32):
            return ctx.enter_context(nc.sbuf_tensor("b_" + name, shape, dt))

        names = ["const", "loaded", "resid", "read", "nstep", "stats", "rstd", "xr", "s", "route_out", "xr_out", "norm",
                 "full", "act_empty", "dve_empty", "scores", "negmax", "probs", "scaled", "pturn", "pmain", "pextra",
                 "outT", "outTcopy", "tanh", "step", "out", "rows", "zero", "ahead", "largest", "all", "bound", "whigh", "wlow", "xhigh", "xsplit"]
        sem = open_phase(nc, used, ["b_" + n for n in names])
        sem = {n: sem["b_" + n] for n in names}
        emptied = {"act": sem["act_empty"], "dve": sem["dve_empty"]}
        WQKV, WO = own
        RT = sb("rt", [P, 2, D])
        LNW, LNB = sb("lnw", [P, CT]), sb("lnb", [P, CT])
        IDF, IDB, NEGB = sb("idf", [P, P]), sb("idb", [P, P], bf16), sb("negb", [P, WIN], bf16)
        GT, TG = sb("gt", [P, 4]), sb("tg", [P, 4])
        X, XL, XA, XB, XR = (sb(n, [P, TT, D]) for n in ("x", "xl", "xa", "xb", "xr"))
        XBT = sb("xbT", [P, CT, S])
        XS, WS = sb("xs", [P, 2, CT, S], f16), sb("ws", [P, 2, CT, 3 * D], f16)
        MXW, ALLM = sb("mxw", [P, 3]), sb("allm", [P, 3])
        BOUND, SC, UN = sb("bound", [P, 2]), sb("sc", [P, 2]), sb("un", [P, 2])
        QT, KT, V = sb("qT", [P, J, S]), sb("kT", [P, J, 2, S]), sb("v", [P, TT, D])
        VL = sb("vlo", [WIN, TT, D])
        BN, MV, RD, POWT = sb("bn", [P, TT, 6]), sb("mv", [P, 3 * TT, 2]), sb("rd", [P, 3 * TT]), sb("pow", [P, 2 * TT])
        VE = sb("ve", [P, 3 * TT])
        SS, SCR = sb("ss", [P, 2, TT]), sb("scr", [P, D])
        PR, NM, SM, RI = sb("pr", [P, 4, 2, 192]), sb("nm", [P, 4, 2]), sb("sm", [P, 4, 2]), sb("ri", [P, 4, 2])
        PTM, PTE = sb("pTm", [P, 2, 2, P]), sb("pTe", [WIN, 2, 2, P])
        OT = XBT
        bank = [ctx.enter_context(nc.psum_tensor(f"b_ps{i}", [P, 512], f32)) for i in range(8)]
        pW, pS, pP = bank[0:2], bank[2:5], bank[5:7]
        pO = bank[7], pW[1]

        with nc.Block() as block:
            @block.sync
            def _(sp):
                sp.dma_start(X[:, :, :], x1[0, :, :].rearrange("(t p) d -> p t d", p=P)).then_inc(sem["loaded"], 16)
                for dst, src in ((RT[:, :, :], a["rt"]), (LNW[:, :], a["ln_w"]),
                                 (LNB[:, :], a["ln_b"]), (IDF[:, :], a["idf"]), (IDB[:, :], a["idb"]), (NEGB[:, :], a["neg64"]),
                                 (GT[:, :], a["gates"])):
                    sp.dma_start(dst, src).then_inc(sem["const"], 16)
                load_ahead(sp, ahead, sem)
                with sp.Fori(0, B) as i:
                    row = lambda t, b=i: t[bass.ds(b, 1), :, :].rearrange("o (t p) d -> p (o t) d", p=P)
                    following = sp.snap((i + 1) % B)
                    sp.wait_ge(sem["read"], after(i, 1, 0))
                    sp.dma_start(X[:, :, :], row(x1, following)).then_inc(sem["loaded"], 16)
                    sp.wait_ge(sem["out"], i * 16 + SEED)
                    sp.dma_start(XL[:, :, :], row(x1)).then_inc(sem["resid"], 16)
                    sp.wait_ge(sem["xr"], after(i, 1, 0))
                    sp.dma_start(row(xr), XR[:, :, :]).then_inc(sem["xr_out"], 16)
                    sp.wait_ge(sem["s"], after(i, 1, 0))
                    sp.dma_start(s_route[bass.ds(i, 1), :, :].rearrange("o p n -> (o p) n"), SS[:, :, :].rearrange("p r t -> p (r t)")).then_inc(sem["route_out"], 16)
                    sp.wait_ge(sem["dve_empty"], banks.emptied(i, NO[-1], "dve"))
                    sp.dma_start(row(x1l), XL[:, :, :]).then_inc(sem["out"], 16)
                loaded_ahead(sp, ahead, sem)
                sp.wait_ge(sem["xr_out"], SEED + 16 * B)
                sp.wait_ge(sem["route_out"], SEED + 16 * B)
                sp.wait_ge(sem["out"], SEED + 16 * B)

            @block.gpsimd
            def _(pool):
                pool.wait_ge(sem["largest"], SEED + 1)
                pool.partition_all_reduce(ALLM[:, :], MXW[:, :], P, bass.bass_isa.ReduceOp.max).then_inc(sem["all"], 1)
                with pool.Fori(0, B + 1) as i:
                    pool.wait_ge(sem["stats"], after(i, 2, 0))
                    pool.tensor_tensor(RD[:, 0:TT], VE[:, 0:TT], POWT[:, 0:TT], ALU.pow).then_inc(sem["rstd"], 1)
                    pool.wait_ge(sem["stats"], after(i, 2, 1))
                    pool.tensor_tensor(RD[:, TT:3 * TT], VE[:, TT:3 * TT], POWT[:, :], ALU.pow).then_inc(sem["rstd"], 1)

            @block.scalar
            def _(act):
                act.wait_ge(sem["const"], SEED + 16 * 7)
                act.activation(TG[:, :], GT[:, :], ACT.Tanh).then_inc(sem["tanh"], 1)
                act.wait_ge(sem["bound"], SEED + 6)
                for c in range(CT):
                    act.mul(WS[:, 0, c, :], WQKV[:, c, :], SC[:, 1:2]).then_inc(sem["whigh"], 1)
                with act.Fori(0, B) as i:
                    for m, (kind, k) in enumerate(jobs):
                        if banks.engine[m] != "act":
                            continue
                        w = pW[m % 2]
                        act.wait_ge(sem["full"], after(i, len(jobs), m))
                        if kind == "x":
                            act.activation(XBT[:, k, :], w[:, :], ACT.Identity, bias=LNB[:, k:k + 1], scale=LNW[:, k:k + 1]).then_inc(sem["act_empty"], 1)
                        if kind == "q":
                            act.mul(QT[:, k, :], w[:, :], UN[:, 1:2]).then_inc(sem["act_empty"], 1)
                        if kind == "k":
                            act.mul(KT[0:64, k, 0, :], w[0:64, :], UN[0:64, 0:1])
                            act.mul(KT[64:128, k, 1, :], w[64:128, :], UN[64:128, 0:1]).then_inc(sem["act_empty"], 1)
                        if kind == "v":
                            act.mul(V[:, k, :], w[:, :], UN[:, 0:1])
                            act.mul(VL[:, k, :], w[64:128, :], UN[64:128, 0:1]).then_inc(sem["act_empty"], 1)
                    n = lambda k: after(i, U, k)
                    for r in range(U + LV):
                        if LP <= r < U + LP:
                            q = (r - LP) % 2
                            act.wait_ge(sem["pturn"], n(r - LP))
                            act.wait_ge(sem["outT"], n(r - LP - 2))
                            act.copy(PTM[:, q, :, :], pP[0][:, 0:256].rearrange("p (v n) -> p v n", v=2)).then_inc(sem["pmain"], 1)
                        if r < U:
                            act.wait_ge(sem["negmax"], n(r))
                            act.wait_ge(sem["pturn"], n(r - 4))
                            for v in range(2):
                                last = act.activation(PR[:, r % 4, v, :], pS[r % 3][:, 256 * v:256 * v + 192], ACT.Exp,
                                                      bias=NM[:, r % 4, v:v + 1], accum_out=SM[:, r % 4, v:v + 1])
                            last.then_inc(sem["probs"], 1)
                        if r >= LV and (r - LV) % TT == TT - 1:
                            j = (r - LV) // TT
                            act.wait_ge(sem["outT"], n(r - LV))
                            act.copy(OT[:, j, :], pO[j % 2][:, :]).then_inc(sem["outTcopy"], 1)

            @block.vector
            def _(dve):
                dve.memset(POWT[:, :], -0.5).then_inc(sem["zero"], 1)
                dve.memset(KT[:, :, :, :], 0.0).then_inc(sem["zero"], 1)
                dve.wait_ge(sem["zero"], SEED + 2)
                def moments(b, src, at, t0):
                    for t in (t0, t0 + 1):
                        last = dve.bn_stats(BN[:, t, :], src[:, t, :])
                    if t0:
                        last.then_inc(sem["nstep"], 1)

                def variance(b, at, e):
                    steps = Steps(b, 6)
                    steps.k = 2 * e
                    dve.wait_ge(sem["nstep"], steps.next())
                    dve.memset(VE[:, 0:1], 0.0)
                    for t in range(TT):
                        last = dve.bn_aggr(MV[:, at + t, :], BN[:, t, :])
                    last.then_inc(sem["nstep"], 1)
                    dve.wait_ge(sem["nstep"], steps.next())
                    if e:
                        dve.tensor_tensor(MV[:, 2 * TT:3 * TT, 0], MV[:, at:at + TT, 0], MV[:, at:at + TT, 0], ALU.mult).then_inc(sem["nstep"], 1)
                        dve.wait_ge(sem["nstep"], steps.next())
                        dve.tensor_tensor(MV[:, 2 * TT:3 * TT, 1], MV[:, 2 * TT:3 * TT, 0], MV[:, at:at + TT, 1], ALU.add).then_inc(sem["nstep"], 1)
                        dve.wait_ge(sem["nstep"], steps.next())
                        dve.tensor_scalar(VE[:, 2 * TT:3 * TT], MV[:, 2 * TT:3 * TT, 1], 1e-24 / D, None, ALU.max)
                    dve.tensor_scalar(VE[:, at:at + TT], MV[:, at:at + TT, 1], EPS, None, ALU.add).then_inc(sem["stats"], 1)

                def normed(b, src, dst, at, e, t0):
                    if t0 == 0:
                        dve.wait_ge(sem["rstd"], after(b, 2, e))
                    for t in (t0, t0 + 1):
                        last = dve.tensor_scalar(dst[:, t, :], src[:, t, :], MV[:, at + t, 0:1], RD[:, at + t:at + t + 1], ALU.subtract, ALU.mult)
                    return last

                def rms_rows(b, t):
                    if t == 0:
                        dve.wait_ge(sem["xr_out"], b * 16 + SEED)
                    last = dve.tensor_scalar(XR[:, t, :], XA[:, t, :], RD[:, 2 * TT + t:2 * TT + t + 1], None, ALU.mult)
                    if t == TT - 1:
                        last.then_inc(sem["xr"], 1)

                def routing(b, t):
                    if t == 0:
                        dve.wait_ge(sem["route_out"], b * 16 + SEED)
                        dve.wait_ge(sem["s"], after(b, 1, -1))
                    for r in range(2):
                        last = dve.tensor_tensor_reduce(out=SCR[:, :].unsqueeze(1), in0=XA[:, t, :].unsqueeze(1), in1=RT[:, r, :].unsqueeze(1), scale=1.0, scalar=0.0,
                                                        op0=ALU.mult, op1=ALU.add, accum_out=SS[:, r, t:t + 1])
                        if not (t == TT - 1 and r == 1):
                            last.then_inc(sem["rows"], 1)
                            dve.wait_ge(sem["rows"], after(b, 7, t * 2 + r))
                    if t == TT - 1:
                        last.then_inc(sem["s"], 1)

                def prepare(b, k):
                    if k == 0:
                        dve.wait_ge(sem["loaded"], b * 16 + (SEED + 16))
                    if k in (0, 1):
                        moments(b, X, 0, 2 * k)
                    if k == 2:
                        variance(b, 0, 0)
                    if k == 3:
                        normed(b, X, XA, 0, 0, 0)
                    if k == 4:
                        normed(b, X, XA, 0, 0, 2).then_inc(sem["read"], 1)
                        dve.wait_ge(sem["read"], after(b, 1, 0))
                    if k in (5, 6):
                        moments(b, XA, TT, 2 * (k - 5))
                    if k == 7:
                        variance(b, TT, 1)
                    if k == 9:
                        dve.wait_ge(sem["full"], after(b, len(jobs), NX[-1] - len(jobs)))
                        normed(b, XA, XB, TT, 1, 0)
                    if k == 10:
                        normed(b, XA, XB, TT, 1, 2).then_inc(sem["norm"], 1)
                    if k >= 12:
                        rms_rows(b, k - 12)
                    if k >= 12:
                        routing(b, k - 12)

                dve.tensor_reduce(MXW[:, 2:3], WQKV[:, :, :].rearrange("p c n -> p (c n)"), axis=AX.X, op=ALU.max, apply_absolute_value=True)
                dve.wait_ge(sem["const"], SEED + 16 * 7)
                dve.tensor_reduce(MXW[:, 0:1], LNW[:, :], axis=AX.X, op=ALU.max, apply_absolute_value=True)
                dve.tensor_reduce(MXW[:, 1:2], LNB[:, :], axis=AX.X, op=ALU.max, apply_absolute_value=True).then_inc(sem["largest"], 1)
                for k in range(3):
                    prepare(0, k)
                dve.wait_ge(sem["all"], SEED + 1)
                dve.tensor_scalar(BOUND[:, 0:1], ALLM[:, 0:1], float(np.sqrt(D)), ALLM[:, 1:2], ALU.mult, ALU.add)
                dve.tensor_copy(BOUND[:, 1:2], ALLM[:, 2:3]).then_inc(sem["bound"], 1)
                dve.wait_ge(sem["bound"], SEED + 1)
                dve.tensor_scalar(BOUND[:, :], BOUND[:, :], 1.0 / TOP, 1e-30, ALU.mult, ALU.max).then_inc(sem["bound"], 1)
                dve.wait_ge(sem["bound"], SEED + 2)
                dve.reciprocal(SC[:, :], BOUND[:, :])
                dve.tensor_scalar(UN[:, 0:1], BOUND[:, 0:1], BOUND[:, 1:2], None, ALU.mult).then_inc(sem["bound"], 1)
                dve.wait_ge(sem["bound"], SEED + 3)
                dve.tensor_scalar(UN[:, 1:2], UN[:, 0:1], SCALE, None, ALU.mult).then_inc(sem["bound"], 1)
                dve.tensor_scalar(LNW[:, :], LNW[:, :], SC[:, 0:1], None, ALU.mult).then_inc(sem["bound"], 1)
                dve.tensor_scalar(LNB[:, :], LNB[:, :], SC[:, 0:1], None, ALU.mult).then_inc(sem["bound"], 1)
                dve.wait_ge(sem["bound"], SEED + 6)
                for k in range(3, 12):
                    prepare(0, k)
                for c in range(CT):
                    dve.wait_ge(sem["whigh"], SEED + c + 1)
                    dve.scalar_tensor_tensor(out=WS[:, 1, c, :], in0=WQKV[:, c, :], scalar=SC[:, 1:2], in1=WS[:, 0, c, :], op0=ALU.mult, op1=ALU.subtract).then_inc(sem["wlow"], 1)
                for k in range(12, 16):
                    prepare(0, k)
                with dve.Fori(0, B) as i:
                    steps = Steps(i, U)

                    def empty(m):
                        kind, k = jobs[m]
                        w = pW[m % 2]
                        dve.wait_ge(sem["full"], after(i, len(jobs), m))
                        if kind == "q":
                            dve.tensor_scalar(QT[:, k, :], w[:, :], UN[:, 1:2], None, ALU.mult).then_inc(sem["dve_empty"], 1)
                        if kind == "k":
                            dve.tensor_scalar(KT[0:64, k, 0, :], w[0:64, :], UN[0:64, 0:1], None, ALU.mult)
                            dve.tensor_scalar(KT[64:128, k, 1, :], w[64:128, :], UN[64:128, 0:1], None, ALU.mult).then_inc(sem["dve_empty"], 1)
                        if kind == "v":
                            dve.tensor_scalar(V[:, k, :], w[:, :], UN[:, 0:1], None, ALU.mult)
                            dve.tensor_scalar(VL[:, k, :], w[64:128, :], UN[64:128, 0:1], None, ALU.mult).then_inc(sem["dve_empty"], 1)
                        if kind == "o":
                            dve.scalar_tensor_tensor(out=XL[:, k, :], in0=w[:, :], scalar=TG[:, 2:3], in1=XL[:, k, :],
                                                     op0=ALU.mult, op1=ALU.add).then_inc(sem["dve_empty"], 1)

                    for m in NX:
                        k = jobs[m][1]
                        dve.wait_ge(sem["act_empty"], banks.emptied(i, m, "act"))
                        dve.tensor_copy(XS[:, 0, k, :], XBT[:, k, :]).then_inc(sem["xhigh"], 1)
                        dve.wait_ge(sem["xhigh"], after(i, CT, k))
                        dve.tensor_tensor(XS[:, 1, k, :], XBT[:, k, :], XS[:, 0, k, :], ALU.subtract).then_inc(sem["xsplit"], 1)
                    for m in range(NO[0]):
                        if banks.engine[m] == "dve":
                            empty(m)
                    n = lambda k: after(i, U, k)
                    for r in range(U + LP):
                        if r < U:
                            dve.wait_ge(sem["scores"], n(r))
                            dve.wait_ge(sem["probs"], n(r - 4))
                            dve.tensor_reduce(NM[:, r % 4, :], pS[r % 3][:, :].rearrange("p (v n) -> p v n", v=2)[:, :, 0:192],
                                              axis=AX.X, op=ALU.max, negate=True).then_inc(sem["negmax"], 1)
                        if 1 <= r <= U:
                            q = (r - 1) % 4
                            dve.wait_ge(sem["probs"], n(r - 1))
                            dve.reciprocal(RI[:, q, :], SM[:, q, :]).then_inc(sem["step"], 1)
                            dve.wait_ge(sem["step"], steps.next())
                            for v in range(2):
                                last = dve.tensor_scalar(PR[:, q, v, :], PR[:, q, v, :], RI[:, q, v:v + 1], None, ALU.mult)
                            last.then_inc(sem["scaled"], 1)
                        if r < U:
                            prepare(i + 1, r)
                        if r >= LP:
                            dve.wait_ge(sem["pturn"], n(r - LP))
                            dve.wait_ge(sem["outT"], n(r - LP - 2))
                            dve.tensor_copy(PTE[:, (r - LP) % 2, :, :], pP[1][0:64, 0:256].rearrange("p (v n) -> p v n", v=2)).then_inc(sem["pextra"], 1)
                    steps.close()
                    dve.wait_ge(sem["tanh"], SEED + 1)
                    dve.wait_ge(sem["resid"], i * 16 + (SEED + 16))
                    dve.wait_ge(sem["out"], i * 16 + SEED)
                    for m in NO:
                        empty(m)

            @block.tensor
            def _(pe):
                pe.wait_ge(sem["const"], SEED + 16 * 7)
                pe.wait_ge(sem["zero"], SEED + 2)
                pe.wait_ge(sem["wlow"], SEED + CT)
                with pe.Fori(0, B) as i:
                    def ready(m):
                        for e in ("act", "dve"):
                            pe.wait_ge(emptied[e], banks.emptied(i, m, e))

                    def free(m):
                        before = banks.engine[(m - 2) % len(jobs)]
                        pe.wait_ge(emptied[before], banks.emptied(i, m - 2, before))

                    for m, (kind, k) in enumerate(jobs):
                        if kind == "o":
                            continue
                        if kind == "x" and k == 0:
                            pe.wait_ge(sem["norm"], after(i, 1, 0))
                        free(m)
                        w = pW[m % 2]
                        for c in range(4):
                            if kind == "x":
                                last = pe.transpose(w[:, P * c:P * c + P], XB[:, c, P * k:P * k + P], IDF[:, :])
                            if kind == "q" and k == 0:
                                pe.wait_ge(sem["xsplit"], after(i, CT, c))
                            for n, (one, two) in enumerate(THREE):
                                first, final = c + n == 0, c + n == CT + 1
                                if kind in "qk":
                                    o = (kind == "k") * D + P * k
                                    last = pe.matmul(w[:, :], WS[:, one, c, o:o + P], XS[:, two, c, :], start=first, stop=final)
                                if kind == "v":
                                    last = pe.matmul(w[:, :], XS[:, one, c, P * k:P * k + P], WS[:, two, c, 2 * D:3 * D], start=first, stop=final)
                        last.then_inc(sem["full"], 1)
                    ready(NK[-1])
                    n = lambda k: after(i, U, k)
                    for r in range(U + LV):
                        if r < U:
                            j, t = r // TT, r % TT
                            pe.wait_ge(sem["probs"], n(r - 3 if r >= 3 else -1))
                            for v in range(2):
                                o = 256 * v
                                pe.matmul(pS[r % 3][:, o:o + P], QT[:, j, P * t:P * t + P], KT[:, j, v, P * t:P * t + P], start=True, stop=True)
                                if t == 0:
                                    pe.matmul(pS[r % 3][0:64, o + P:o + 192], IDB[:, 0:64], NEGB[:, :], start=True, stop=True)
                                else:
                                    pe.matmul(pS[r % 3][0:64, o + P:o + 192], QT[:, j, P * t:P * t + 64], KT[:, j, v, P * t - 64:P * t], start=True, stop=True)
                                if t == TT - 1:
                                    last = pe.matmul(pS[r % 3][64:128, o + P:o + 192], IDB[:, 64:128], NEGB[:, :], start=True, stop=True)
                                else:
                                    last = pe.matmul(pS[r % 3][64:128, o + P:o + 192], QT[:, j, P * t + 64:P * t + P],
                                                     KT[:, j, v, P * t + P:P * t + 192], start=True, stop=True)
                            last.then_inc(sem["scores"], 1)
                        if LP <= r < U + LP:
                            q = (r - LP) % 4
                            pe.wait_ge(sem["scaled"], n(r - LP))
                            pe.wait_ge(sem["pmain"], n(r - LP - 1))
                            pe.wait_ge(sem["pextra"], n(r - LP - 1))
                            for v in range(2):
                                pe.transpose(pP[0][:, P * v:P * v + P], PR[:, q, v, 0:P], IDF[:, :])
                                last = pe.transpose(pP[1][0:64, P * v:P * v + P], PR[:, q, v, P:192], IDF[:, :])
                            last.then_inc(sem["pturn"], 1)
                        if r == LV:
                            ready(NVV[-1])
                        if r >= LV:
                            q = (r - LV) % 2
                            j, t = (r - LV) // TT, (r - LV) % TT
                            pe.wait_ge(sem["pmain"], n(r - LV))
                            pe.wait_ge(sem["pextra"], n(r - LV))
                            if t == 0:
                                pe.wait_ge(sem["outTcopy"], after(i, J, j - 2))
                            for v in range(2):
                                h = 2 * j + v
                                vc = slice(64 * h, 64 * h + 64)
                                dst = pO[j % 2][64 * v:64 * v + 64, P * t:P * t + P]
                                last = pe.matmul(dst, V[:, t, vc], PTM[:, q, v, :], start=True, stop=False, skip_group_check=True)
                                if t > 0:
                                    last = pe.matmul(dst[:, 0:64], VL[:, t - 1, vc], PTE[:, q, v, 0:64], start=False, stop=t == TT - 1, skip_group_check=True)
                                if t < TT - 1:
                                    last = pe.matmul(dst[:, 64:P], V[0:64, t + 1, vc], PTE[:, q, v, 64:P], start=False, stop=True, skip_group_check=True)
                            last.then_inc(sem["outT"], 1)
                    for m in NO:
                        k = jobs[m][1]
                        free(m)
                        for c in range(4):
                            if m == NO[0] and c in (0, 3):
                                pe.wait_ge(sem["outTcopy"], after(i, J, J - 2 + c // 3))
                            last = pe.matmul(pW[m % 2][:, :], OT[:, c, P * k:P * k + P], WO[:, c, :], start=c == 0, stop=c == 3)
                        last.then_inc(sem["full"], 1)


def phase_route(nc, used, a, s_route, sel, qsel, qidx):
    NQ, ITERS, LAPS, RISE = 256, 50, 7, 6.0
    WINDOWS = (ITERS - 1) // LAPS
    assert WINDOWS * LAPS == ITERS - 1
    R2, QT2 = 2 * B, NQ // P
    with ExitStack() as ctx:
        def sb(name, shape, dt=f32):
            return ctx.enter_context(nc.sbuf_tensor("r_" + name, shape, dt))

        names = ["const", "loaded", "turned", "copied", "step", "low", "start", "window", "log", "kth", "expd", "rows", "turned2", "out", "stored", "top"]
        sem = open_phase(nc, used, ["r_" + n for n in names])
        sem = {n: sem["r_" + n] for n in names}
        u32 = mybir.dt.uint32
        SA = sb("sa", [P, B, 2, TT])
        SG = sb("sg", [P, TT, R2])
        IDF, LK, BASE = sb("idf", [P, P]), sb("lk", [R2, 2]), sb("base", [P, B])
        SR, T, E, MN = sb("sr", [R2, S]), sb("t", [R2, S]), sb("e", [R2, S]), sb("mn", [R2, S])
        SMX, NA, ML, NB, NBC, LG = (sb(n, [R2, 1]) for n in ("smx", "na", "ml", "nb", "nbc", "lg"))
        C, INVK = sb("c", [R2, LAPS + 1]), sb("invk", [R2, S])
        WK, M8, I8, IF = sb("wk", [B, S]), sb("m8", [B, NQ]), sb("i8", [B, NQ], u32), sb("if", [B, NQ])
        OUTW, OUTN, QW = sb("outw", [R2, S]), sb("outn", [B, S]), sb("qw", [B, NQ])
        SEL, QSEL, QIDX = sb("sel", [P, TT, 3 * B]), sb("qsel", [P, QT2, B]), sb("qidx", [P, QT2, B], u32)
        ps = [ctx.enter_context(nc.psum_tensor(f"r_ps{i}", [P, 512], f32)) for i in range(2)]
        with nc.Block() as block:
            @block.sync
            def _(sp):
                sp.dma_start(IDF[:, :], a["idf"]).then_inc(sem["const"], 16)
                sp.dma_start(LK[:, :], a["router_k"]).then_inc(sem["const"], 16)
                sp.dma_start(BASE[:, :], a["batch_base"]).then_inc(sem["const"], 16)
                sp.dma_start(SA[:, :, :, :].rearrange("p b r t -> p b (r t)"), s_route.rearrange("b p n -> p b n")).then_inc(sem["loaded"], 16)
                sp.wait_ge(sem["out"], SEED + 1)
                sp.dma_start(sel, SEL[:, :, :]).then_inc(sem["stored"], 16)
                sp.dma_start(qsel, QSEL[:, :, :]).then_inc(sem["stored"], 16)
                sp.dma_start(qidx, QIDX[:, :, :]).then_inc(sem["stored"], 16)
                sp.wait_ge(sem["stored"], SEED + 48)

            @block.tensor
            def _(pe):
                pe.wait_ge(sem["const"], SEED + 48)
                pe.wait_ge(sem["copied"], SEED + 1)
                for t in range(TT):
                    last = pe.transpose(ps[0][0:R2, P * t:P * t + P], SG[:, t, :], IDF[:, :])
                last.then_inc(sem["turned"], 1)
                pe.wait_ge(sem["rows"], SEED + 1)
                pe.wait_ge(sem["copied"], SEED + 2)
                for t in range(TT):
                    pe.transpose(ps[1][:, 24 * t:24 * t + R2], OUTW[:, P * t:P * t + P], IDF[0:R2, 0:R2])
                    pe.transpose(ps[1][:, 24 * t + R2:24 * t + 24], OUTN[:, P * t:P * t + P], IDF[0:B, 0:B])
                for t in range(QT2):
                    pe.transpose(ps[1][:, 128 + B * t:128 + B * t + B], QW[:, P * t:P * t + P], IDF[0:B, 0:B])
                    last = pe.transpose(ps[1][:, 192 + B * t:192 + B * t + B], IF[:, P * t:P * t + P], IDF[0:B, 0:B])
                last.then_inc(sem["turned2"], 1)

            @block.scalar
            def _(act):
                with act.Fori(0, WINDOWS) as i:
                    act.wait_ge(sem["low"], after(i, 1, 0))
                    act.activation(E[:, :], T[:, :], ACT.Exp, bias=NB[:, 0:1])
                    act.activation(C[:, 0:1], NBC[:, :], ACT.Exp).then_inc(sem["start"], 1)
                    act.wait_ge(sem["window"], after(i, 1, 0))
                    act.activation(LG[:, :], C[:, LAPS:LAPS + 1], ACT.Ln).then_inc(sem["log"], 1)
                act.wait_ge(sem["kth"], SEED + 1)
                act.activation(E[:, :], T[:, :], ACT.Exp).then_inc(sem["expd"], 1)

            @block.vector
            def _(dve):
                dve.wait_ge(sem["loaded"], SEED + 16)
                dve.tensor_copy(SG[:, :, :].rearrange("p t (r b) -> p t r b", r=2), SA[:, :, :, :].rearrange("p b r t -> p t r b")).then_inc(sem["copied"], 1)
                dve.wait_ge(sem["turned"], SEED + 1)
                dve.tensor_copy(SR[:, :], ps[0][0:R2, :]).then_inc(sem["copied"], 1)
                dve.wait_ge(sem["copied"], SEED + 2)
                dve.reduce_max(SMX[:, :], SR[:, :], axis=AX.X)
                dve.wait_ge(sem["const"], SEED + 48)
                dve.tensor_copy(INVK[:, :], LK[:, 1:2].broadcast_to([R2, S]))
                dve.tensor_copy(NA[:, :], LK[:, 0:1]).then_inc(sem["top"], 1)
                dve.wait_ge(sem["top"], SEED + 1)
                with dve.Fori(0, WINDOWS) as i:
                    steps = Steps(i, LAPS + 1)
                    dve.tensor_scalar(ML[:, :], SMX[:, :], NA[:, 0:1], -1.0, ALU.min, ALU.mult)
                    dve.tensor_scalar(T[:, :], SR[:, :], NA[:, 0:1], RISE, ALU.subtract, ALU.min).then_inc(sem["step"], 1)
                    dve.wait_ge(sem["step"], steps.next())
                    dve.tensor_scalar(NB[:, :], NA[:, :], ML[:, 0:1], None, ALU.add)
                    dve.tensor_scalar(NBC[:, :], NA[:, :], ML[:, 0:1], 80.0, ALU.add, ALU.min).then_inc(sem["low"], 1)
                    dve.wait_ge(sem["start"], after(i, 1, 0))
                    for lap in range(LAPS):
                        last = dve.scalar_tensor_tensor(out=MN[:, :], in0=E[:, :], scalar=C[:, lap:lap + 1], in1=INVK[:, :], op0=ALU.min, op1=ALU.mult,
                                                        accum_out=C[:, lap + 1:lap + 2])
                        if lap < LAPS - 1:
                            last.then_inc(sem["step"], 1)
                            dve.wait_ge(sem["step"], steps.next())
                    last.then_inc(sem["window"], 1)
                    dve.wait_ge(sem["log"], after(i, 1, 0))
                    dve.tensor_scalar(NA[:, :], LG[:, :], ML[:, 0:1], None, ALU.subtract).then_inc(sem["step"], 1)
                    dve.wait_ge(sem["step"], steps.next())
                    steps.close()
                dve.tensor_scalar(T[:, :], SR[:, :], NA[:, 0:1], 0.0, ALU.subtract, ALU.min).then_inc(sem["kth"], 1)
                dve.wait_ge(sem["expd"], SEED + 1)
                dve.tensor_scalar(OUTW[:, :], E[:, :], -1.0, 1.0, ALU.mult, ALU.add)
                dve.tensor_copy(WK[:, :], E[0:B, :]).then_inc(sem["top"], 1)
                dve.wait_ge(sem["top"], SEED + 2)
                dve.tensor_tensor(OUTW[:, :], OUTW[:, :], E[:, :], ALU.add)
                k = 2
                for r in range(NQ // 8):
                    eight = slice(8 * r, 8 * r + 8)
                    dve.max(M8[:, eight], WK[:, :]).then_inc(sem["top"], 1)
                    dve.wait_ge(sem["top"], SEED + k + 1)
                    dve.max_index(I8[:, eight], M8[:, eight], WK[:, :])
                    dve.match_replace(WK[:, :], M8[:, eight], WK[:, :], -1.0).then_inc(sem["top"], 1)
                    dve.wait_ge(sem["top"], SEED + k + 2)
                    k += 2
                dve.tensor_scalar(OUTN[:, :], WK[:, :], 0.0, None, ALU.is_ge)
                dve.tensor_copy(IF[:, :], I8[:, :])
                dve.tensor_scalar(QW[:, :], M8[:, :], -1.0, 1.0, ALU.mult, ALU.add).then_inc(sem["top"], 1)
                dve.wait_ge(sem["top"], SEED + k + 1)
                dve.tensor_tensor(QW[:, :], QW[:, :], M8[:, :], ALU.add).then_inc(sem["rows"], 1)
                dve.wait_ge(sem["turned2"], SEED + 1)
                dve.tensor_copy(SEL[:, :, :], ps[1][:, 0:24 * TT].rearrange("p (t n) -> p t n", n=24))
                dve.tensor_copy(QSEL[:, :, :], ps[1][:, 128:128 + QT2 * B].rearrange("p (t b) -> p t b", b=B))
                dve.tensor_tensor(QIDX[:, :, :], ps[1][:, 192:192 + QT2 * B].rearrange("p (t b) -> p t b", b=B),
                                  BASE[:, :].unsqueeze(1).broadcast_to([P, QT2, B]), ALU.add).then_inc(sem["out"], 1)

def phase_heavy(nc, used, a, xr, x1l, sel, qsel, qidx, x2, own, ahead):
    H, DH = 8, 64
    SCALE = DH ** -0.5
    J = 4
    QT2 = 2
    NQ_ = QT2 * P
    U = H * QT2
    LP, LV = 3, 4
    jobs = [("x", c) for c in range(4)] + [("k", j) for j in range(4)] + [("g", c) for c in (0, 2)] + \
           [("v", t) for t in range(3)] + [("q", j) for j in (0, 2)] + [("v", 3)] + \
           [("n", t) for t in range(QT2)] + [("z", j) for j in range(4)] + [("o", t) for t in range(QT2)]
    banks = Banks(jobs, lambda m, job: "dve" if job[0] in "on" else "act" if job[0] in "xgz" else ("act", "dve")[m % 2])
    NX, NK, NVV, NG, NQ, NN, NZ, NO = (banks.of(k) for k in "xkvgqnzo")
    with ExitStack() as ctx:
        def sb(name, shape, dt=f32):
            return ctx.enter_context(nc.sbuf_tensor("h_" + name, shape, dt))

        names = ["const", "loaded", "resid", "tanh", "zero", "full", "act_empty", "dve_empty", "scores", "negmax", "probs",
                 "scaled", "pturn", "pcopy", "outT", "outTcopy", "step", "base_out", "base", "weights", "idx", "go", "qnext", "ahead",
                 "largest", "all", "bound", "whigh", "wlow", "xhigh", "xsplit", "ghigh", "gsplit"]
        h_gather = semaphore(nc, used, "h_gather")
        h_scatter = semaphore(nc, used, "h_scatter")
        sem = open_phase(nc, used, ["h_" + n for n in names])
        sem = {n: sem["h_" + n] for n in names}
        emptied = {"act": sem["act_empty"], "dve": sem["dve_empty"]}
        WQ, WK, WV, WO = own
        GA, NKB, NVB, NQB = sb("ga", [P, CT]), sb("nkb", [P, J, 2]), sb("nvb", [P, J, P]), sb("nqb", [P, D])
        SEL, TSEL = sb("sel", [P, TT, 3 * B]), sb("tsel", [P, TT, 3 * B])
        QSEL, QIDX = sb("qsel", [P, QT2, B]), sb("qidx", [P, QT2, B], mybir.dt.uint32)
        QROW = sb("qrow", [P, 2, QT2], mybir.dt.uint32)
        IDF = sb("idf", [P, P])
        GT, TG = sb("gt", [P, 4]), sb("tg", [P, 4])
        X, XL = sb("x", [P, TT, D]), sb("xl", [P, TT, D])
        XG, XLG, YG = (sb(n, [P, QT2, D]) for n in ("xg", "xlg", "yg"))
        XGT = sb("xgT", [P, CT, NQ_])
        XT = sb("xT", [P, CT, S])
        XS, XGS, WS = sb("xs", [P, 2, CT, S], f16), sb("xgs", [P, 2, CT, NQ_], f16), sb("ws", [P, 2, 3, CT, D], f16)
        WMAX, MXW, ALLM = sb("wmax", [P, 3]), sb("mxw", [P, 3]), sb("allm", [P, 3])
        BOUND, SC3 = sb("bound", [P, 3]), sb("sc3", [P, 3])
        UN = sb("un", [P, 2])
        QT, KT, V = sb("qT", [P, J, NQ_]), sb("kT", [P, J, 2, S]), sb("v", [P, TT, D])
        WCOL, QCOL = sb("wcol", [P, TT, 3]), sb("qcol", [P, QT2])
        NS = sb("ns", [P, QT2, H])
        PR, PT = sb("pr", [P, 4, S]), sb("pT", [P, 2, TT, NQ_])
        SC = sb("sc", [P, 4, 8])
        PN, PNT = sb("pn", [P, 2, QT2, P]), sb("pnT", [P, NQ_])
        OT, Y = sb("oT", [P, J, NQ_]), sb("y", [P, TT, D])
        bank = [ctx.enter_context(nc.psum_tensor(f"h_ps{i}", [P, 512], f32)) for i in range(8)]
        pW, pS, pP, pO = bank[0:2], bank[2:5], bank[5:7], bank[7]

        with nc.Block() as block:
            @block.sync
            def _(sp):
                for dst, src in ((GA[:, :], a["gamma"]), (NKB[:, :, :], a["null_k"]), (NVB[:, :, :], a["null_v"]), (NQB[:, :], a["null_q"]),
                                 (SEL[:, :, :], sel), (QSEL[:, :, :], qsel), (QIDX[:, :, :], qidx), (IDF[:, :], a["idf"]), (GT[:, :], a["gates"])):
                    sp.dma_start(dst, src).then_inc(sem["const"], 16)
                with sp.Fori(0, B) as i:
                    row = lambda t: t[bass.ds(i, 1), :, :].rearrange("o (t p) d -> p (o t) d", p=P)
                    sp.wait_ge(sem["full"], after(i, len(jobs), NX[-1] - len(jobs)))
                    sp.dma_start(X[:, :, :], row(xr)).then_inc(sem["loaded"], 16)
                    sp.wait_ge(sem["base"], after(i, 1, -1))
                    sp.dma_start(XL[:, :, :], row(x1l)).then_inc(sem["resid"], 16)
                    sp.wait_ge(sem["base"], after(i, 1, 0))
                    sp.dma_start(row(x2), Y[:, :, :]).then_inc(sem["base_out"], 16)
                loaded_ahead(sp, ahead, sem)
                sp.wait_ge(sem["base_out"], SEED + 16 * B)

            @block.gpsimd
            def _(pool):
                flat = lambda t: t.rearrange("b s d -> (b s) d")

                def gather(b, parity):
                    for t in range(QT2):
                        for dst, src in ((XG, xr), (XLG, x1l)):
                            pool.indirect_dma_start(out=dst[:, t, :], out_offset=None, in_=flat(src),
                                                    in_offset=bass.IndirectOffsetOnAxis(ap=QROW[:, parity, t:t + 1], axis=0)).then_inc(h_gather, 16)

                pool.wait_ge(sem["largest"], SEED + 1)
                pool.partition_all_reduce(ALLM[:, :], MXW[:, :], P, bass.bass_isa.ReduceOp.max).then_inc(sem["all"], 1)
                pool.wait_ge(sem["idx"], SEED + 1)
                gather(0, 0)
                with pool.Fori(0, B // 2) as i2:
                    for u in range(2):
                        i = i2 * 2 + u
                        pool.wait_ge(sem["dve_empty"], banks.emptied(i, NO[-1], "dve"))
                        pool.wait_ge(sem["base_out"], i * 16 + (SEED + 16))
                        pool.sem_inc(sem["go"], 1)
                        for t in range(QT2):
                            pool.indirect_dma_start(out=flat(x2), out_offset=bass.IndirectOffsetOnAxis(ap=QROW[:, u, t:t + 1], axis=0),
                                                    in_=YG[:, t, :], in_offset=None).then_inc(h_scatter, 16)
                        pool.wait_ge(sem["idx"], after(i, 1, 1))
                        pool.sem_inc(sem["go"], 1)
                        gather(i + 1, 1 - u)
                        pool.wait_ge(h_scatter, i * 32 + 32)
                        pool.sem_inc(sem["qnext"], 1)
                pool.wait_ge(h_gather, 64 * (B + 1))

            @block.scalar
            def _(act):
                act.wait_ge(sem["const"], SEED + 16 * 9)
                act.activation(TG[:, :], GT[:, :], ACT.Tanh).then_inc(sem["tanh"], 1)
                act.wait_ge(sem["bound"], SEED + 6)
                for n, W in enumerate((WQ, WK, WV)):
                    act.mul(WS[:, 0, n, :, :], W[:, :, :], SC3[:, min(n, 1) + 1:min(n, 1) + 2]).then_inc(sem["whigh"], 1)
                act.wait_ge(sem["loaded"], SEED + 16)
                load_ahead(act, ahead, sem)
                with act.Fori(0, B) as i:
                    def empty(m):
                        kind, k = jobs[m]
                        w = pW[m % 2]
                        act.wait_ge(sem["full"], after(i, len(jobs), m))
                        if kind == "x":
                            act.mul(XT[:, k, :], w[:, :], GA[:, k:k + 1]).then_inc(sem["act_empty"], 1)
                        if kind == "g":
                            act.mul(XGT[:, k, :], w[:, 0:NQ_], GA[:, k:k + 1])
                            act.mul(XGT[:, k + 1, :], w[:, NQ_:], GA[:, k + 1:k + 2]).then_inc(sem["act_empty"], 1)
                        if kind == "q":
                            act.mul(QT[:, k:k + 2, :], w[:, :].rearrange("p (j q) -> p j q", j=2), UN[:, 1:2]).then_inc(sem["act_empty"], 1)
                        if kind == "k":
                            act.mul(KT[0:64, k, 0, :], w[0:64, :], UN[0:64, 0:1])
                            act.mul(KT[64:128, k, 1, :], w[64:128, :], UN[64:128, 0:1]).then_inc(sem["act_empty"], 1)
                        if kind == "v":
                            act.wait_ge(sem["weights"], after(i, 1, 0))
                            act.mul(V[:, k, :], w[:, :], WCOL[:, k, 1:2]).then_inc(sem["act_empty"], 1)
                        if kind == "z":
                            act.copy(PNT[:, :], w[:, 0:NQ_]).then_inc(sem["act_empty"], 1)

                    for m in range(NN[0]):
                        if banks.engine[m] == "act":
                            empty(m)
                    n = lambda k: after(i, U, k)
                    for r in range(U + LV + 1):
                        if LP <= r < U + LP:
                            h, t = (r - LP) // QT2, (r - LP) % QT2
                            act.wait_ge(sem["pturn"], n(r - LP))
                            act.wait_ge(sem["outT"], after(i, H, h - 2))
                            act.copy(PT[:, h % 2, :, P * t:P * t + P], pP[r % 2][:, :].rearrange("p (k q) -> p k q", k=TT)).then_inc(sem["pcopy"], 1)
                        if r < U:
                            h, t = r // QT2, r % QT2
                            act.wait_ge(sem["negmax"], n(r))
                            act.wait_ge(sem["pturn"], n(r - 4))
                            act.activation(PR[:, r % 4, :], pS[r % 3][:, :], ACT.Exp, bias=SC[:, r % 4, 0:1], accum_out=SC[:, r % 4, 1:2])
                            act.activation(SC[:, r % 4, 2:3], NS[:, t, h:h + 1], ACT.Exp, bias=SC[:, r % 4, 0:1]).then_inc(sem["probs"], 1)
                        if r >= LV and (r - LV) % (2 * QT2) == 2 * QT2 - 1:
                            empty(NZ[(r - LV) // (2 * QT2)])
                        if r > LV and (r - LV - 1) % (2 * QT2) == 2 * QT2 - 1:
                            j = (r - LV - 1) // (2 * QT2)
                            act.wait_ge(sem["outT"], after(i, H, 2 * j + 1))
                            act.copy(OT[:, j, :], pO[:, 0:NQ_]).then_inc(sem["outTcopy"], 1)

            @block.vector
            def _(dve):
                dve.memset(PN[:, :, :, :], 0.0).then_inc(sem["zero"], 1)
                dve.memset(KT[:, :, :, :], 0.0).then_inc(sem["zero"], 1)
                dve.wait_ge(sem["const"], SEED + 16 * 9)
                for k, W in enumerate((WQ[:, :, :], WK[:, :, :], WV[:, :, :])):
                    dve.tensor_reduce(WMAX[:, k:k + 1], W.rearrange("p c n -> p (c n)"), axis=AX.X, op=ALU.max, apply_absolute_value=True)
                dve.tensor_reduce(MXW[:, 0:1], GA[:, :], axis=AX.X, op=ALU.max, apply_absolute_value=True).then_inc(sem["bound"], 1)
                dve.wait_ge(sem["bound"], SEED + 1)
                dve.tensor_copy(MXW[:, 1:2], WMAX[:, 0:1])
                dve.tensor_scalar(MXW[:, 2:3], WMAX[:, 1:2], WMAX[:, 2:3], None, ALU.max).then_inc(sem["largest"], 1)
                dve.wait_ge(sem["tanh"], SEED + 1)
                dve.wait_ge(sem["zero"], SEED + 2)
                dve.tensor_scalar(TSEL[:, :, :], SEL[:, :, :], TG[:, 2:3], None, ALU.mult).then_inc(sem["zero"], 1)
                dve.wait_ge(sem["zero"], SEED + 3)
                dve.tensor_scalar(QSEL[:, :, :], QSEL[:, :, :], TG[:, 2:3], None, ALU.mult).then_inc(sem["zero"], 1)
                dve.tensor_copy(QROW[:, 0, :], QIDX[:, :, 0]).then_inc(sem["idx"], 1)
                dve.wait_ge(sem["zero"], SEED + 4)
                dve.wait_ge(sem["all"], SEED + 1)
                dve.tensor_scalar(BOUND[:, 0:1], ALLM[:, 0:1], float(np.sqrt(D)) / TOP, 1e-30, ALU.mult, ALU.max)
                dve.tensor_scalar(BOUND[:, 1:3], ALLM[:, 1:3], 1.0 / TOP, 1e-30, ALU.mult, ALU.max).then_inc(sem["bound"], 1)
                dve.wait_ge(sem["bound"], SEED + 2)
                dve.reciprocal(SC3[:, :], BOUND[:, :]).then_inc(sem["bound"], 1)
                dve.tensor_scalar(UN[:, 0:1], BOUND[:, 0:1], BOUND[:, 2:3], None, ALU.mult).then_inc(sem["bound"], 1)
                dve.tensor_scalar(UN[:, 1:2], BOUND[:, 0:1], BOUND[:, 1:2], SCALE, ALU.mult, ALU.mult).then_inc(sem["bound"], 1)
                dve.wait_ge(sem["bound"], SEED + 5)
                dve.tensor_scalar(GA[:, :], GA[:, :], SC3[:, 0:1], None, ALU.mult).then_inc(sem["bound"], 1)
                dve.wait_ge(sem["bound"], SEED + 6)
                for n, W in enumerate((WQ, WK, WV)):
                    dve.wait_ge(sem["whigh"], SEED + n + 1)
                    dve.scalar_tensor_tensor(out=WS[:, 1, n, :, :], in0=W[:, :, :], scalar=SC3[:, min(n, 1) + 1:min(n, 1) + 2], in1=WS[:, 0, n, :, :],
                                             op0=ALU.mult, op1=ALU.subtract).then_inc(sem["wlow"], 1)
                with dve.Fori(0, B) as i:
                    following = dve.snap((i + 1) % B)
                    parity = dve.snap((i + 1) % 2)
                    steps = Steps(i, 3 * U)
                    dve.wait_ge(sem["dve_empty"], banks.emptied(i, -1, "dve"))
                    dve.tensor_copy(QCOL[:, :], QSEL[:, :, bass.ds(i, 1)].rearrange("p t o -> p (t o)"))
                    dve.tensor_scalar(WCOL[:, :, 1], SEL[:, :, bass.ds(i + B, 1)].rearrange("p t o -> p (t o)"), UN[:, 0:1], None, ALU.mult)
                    dve.tensor_copy(WCOL[:, :, 2], TSEL[:, :, bass.ds(i + 2 * B, 1)].rearrange("p t o -> p (t o)")).then_inc(sem["weights"], 1)
                    dve.wait_ge(sem["weights"], after(i, 1, 0))

                    def empty(m):
                        kind, k = jobs[m]
                        w = pW[m % 2]
                        dve.wait_ge(sem["full"], after(i, len(jobs), m))
                        if kind == "q":
                            dve.tensor_scalar(QT[:, k:k + 2, :], w[:, :].rearrange("p (j q) -> p j q", j=2), UN[:, 1:2], None, ALU.mult).then_inc(sem["dve_empty"], 1)
                        if kind == "k":
                            dve.tensor_scalar(KT[0:64, k, 0, :], w[0:64, :], UN[0:64, 0:1], None, ALU.mult)
                            dve.tensor_scalar(KT[64:128, k, 1, :], w[64:128, :], UN[64:128, 0:1], None, ALU.mult).then_inc(sem["dve_empty"], 1)
                        if kind == "v":
                            dve.tensor_scalar(V[:, k, :], w[:, :], WCOL[:, k, 1:2], None, ALU.mult).then_inc(sem["dve_empty"], 1)
                        if kind == "n":
                            dve.tensor_copy(NS[:, k, :], w[:, 0:H]).then_inc(sem["dve_empty"], 1)
                        if kind == "o":
                            dve.scalar_tensor_tensor(out=YG[:, k, :], in0=w[:, :], scalar=QCOL[:, k:k + 1], in1=XLG[:, k, :],
                                                     op0=ALU.mult, op1=ALU.add).then_inc(sem["dve_empty"], 1)

                    def split(m):
                        kind, k = jobs[m]
                        dve.wait_ge(sem["act_empty"], banks.emptied(i, m, "act"))
                        if kind == "x":
                            dve.tensor_copy(XS[:, 0, k, :], XT[:, k, :]).then_inc(sem["xhigh"], 1)
                            dve.wait_ge(sem["xhigh"], after(i, CT, k))
                            dve.tensor_tensor(XS[:, 1, k, :], XT[:, k, :], XS[:, 0, k, :], ALU.subtract).then_inc(sem["xsplit"], 1)
                        else:
                            both = slice(k, k + 2)
                            dve.tensor_copy(XGS[:, 0, both, :], XGT[:, both, :]).then_inc(sem["ghigh"], 1)
                            dve.wait_ge(sem["ghigh"], after(i, 2, k // 2))
                            dve.tensor_tensor(XGS[:, 1, both, :], XGT[:, both, :], XGS[:, 0, both, :], ALU.subtract).then_inc(sem["gsplit"], 1)

                    for m in range(NZ[0]):
                        if jobs[m][0] in "xg":
                            split(m)
                        elif banks.engine[m] == "dve":
                            empty(m)
                    dve.wait_ge(sem["dve_empty"], banks.emptied(i, NN[-1], "dve"))
                    n = lambda k: after(i, U, k)
                    for r in range(U + 1):
                        if r < U:
                            h, t = r // QT2, r % QT2
                            dve.wait_ge(sem["scores"], n(r))
                            dve.wait_ge(sem["scaled"], n(r - 4))
                            dve.reduce_max(SC[:, r % 4, 4:5], pS[r % 3][:, :], axis=AX.X).then_inc(sem["step"], 1)
                            dve.wait_ge(sem["step"], steps.next())
                            dve.tensor_scalar(SC[:, r % 4, 0:1], SC[:, r % 4, 4:5], NS[:, t, h:h + 1], -1.0, ALU.max, ALU.mult).then_inc(sem["negmax"], 1)
                        if r >= 1:
                            q = (r - 1) % 4
                            h, t = (r - 1) // QT2, (r - 1) % QT2
                            dve.wait_ge(sem["probs"], n(r - 1))
                            dve.tensor_scalar(SC[:, q, 5:6], SC[:, q, 1:2], SC[:, q, 2:3], None, ALU.add).then_inc(sem["step"], 1)
                            dve.wait_ge(sem["step"], steps.next())
                            dve.reciprocal(SC[:, q, 3:4], SC[:, q, 5:6]).then_inc(sem["step"], 1)
                            dve.wait_ge(sem["step"], steps.next())
                            if t == 0 and h % 2 == 0:
                                dve.wait_ge(sem["full"], after(i, len(jobs), (NZ[h // 2 - 2] if h >= 4 else NZ[h // 2 + 2] - len(jobs))))
                            dve.tensor_scalar(PN[:, h // 2 % 2, t, h:h + 1], SC[:, q, 2:3], SC[:, q, 3:4], None, ALU.mult)
                            dve.tensor_scalar(PR[:, q, :], PR[:, q, :], SC[:, q, 3:4], None, ALU.mult).then_inc(sem["scaled"], 1)
                        if r == 3:
                            dve.wait_ge(sem["qnext"], after(i, 1, -1))
                            dve.tensor_copy(QROW[:, bass.ds(parity, 1), :].rearrange("p o t -> p (o t)"), QIDX[:, :, bass.ds(following, 1)].rearrange("p t o -> p (t o)")).then_inc(sem["idx"], 1)
                        if r in (4, 6, 8, 10):
                            t = (r - 4) // 2
                            if t == 0:
                                dve.wait_ge(sem["resid"], i * 16 + (SEED + 16))
                                dve.wait_ge(sem["base_out"], i * 16 + SEED)
                            last = dve.scalar_tensor_tensor(out=Y[:, t, :], in0=NQB[:, :], scalar=WCOL[:, t, 2:3], in1=XL[:, t, :], op0=ALU.mult, op1=ALU.add)
                            if t == TT - 1:
                                last.then_inc(sem["base"], 1)
                    dve.wait_ge(h_gather, i * 64 + 64)
                    dve.wait_ge(sem["qnext"], after(i, 1, -1))
                    for m in NO:
                        empty(m)
                    steps.close()

            @block.tensor
            def _(pe):
                pe.wait_ge(sem["const"], SEED + 16 * 9)
                pe.wait_ge(sem["wlow"], SEED + 3)
                pe.wait_ge(sem["zero"], SEED + 2)
                with pe.Fori(0, B) as i:
                    def ready(m):
                        for e in ("act", "dve"):
                            pe.wait_ge(emptied[e], banks.emptied(i, m, e))

                    def free(m):
                        before = banks.engine[(m - 2) % len(jobs)]
                        pe.wait_ge(emptied[before], banks.emptied(i, m - 2, before))

                    for m in range(NZ[0]):
                        kind, k = jobs[m]
                        if kind == "x" and k == 0:
                            pe.wait_ge(sem["loaded"], i * 16 + (SEED + 16))
                        if kind == "g" and k == 0:
                            pe.wait_ge(h_gather, i * 64 + 64)
                        if kind == "q" and k == 0:
                            pe.wait_ge(sem["gsplit"], after(i, 2, 1))
                        if kind == "n" and k == 0:
                            ready(NQ[-1])
                        free(m)
                        w = pW[m % 2]
                        for c in range(4):
                            if kind == "x":
                                last = pe.transpose(w[:, P * c:P * c + P], X[:, c, P * k:P * k + P], IDF[:, :])
                            if kind == "g":
                                g, t = k + c // 2, c % 2
                                last = pe.transpose(w[:, P * c:P * c + P], XG[:, t, P * g:P * g + P], IDF[:, :])
                            if kind == "q":
                                for n in range(2):
                                    ch = 2 * (c % 2) + n
                                    for e, (one, two) in enumerate(THREE):
                                        last = pe.matmul(w[:, NQ_ * (c // 2):NQ_ * (c // 2) + NQ_], WS[:, one, 0, ch, P * (k + c // 2):P * (k + c // 2) + P],
                                                         XGS[:, two, ch, :], start=ch + e == 0, stop=ch + e == CT + 1)
                            if kind == "k" and k == 0:
                                pe.wait_ge(sem["xsplit"], after(i, CT, c))
                            for e, (one, two) in enumerate(THREE):
                                first, final = c + e == 0, c + e == CT + 1
                                if kind == "k":
                                    last = pe.matmul(w[:, :], WS[:, one, 1, c, P * k:P * k + P], XS[:, two, c, :], start=first, stop=final)
                                if kind == "v":
                                    last = pe.matmul(w[:, :], XS[:, one, c, P * k:P * k + P], WS[:, two, 2, c, :], start=first, stop=final)
                            if kind == "n":
                                last = pe.matmul(w[:, 2 * c:2 * c + 2], QT[:, c, P * k:P * k + P], NKB[:, c, :], start=True, stop=True)
                        last.then_inc(sem["full"], 1)
                    n = lambda k: after(i, U, k)
                    for r in range(U + LV):
                        if r < U:
                            h, t = r // QT2, r % QT2
                            pe.wait_ge(sem["probs"], n(r - 3 if r >= 3 else -1))
                            pe.matmul(pS[r % 3][:, :], QT[:, h // 2, P * t:P * t + P], KT[:, h // 2, h % 2, :], start=True, stop=True).then_inc(sem["scores"], 1)
                        if LP <= r < U + LP:
                            q = (r - LP) % 4
                            pe.wait_ge(sem["scaled"], n(r - LP))
                            pe.wait_ge(sem["pcopy"], n(r - LP - 2))
                            for k in range(TT):
                                last = pe.transpose(pP[r % 2][:, P * k:P * k + P], PR[:, q, P * k:P * k + P], IDF[:, :])
                            last.then_inc(sem["pturn"], 1)
                        if r == LV:
                            ready(NVV[-1])
                        if r >= LV and (r - LV) % QT2 == QT2 - 1:
                            h = (r - LV) // QT2
                            j, v = h // 2, h % 2
                            if v == 1:
                                free(NZ[j])
                                for t in range(QT2):
                                    last = pe.transpose(pW[NZ[j] % 2][:, P * t:P * t + P], PN[:, j % 2, t, :], IDF[:, :])
                                last.then_inc(sem["full"], 1)
                            pe.wait_ge(sem["pcopy"], n(QT2 * h + QT2 - 1))
                            if v == 0:
                                pe.wait_ge(sem["outTcopy"], after(i, J, j - 1))
                            for k in range(TT):
                                last = pe.matmul(pO[64 * v:64 * v + 64, 0:NQ_], V[:, k, 64 * h:64 * h + 64], PT[:, h % 2, k, :],
                                                 start=k == 0, stop=False, skip_group_check=True)
                            if v == 1:
                                pe.wait_ge(emptied["act"], banks.emptied(i, NZ[j], "act"))
                                last = pe.matmul(pO[:, 0:NQ_], NVB[:, j, :], PNT[:, :], start=False, stop=True, skip_group_check=True)
                            last.then_inc(sem["outT"], 1)
                    for m in NO:
                        k = jobs[m][1]
                        free(m)
                        for c in range(4):
                            if m == NO[0] and c in (0, 3):
                                pe.wait_ge(sem["outTcopy"], after(i, J, J - 2 + c // 3))
                            last = pe.matmul(pW[m % 2][:, :], OT[:, c, P * k:P * k + P], WO[:, c, :], start=c == 0, stop=c == 3)
                        last.then_inc(sem["full"], 1)


def phase_window(nc, used, a, x2, x3, own, ahead):
    H, DH = 16, 32
    SCALE = DH ** -0.5
    J = 4
    U = H * TT
    LP, LV = 3, 5
    jobs = [("x", c) for c in range(4)] + [("q", j) for j in range(4)] + [("k", j) for j in range(4)] + \
           [("v", t) for t in range(4)] + [("o", t) for t in range(4)]
    banks = Banks(jobs, lambda m, job: "dve" if job[0] in "xvo" else "act")
    NX, NQ, NK, NVV, NO = (banks.of(k) for k in "xqkvo")

    def tiles(t):
        return min(t + 1, 3)
    with ExitStack() as ctx:
        def sb(name, shape, dt=f32):
            return ctx.enter_context(nc.sbuf_tensor("c_" + name, shape, dt))

        names = ["const", "loaded", "resid", "ctx", "tanh", "zero", "read", "nstep", "stats", "rstd", "norm", "full", "act_empty", "dve_empty",
                 "scores", "negmax", "probs", "scaled", "pturn", "pcopy", "outT", "outTcopy", "step", "out", "biased", "once", "ahead",
                 "largest", "all", "bound", "whigh", "wlow", "xhigh"]
        sem = open_phase(nc, used, ["c_" + n for n in names])
        sem = {n: sem["c_" + n] for n in names}
        emptied = {"act": sem["act_empty"], "dve": sem["dve_empty"]}
        WQ, WK, WV, WO = own
        BQ, BK, BQS, BV, BO = sb("bq", [P, CT]), sb("bk", [P, CT]), sb("bqs", [P, CT]), sb("bv", [P, D]), sb("bo", [P, D])
        IDF, IDB, MASK = sb("idf", [P, P]), sb("idb", [P, P], bf16), sb("mask", [P, 3 * P], bf16)
        GT, TG = sb("gt", [P, 4]), sb("tg", [P, 4])
        X, XL, XB, C = (sb(n, [P, TT, D]) for n in ("x", "xl", "xb", "cT"))
        QT, V = sb("qT", [P, J, S]), sb("v", [P, TT, D])
        XS, WS = sb("xs", [P, 2, CT, S], f16), sb("ws", [P, 2, CT, D], f16)
        MXW, ALLM, BOUND, WSC, UQ = (sb(n, [P, 1]) for n in ("mxw", "allm", "bound", "wsc", "uq"))
        KT = sb("kT", [P, J, 4, S])
        BN, MV, VE, RD, POWT = sb("bn", [P, TT, 6]), sb("mv", [P, TT, 2]), sb("ve", [P, TT]), sb("rd", [P, TT]), sb("pow", [P, TT])
        PR, PT = sb("pr", [P, 4, 3 * P]), sb("pT", [P, 3, 3 * P])
        NM, SM, RI = sb("nm", [P, 4]), sb("sm", [P, 4]), sb("ri", [P, 4])
        OT, Y = sb("oT", [P, J, S]), sb("y", [P, TT, D])
        bank = [ctx.enter_context(nc.psum_tensor(f"c_ps{i}", [P, 512], f32)) for i in range(8)]
        pW, pS, pP = bank[0:2], bank[2:5], bank[5:7]
        pO = bank[7], pW[1]
        with nc.Block() as block:
            @block.sync
            def _(sp):
                sp.dma_start(X[:, :, :], x2[0, :, :].rearrange("(t p) d -> p t d", p=P)).then_inc(sem["loaded"], 16)
                for dst, src in ((BQ[:, :], a["xbq"]), (BK[:, :], a["xbk"]), (BV[:, :], a["xbv"]), (BO[:, :], a["xbo"]),
                                 (IDF[:, :], a["idf"]), (IDB[:, :], a["idb"]), (MASK[:, :], a["mask_w"]), (GT[:, :], a["gates"])):
                    sp.dma_start(dst, src).then_inc(sem["const"], 16)
                load_ahead(sp, ahead, sem)
                with sp.Fori(0, B) as i:
                    row = lambda t, b=i: t[bass.ds(b, 1), :, :].rearrange("o (t p) d -> p (o t) d", p=P)
                    following = sp.snap((i + 1) % B)
                    sp.wait_ge(sem["read"], after(i, 1, 0))
                    sp.dma_start(X[:, :, :], row(x2, following)).then_inc(sem["loaded"], 16)
                    sp.wait_ge(sem["full"], after(i, len(jobs), NVV[-1] - len(jobs)))
                    sp.dma_start(C[:, :, :], a["ctxT"][bass.ds(i, 1), :, :, :].rearrange("o p c n -> (o p) c n")).then_inc(sem["ctx"], 16)
                    sp.wait_ge(sem["dve_empty"], banks.emptied(i, -1, "dve"))
                    sp.dma_start(XL[:, :, :], row(x2)).then_inc(sem["resid"], 16)
                    sp.wait_ge(sem["dve_empty"], banks.emptied(i, NO[-1], "dve"))
                    sp.dma_start(row(x3), Y[:, :, :]).then_inc(sem["out"], 16)
                loaded_ahead(sp, ahead, sem)
                sp.wait_ge(sem["out"], SEED + 16 * B)

            @block.gpsimd
            def _(pool):
                pool.wait_ge(sem["largest"], SEED + 1)
                pool.partition_all_reduce(ALLM[:, :], MXW[:, :], P, bass.bass_isa.ReduceOp.max).then_inc(sem["all"], 1)
                pool.wait_ge(sem["once"], SEED + 1)
                pool.wait_ge(sem["stats"], SEED + 1)
                pool.tensor_tensor(RD[:, :], VE[:, :], POWT[:, :], ALU.pow).then_inc(sem["rstd"], 1)
                with pool.Fori(0, B) as i:
                    pool.wait_ge(sem["resid"], i * 16 + (SEED + 16))
                    for t in range(TT):
                        last = pool.tensor_tensor(XL[:, t, :], XL[:, t, :], BO[:, :], ALU.add)
                    last.then_inc(sem["biased"], 1)
                    pool.wait_ge(sem["stats"], after(i, 1, 1))
                    pool.tensor_tensor(RD[:, :], VE[:, :], POWT[:, :], ALU.pow).then_inc(sem["rstd"], 1)

            @block.scalar
            def _(act):
                act.wait_ge(sem["const"], SEED + 16 * 8)
                act.activation(TG[:, :], GT[:, :], ACT.Tanh).then_inc(sem["tanh"], 1)
                act.mul(BQS[:, :], BQ[:, :], SCALE).then_inc(sem["tanh"], 1)
                act.wait_ge(sem["tanh"], SEED + 2)
                act.wait_ge(sem["bound"], SEED + 3)
                act.mul(WS[:, 0, :, :], WQ[:, :, :], WSC[:, 0:1]).then_inc(sem["whigh"], 1)
                with act.Fori(0, B) as i:
                    for m in range(NVV[0]):
                        kind, k = jobs[m]
                        w = pW[m % 2]
                        act.wait_ge(sem["full"], after(i, len(jobs), m))
                        if kind == "x":
                            act.mul(XS[:, 0, k, :], w[:, :], XSCALE).then_inc(sem["xhigh"], 1)
                            continue
                        if kind == "q":
                            last = act.activation(QT[:, k, :], w[:, :], ACT.Identity, bias=BQS[:, k:k + 1], scale=UQ[:, 0:1])
                        if kind == "k":
                            for n in range(4):
                                rows = slice(DH * n, DH * n + DH)
                                last = act.activation(KT[rows, k, n, :], w[rows, :], ACT.Identity, bias=BK[rows, k:k + 1])
                        last.then_inc(sem["act_empty"], 1)
                    n = lambda k: after(i, U, k)
                    for r in range(U + LV + 1):
                        if LP <= r < U + LP:
                            w, q = P * tiles((r - LP) % TT), (r - LP) % 3
                            act.wait_ge(sem["pturn"], n(r - LP))
                            act.wait_ge(sem["outT"], n(r - LP - 3))
                            act.copy(PT[:, q, 0:w], pP[(r - LP) % 2][:, 0:w]).then_inc(sem["pcopy"], 1)
                        if r < U:
                            w = P * tiles(r % TT)
                            act.wait_ge(sem["negmax"], n(r))
                            act.wait_ge(sem["pturn"], n(r - 4))
                            act.activation(PR[:, r % 4, 0:w], pS[r % 3][:, 0:w], ACT.Exp, bias=NM[:, r % 4:r % 4 + 1],
                                           accum_out=SM[:, r % 4:r % 4 + 1]).then_inc(sem["probs"], 1)
                        if r > LV and (r - LV - 1) % (4 * TT) == 4 * TT - 1:
                            j = (r - LV - 1) // (4 * TT)
                            act.wait_ge(sem["outT"], n(r - LV - 1))
                            act.copy(OT[:, j, :], pO[j % 2][:, :]).then_inc(sem["outTcopy"], 1)

            @block.vector
            def _(dve):
                dve.memset(POWT[:, :], -0.5).then_inc(sem["zero"], 1)
                dve.memset(KT[:, :, :, :], 0.0).then_inc(sem["zero"], 1)
                dve.tensor_reduce(MXW[:, 0:1], WQ[:, :, :].rearrange("p c n -> p (c n)"), axis=AX.X, op=ALU.max, apply_absolute_value=True).then_inc(sem["largest"], 1)
                dve.wait_ge(sem["all"], SEED + 1)
                dve.tensor_scalar(BOUND[:, :], ALLM[:, :], 1.0 / TOP, 1e-30, ALU.mult, ALU.max).then_inc(sem["bound"], 1)
                dve.wait_ge(sem["bound"], SEED + 1)
                dve.reciprocal(WSC[:, :], BOUND[:, :]).then_inc(sem["bound"], 1)
                dve.tensor_scalar(UQ[:, :], BOUND[:, :], SCALE / XSCALE, None, ALU.mult).then_inc(sem["bound"], 1)
                dve.wait_ge(sem["const"], SEED + 16 * 8)
                dve.wait_ge(sem["tanh"], SEED + 2)
                dve.wait_ge(sem["zero"], SEED + 2)
                dve.tensor_scalar(BO[:, :], BO[:, :], TG[:, 1:2], None, ALU.mult).then_inc(sem["once"], 1)

                def prepare(b, k):
                    steps = Steps(b, 2)
                    if k == 0:
                        dve.wait_ge(sem["loaded"], b * 16 + (SEED + 16))
                    if k < 4:
                        last = dve.bn_stats(BN[:, k, :], X[:, k, :])
                        if k == 3:
                            last.then_inc(sem["nstep"], 1)
                    if k == 4:
                        dve.wait_ge(sem["nstep"], steps.next())
                        dve.memset(VE[:, 0:1], 0.0)
                        for t in range(TT):
                            last = dve.bn_aggr(MV[:, t, :], BN[:, t, :])
                        last.then_inc(sem["nstep"], 1)
                        dve.wait_ge(sem["nstep"], steps.next())
                        dve.tensor_scalar(VE[:, :], MV[:, :, 1], EPS, None, ALU.add).then_inc(sem["stats"], 1)
                    if k == 8:
                        dve.wait_ge(sem["rstd"], after(b, 1, 0))
                        dve.wait_ge(sem["full"], after(b, len(jobs), NX[-1] - len(jobs)))
                    if k >= 8:
                        t = k - 8
                        last = dve.tensor_scalar(XB[:, t, :], X[:, t, :], MV[:, t, 0:1], RD[:, t:t + 1], ALU.subtract, ALU.mult)
                        if k == 11:
                            last.then_inc(sem["norm"], 1)
                            dve.wait_ge(sem["norm"], after(b, 1, 0))
                            dve.sem_inc(sem["read"], 1)

                for k in (0, 1, 2, 3, 4, 8, 9, 10, 11):
                    prepare(0, k)
                dve.wait_ge(sem["whigh"], SEED + 1)
                dve.scalar_tensor_tensor(out=WS[:, 1, :, :], in0=WQ[:, :, :], scalar=WSC[:, 0:1], in1=WS[:, 0, :, :], op0=ALU.mult, op1=ALU.subtract).then_inc(sem["wlow"], 1)
                with dve.Fori(0, B) as i:
                    steps = Steps(i, U)
                    for m in NX:
                        k = jobs[m][1]
                        dve.wait_ge(sem["xhigh"], after(i, CT, k))
                        dve.scalar_tensor_tensor(out=XS[:, 1, k, :], in0=pW[m % 2][:, :], scalar=XSCALE, in1=XS[:, 0, k, :],
                                                 op0=ALU.mult, op1=ALU.subtract).then_inc(sem["dve_empty"], 1)
                    for m in NVV:
                        k = jobs[m][1]
                        dve.wait_ge(sem["full"], after(i, len(jobs), m))
                        dve.tensor_tensor(V[:, k, :], pW[m % 2][:, :], BV[:, :], ALU.add).then_inc(sem["dve_empty"], 1)
                    n = lambda k: after(i, U, k)
                    for r in range(U + 1):
                        if r < U:
                            w = P * tiles(r % TT)
                            dve.wait_ge(sem["scores"], n(r))
                            dve.wait_ge(sem["probs"], n(r - 4))
                            dve.tensor_reduce(NM[:, r % 4:r % 4 + 1], pS[r % 3][:, 0:w], axis=AX.X, op=ALU.max, negate=True).then_inc(sem["negmax"], 1)
                        if 20 <= r < 40 and r % 2 == 0 and (r < 30 or r >= 32):
                            prepare(i + 1, {20: 0, 22: 1, 24: 2, 26: 3, 28: 4, 32: 8, 34: 9, 36: 10, 38: 11}[r])
                        if r >= 1:
                            q = (r - 1) % 4
                            w = P * tiles((r - 1) % TT)
                            dve.wait_ge(sem["probs"], n(r - 1))
                            dve.reciprocal(RI[:, q:q + 1], SM[:, q:q + 1]).then_inc(sem["step"], 1)
                            dve.wait_ge(sem["step"], steps.next())
                            dve.tensor_scalar(PR[:, q, 0:w], PR[:, q, 0:w], RI[:, q:q + 1], None, ALU.mult).then_inc(sem["scaled"], 1)
                    steps.close()
                    dve.wait_ge(sem["biased"], after(i, 1, 0))
                    dve.wait_ge(sem["out"], i * 16 + SEED)
                    for m in NO:
                        k = jobs[m][1]
                        dve.wait_ge(sem["full"], after(i, len(jobs), m))
                        dve.scalar_tensor_tensor(out=Y[:, k, :], in0=pW[m % 2][:, :], scalar=TG[:, 1:2], in1=XL[:, k, :],
                                                 op0=ALU.mult, op1=ALU.add).then_inc(sem["dve_empty"], 1)

            @block.tensor
            def _(pe):
                pe.wait_ge(sem["const"], SEED + 16 * 8)
                pe.wait_ge(sem["zero"], SEED + 2)
                pe.wait_ge(sem["wlow"], SEED + 1)
                with pe.Fori(0, B) as i:
                    def ready(m):
                        for e in ("act", "dve"):
                            pe.wait_ge(emptied[e], banks.emptied(i, m, e))

                    def taken(m):
                        e = banks.engine[m]
                        pe.wait_ge(emptied[e], banks.emptied(i, m, e))

                    def free(m):
                        before = banks.engine[(m - 2) % len(jobs)]
                        pe.wait_ge(emptied[before], banks.emptied(i, m - 2, before))

                    for m in range(NO[0]):
                        kind, k = jobs[m]
                        if kind == "x" and k == 0:
                            pe.wait_ge(sem["norm"], after(i, 1, 0))
                        if kind == "k" and k == 0:
                            pe.wait_ge(sem["ctx"], i * 16 + (SEED + 16))
                        free(m)
                        w = pW[m % 2]
                        for c in range(4):
                            if kind == "x":
                                last = pe.transpose(w[:, P * c:P * c + P], XB[:, c, P * k:P * k + P], IDF[:, :])
                            if kind == "q" and k == 0 and c > 0:
                                taken(NX[c])
                            if kind == "q":
                                for n, (one, two) in enumerate(THREE):
                                    last = pe.matmul(w[:, :], WS[:, one, c, P * k:P * k + P], XS[:, two, c, :], start=c + n == 0, stop=c + n == CT + 1)
                            if kind == "k":
                                last = pe.matmul(w[:, :], WK[:, c, P * k:P * k + P], C[:, c, :], start=c == 0, stop=c == 3)
                            if kind == "v":
                                last = pe.matmul(w[:, :], C[:, c, P * k:P * k + P], WV[:, c, :], start=c == 0, stop=c == 3)
                        last.then_inc(sem["full"], 1)
                    ready(NK[-1])
                    n = lambda k: after(i, U, k)
                    for r in range(U + LV):
                        if r < U:
                            h, t = r // TT, r % TT
                            w = P * tiles(t)
                            j, v = h // 4, h % 4
                            pe.wait_ge(sem["probs"], n(r - 3 if r >= 3 else -1))
                            pe.matmul(pS[r % 3][:, 0:w], IDB[:, :], MASK[:, 3 * P - w:3 * P], start=True, stop=False)
                            pe.matmul(pS[r % 3][:, 0:w], QT[:, j, P * t:P * t + P], KT[:, j, v, P * (t + 1) - w:P * (t + 1)],
                                      start=False, stop=True).then_inc(sem["scores"], 1)
                        if LP <= r < U + LP:
                            q = (r - LP) % 4
                            pe.wait_ge(sem["scaled"], n(r - LP))
                            pe.wait_ge(sem["pcopy"], n(r - LP - 2))
                            for k in range(tiles((r - LP) % TT)):
                                last = pe.transpose(pP[(r - LP) % 2][:, P * k:P * k + P], PR[:, q, P * k:P * k + P], IDF[:, :])
                            last.then_inc(sem["pturn"], 1)
                        if r == LV:
                            ready(NVV[-1])
                        if r >= LV:
                            h, t = (r - LV) // TT, (r - LV) % TT
                            j, v = h // 4, h % 4
                            pe.wait_ge(sem["pcopy"], n(r - LV))
                            if v == 0 and t == 0:
                                pe.wait_ge(sem["outTcopy"], after(i, J, j - 2))
                            nk = tiles(t)
                            for k in range(nk):
                                last = pe.matmul(pO[j % 2][DH * v:DH * v + DH, P * t:P * t + P], V[:, t + 1 - nk + k, DH * h:DH * h + DH],
                                                 PT[:, (r - LV) % 3, P * k:P * k + P], start=k == 0, stop=k == nk - 1, skip_group_check=True)
                            last.then_inc(sem["outT"], 1)
                    for m in NO:
                        k = jobs[m][1]
                        free(m)
                        for c in range(4):
                            if m == NO[0] and c in (0, 3):
                                pe.wait_ge(sem["outTcopy"], after(i, J, J - 2 + c // 3))
                            last = pe.matmul(pW[m % 2][:, :], OT[:, c, P * k:P * k + P], WO[:, c, :], start=c == 0, stop=c == 3)
                        last.then_inc(sem["full"], 1)


def phase_ffn(nc, used, a, x3, out, own, room):
    F, RANK = 2048, 16
    FT = F // P
    QMAX = 127.0
    MAGIC = 1.5 * 2.0 ** 23
    with ExitStack() as ctx:
        def sb(name, shape, dt=f32):
            return ctx.enter_context(nc.sbuf_tensor("d_" + name, shape, dt))

        names = ["const", "wproj", "loaded", "resid", "tanh", "zero", "read", "stats", "rstd", "norm", "xfull", "xempty", "wstep", "wmax", "wall",
                 "ab", "abdone", "high", "split", "xhigh", "hfull", "hempty", "hhigh", "hsplit", "ofull", "step", "out", "biased", "done"]
        sem = open_phase(nc, used, ["d_" + n for n in names])
        sem = {n: sem["d_" + n] for n in names}
        WF, = own
        (WP, wproj), = placed(room, a, ["wprojT"])
        X, XL, XB, Y = (WF[:, c, :].rearrange("p (t d) -> p t d", t=TT) for c in range(CT))
        WFS, WPS = sb("wfs", [P, 2, CT, F], f16), sb("wps", [P, 2, FT, D], f16)
        XS, HS = sb("xs", [P, 2, CT, S], f16), sb("hs", [P, 2, 4, S], f16)
        HF = sb("hf", [P, 2, S])
        AF, BF, AP_, BP = sb("af", [P, D]), sb("bf", [P, F]), sb("ap", [P, F]), sb("bp", [P, D])
        MXW, ALLM, BOUND = sb("mxw", [P, 7]), sb("allm", [P, 7]), sb("bound", [P, 3])
        SC = sb("sc", [P, 2, 6])
        HSC, FSC, PSC = sb("hsc", [P, 1]), sb("fsc", [P, 1]), sb("psc", [P, 1])
        BFC, BPR = sb("bfc", [P, FT]), sb("bpr", [P, D])
        IDF = sb("idf", [P, P])
        GT, TG = sb("gt", [P, 4]), sb("tg", [P, 4])
        BN, MV, VE, RD, POWT = sb("bn", [P, TT, 6]), sb("mv", [P, TT, 2]), sb("ve", [P, TT]), sb("rd", [P, TT]), sb("pow", [P, TT])
        bank = [ctx.enter_context(nc.psum_tensor(f"d_ps{i}", [P, 512], f32)) for i in range(8)]
        pW, pO = bank[0:4], bank[4:8]

        def pieces(m):
            if m < FT:
                c, f = m // 4, slice(512 * (m % 4), 512 * (m % 4) + 512)
                return WF[:, c, f], WFS[:, 0, c, f], WFS[:, 1, c, f]
            return WP[:, m - FT, :], WPS[:, 0, m - FT, :], WPS[:, 1, m - FT, :]

        with nc.Block() as block:
            @block.sync
            def _(sp):
                rows = lambda t, b: t[bass.ds(b, 1), :, :].rearrange("o (t p) d -> p (o t) d", p=P)
                sp.dma_start(WP[:, :, :], wproj).then_inc(sem["wproj"], 16)
                sp.wait_ge(sem["zero"], SEED + 2)
                for dst, src in ((AF[0:RANK, :], a["afc"]), (BF[0:RANK, :], a["bfcT"]), (AP_[0:RANK, :], a["aproj"]), (BP[0:RANK, :], a["bprojT"]),
                                 (BFC[:, :], a["b_fc"]), (BPR[:, :], a["b_proj"]), (IDF[:, :], a["idf"]), (GT[:, :], a["gates"])):
                    sp.dma_start(dst, src).then_inc(sem["const"], 16)
                sp.wait_ge(sem["split"], SEED + FT)
                sp.dma_start(X[:, :, :], rows(x3, 0)).then_inc(sem["loaded"], 16)
                with sp.Fori(0, B) as i:
                    following = sp.snap((i + 1) % B)
                    sp.wait_ge(sem["read"], after(i, 1, 0))
                    sp.dma_start(X[:, :, :], rows(x3, following)).then_inc(sem["loaded"], 16)
                    sp.wait_ge(sem["done"], after(i, 1, -1))
                    sp.dma_start(XL[:, :, :], rows(x3, i)).then_inc(sem["resid"], 16)
                    sp.wait_ge(sem["done"], after(i, 1, 0))
                    sp.dma_start(rows(out, i), Y[:, :, :]).then_inc(sem["out"], 16)
                sp.wait_ge(sem["out"], SEED + 16 * B)

            @block.gpsimd
            def _(pool):
                pool.wait_ge(sem["zero"], SEED + 1)
                for lora in (AF, BF, AP_, BP):
                    last = pool.memset(lora[:, :], 0.0)
                last.then_inc(sem["zero"], 1)
                pool.wait_ge(sem["wmax"], SEED + 1)
                pool.partition_all_reduce(ALLM[:, :], MXW[:, :], P, bass.bass_isa.ReduceOp.max).then_inc(sem["wall"], 1)
                for m in range(2 * FT):
                    part, high, low = pieces(m)
                    pool.wait_ge(sem["high"], SEED + m + 1)
                    pool.tensor_tensor(low, part, high, ALU.subtract).then_inc(sem["split"], 1)
                pool.wait_ge(sem["zero"], SEED + 3)
                pool.wait_ge(sem["stats"], SEED + 1)
                pool.tensor_tensor(RD[:, :], VE[:, :], POWT[:, :], ALU.pow).then_inc(sem["rstd"], 1)
                with pool.Fori(0, B) as i:
                    pool.wait_ge(sem["stats"], after(i, 1, 1))
                    pool.tensor_tensor(RD[:, :], VE[:, :], POWT[:, :], ALU.pow).then_inc(sem["rstd"], 1)
                    pool.wait_ge(sem["resid"], i * 16 + (SEED + 16))
                    for t in range(TT):
                        last = pool.tensor_tensor(XL[:, t, :], XL[:, t, :], BPR[:, :], ALU.add)
                    last.then_inc(sem["biased"], 1)

            @block.scalar
            def _(act):
                act.wait_ge(sem["const"], SEED + 16 * 8)
                act.activation(TG[:, :], GT[:, :], ACT.Tanh).then_inc(sem["tanh"], 1)
                for m in range(2 * FT):
                    part, high, low = pieces(m)
                    act.wait_ge(sem["abdone"], SEED + m + 1)
                    act.copy(high, part).then_inc(sem["high"], 1)
                with act.Fori(0, B) as i:
                    for c in range(CT):
                        act.wait_ge(sem["xfull"], after(i, CT, c))
                        act.mul(XS[:, 0, c, :], pW[c][:, :], XSCALE).then_inc(sem["xhigh"], 1)
                    for f in range(FT):
                        act.wait_ge(sem["hfull"], after(i, FT, f))
                        act.wait_ge(sem["hsplit"], after(i, FT, f - 2))
                        act.activation(HF[:, f % 2, :], pW[f % 4][:, :], ACT.Gelu, bias=BFC[:, f:f + 1], scale=FSC[:, 0:1]).then_inc(sem["hempty"], 1)

            @block.vector
            def _(dve):
                dve.memset(POWT[:, :], -0.5)
                dve.memset(MXW[:, :], 0.0).then_inc(sem["zero"], 1)
                dve.wait_ge(sem["zero"], SEED + 1)
                flat = [W[:, :, :].rearrange("p c f -> p (c f)") for W in (WF, WP)]
                dve.tensor_reduce(MXW[:, 0:1], flat[0], axis=AX.X, op=ALU.max, apply_absolute_value=True)
                dve.wait_ge(sem["const"], SEED + 16 * 8)
                for k, small in enumerate((AF, BF, AP_, BP, BFC)):
                    dve.tensor_reduce(MXW[:, 2 + k:3 + k], small[:, :], axis=AX.X, op=ALU.max, apply_absolute_value=True)
                dve.wait_ge(sem["wproj"], SEED + 16)
                dve.tensor_reduce(MXW[:, 1:2], flat[1], axis=AX.X, op=ALU.max, apply_absolute_value=True).then_inc(sem["wmax"], 1)
                dve.wait_ge(sem["tanh"], SEED + 1)
                dve.tensor_scalar(BPR[:, :], BPR[:, :], TG[:, 3:4], None, ALU.mult).then_inc(sem["zero"], 1)
                dve.wait_ge(sem["wall"], SEED + 1)

                def in_turn(k, instruction):
                    instruction.then_inc(sem["wstep"], 1)
                    dve.wait_ge(sem["wstep"], SEED + k + 1)

                column = lambda n, c: SC[:, n, c:c + 1]
                k = 0
                for n in range(2):
                    fa, fb = ALLM[:, 2 + 2 * n:3 + 2 * n], ALLM[:, 3 + 2 * n:4 + 2 * n]
                    in_turn(k, dve.tensor_scalar(column(n, 0), ALLM[:, n:n + 1], 1.0 / QMAX, None, ALU.mult))
                    in_turn(k + 1, dve.reciprocal(column(n, 1), column(n, 0)))
                    in_turn(k + 2, dve.tensor_scalar(column(n, 2), fa, fb, 2.0 * RANK / TOP, ALU.mult, ALU.mult))
                    in_turn(k + 3, dve.tensor_scalar(BOUND[:, n:n + 1], column(n, 0), (QMAX + 1) / TOP, column(n, 2), ALU.mult, ALU.add))
                    in_turn(k + 4, dve.reciprocal(column(n, 3), BOUND[:, n:n + 1]))
                    in_turn(k + 5, dve.tensor_scalar(column(n, 4), column(n, 0), column(n, 3), None, ALU.mult))
                    in_turn(k + 6, dve.tensor_scalar(column(n, 5), column(n, 3), 2.0, None, ALU.mult))
                    k += 7
                in_turn(k, dve.tensor_scalar(HSC[:, :], ALLM[:, 6:7], 1.0 / TOP, None, ALU.mult))
                in_turn(k + 1, dve.tensor_scalar(BOUND[:, 2:3], BOUND[:, 0:1], float(D), HSC[:, 0:1], ALU.mult, ALU.add))
                in_turn(k + 2, dve.reciprocal(HSC[:, :], BOUND[:, 2:3]))
                in_turn(k + 3, dve.tensor_scalar(FSC[:, :], BOUND[:, 0:1], 1.0 / XSCALE, None, ALU.mult))
                in_turn(k + 4, dve.tensor_scalar(PSC[:, :], BOUND[:, 1:2], BOUND[:, 2:3], TG[:, 3:4], ALU.mult, ALU.mult))
                k += 5
                for n in range(2):
                    in_turn(k, dve.tensor_scalar(flat[n], flat[n], column(n, 1), MAGIC, ALU.mult, ALU.add))
                    in_turn(k + 1, dve.tensor_scalar(flat[n], flat[n], MAGIC, QMAX, ALU.subtract, ALU.min))
                    in_turn(k + 2, dve.tensor_scalar(flat[n], flat[n], -QMAX - 1, column(n, 4), ALU.max, ALU.mult))
                    k += 3
                    for m in range(FT * n, FT * n + FT):
                        part, _, _ = pieces(m)
                        dve.wait_ge(sem["ab"], SEED + m + 1)
                        dve.scalar_tensor_tensor(out=part, in0=pW[m % 4][:, :], scalar=column(n, 5), in1=part, op0=ALU.mult, op1=ALU.add).then_inc(sem["abdone"], 1)

                def prepare(i, k):
                    dve.wait_ge(sem["loaded"], i * 16 + (SEED + 16 * k + 16))
                    for t in range(TT):
                        last = dve.bn_stats(BN[:, t, :], X[:, t, :])
                    last.then_inc(sem["step"], 1)
                    dve.wait_ge(sem["step"], after(i, 2, 2 * k))
                    dve.memset(VE[:, 0:1], 0.0)
                    for t in range(TT):
                        last = dve.bn_aggr(MV[:, t, :], BN[:, t, :])
                    last.then_inc(sem["step"], 1)
                    dve.wait_ge(sem["step"], after(i, 2, 2 * k + 1))
                    dve.tensor_scalar(VE[:, :], MV[:, :, 1], EPS, None, ALU.add).then_inc(sem["stats"], 1)
                    dve.wait_ge(sem["rstd"], after(i, 1, k))
                    dve.wait_ge(sem["xfull"], after(i, CT, CT * (k - 1) + CT - 1))
                    for t in range(TT):
                        last = dve.tensor_scalar(XB[:, t, :], X[:, t, :], MV[:, t, 0:1], RD[:, t:t + 1], ALU.subtract, ALU.mult)
                    last.then_inc(sem["norm"], 1)
                    dve.wait_ge(sem["norm"], after(i, 1, k))
                    dve.sem_inc(sem["read"], 1)

                prepare(0, 0)
                with dve.Fori(0, B) as i:
                    for c in range(CT):
                        dve.wait_ge(sem["xhigh"], after(i, CT, c))
                        dve.scalar_tensor_tensor(out=XS[:, 1, c, :], in0=pW[c][:, :], scalar=XSCALE, in1=XS[:, 0, c, :],
                                                 op0=ALU.mult, op1=ALU.subtract).then_inc(sem["xempty"], 1)
                    for f in range(FT):
                        h = HF[:, f % 2, :]
                        dve.wait_ge(sem["hempty"], after(i, FT, f))
                        dve.wait_ge(sem["ofull"], after(i, FT, f - 4))
                        dve.tensor_scalar(HS[:, 0, f % 4, :], h, HSC[:, 0:1], None, ALU.mult).then_inc(sem["hhigh"], 1)
                        dve.wait_ge(sem["hhigh"], after(i, FT, f))
                        dve.scalar_tensor_tensor(out=HS[:, 1, f % 4, :], in0=h, scalar=HSC[:, 0:1], in1=HS[:, 0, f % 4, :],
                                                 op0=ALU.mult, op1=ALU.subtract).then_inc(sem["hsplit"], 1)
                        if f == 4:
                            prepare(i, 1)
                    dve.wait_ge(sem["biased"], after(i, 1, 0))
                    dve.wait_ge(sem["out"], i * 16 + SEED)
                    dve.wait_ge(sem["ofull"], after(i, FT, FT - 1))
                    for t in range(TT):
                        last = dve.scalar_tensor_tensor(out=Y[:, t, :], in0=pO[t][:, :], scalar=PSC[:, 0:1], in1=XL[:, t, :], op0=ALU.mult, op1=ALU.add)
                    last.then_inc(sem["done"], 1)

            @block.tensor
            def _(pe):
                pe.wait_ge(sem["const"], SEED + 16 * 8)
                for m in range(2 * FT):
                    if m >= 4:
                        pe.wait_ge(sem["abdone"], SEED + m - 3)
                    if m < FT:
                        c, f = m // 4, m % 4
                        last = pe.matmul(pW[m % 4][:, :], AF[:, P * c:P * c + P], BF[:, 512 * f:512 * f + 512], start=True, stop=True)
                    else:
                        f = m - FT
                        last = pe.matmul(pW[m % 4][:, :], AP_[:, P * f:P * f + P], BP[:, :], start=True, stop=True)
                    last.then_inc(sem["ab"], 1)
                pe.wait_ge(sem["split"], SEED + 2 * FT)
                with pe.Fori(0, B) as i:
                    pe.wait_ge(sem["norm"], after(i, 1, 0))
                    for c in range(CT):
                        pe.wait_ge(sem["hempty"], after(i, FT, c - 4))
                        for t in range(TT):
                            last = pe.transpose(pW[c][:, P * t:P * t + P], XB[:, t, P * c:P * c + P], IDF[:, :])
                        last.then_inc(sem["xfull"], 1)
                    pe.wait_ge(sem["xempty"], after(i, CT, CT - 1))
                    for f in range(FT + 2):
                        if f < FT:
                            pe.wait_ge(sem["hempty"], after(i, FT, f - 4))
                            for c in range(CT):
                                for n, (wn, xn) in enumerate(THREE):
                                    last = pe.matmul(pW[f % 4][:, :], WFS[:, wn, c, P * f:P * f + P], XS[:, xn, c, :],
                                                     start=c + n == 0, stop=c + n == CT + 1)
                            last.then_inc(sem["hfull"], 1)
                        if f >= 2:
                            g = f - 2
                            pe.wait_ge(sem["hsplit"], after(i, FT, g))
                            if g == 0:
                                pe.wait_ge(sem["done"], after(i, 1, -1))
                            for t in range(TT):
                                for n, (hn, wn) in enumerate(THREE):
                                    last = pe.matmul(pO[t][:, :], HS[:, hn, g % 4, P * t:P * t + P], WPS[:, wn, g, :],
                                                     start=g + n == 0, stop=g + n == FT + 1)
                            last.then_inc(sem["ofull"], 1)


def program(nc, a, out, x1, x1l, xr, s_route, sel, qsel, qidx, x2, x3):
    def run(phase, *args):
        used = []
        phase(nc, used, *args)
        close_phase(nc, used)

    def places(pairs):
        return [place for place, _ in pairs]

    with ExitStack() as ctx:
        room = ctx.enter_context(nc.sbuf_tensor("room", [P, 4 * CT * D], f32))
        local = placed(room, a, ["wqkvT", "woutlT"])
        window = placed(room, a, ["xwqT", "xwkT", "xwvT", "xwoT"])
        run(phase_token_heads, a["x_th"], a["v_th"], a["kT_th"], a, a["gates"], x1, local)
        second = ctx.enter_context(nc.sbuf_tensor("second_room", [P, 4 * CT * D], f32))
        heavy = placed(second, a, ["hwqT", "hwkT", "hwvT", "hwoT"])
        fc = placed(second, a, ["wfcT"])
        run(phase_local, a, x1, x1l, xr, s_route, places(local), heavy)
        run(phase_route, a, s_route, sel, qsel, qidx)
        run(phase_heavy, a, xr, x1l, sel, qsel, qidx, x2, places(heavy), window)
        run(phase_window, a, x2, x3, places(window), fc)
        run(phase_ffn, a, x3, out, places(fc), room)


BF16_CONSTANTS = ("idb", "mask_th", "neg64", "mask_w")


def bf16_bits(constant):
    return (constant.astype(np.float32).view(np.uint32) >> 16).astype(np.uint16)


def dram_inputs(nc, arrays):
    a = {k: nc.dram_tensor(f"in_{k}", v.shape, mybir.dt.from_np(v.dtype), kind="ExternalInput").ap() for k, v in arrays.items()}
    return {k: v.bitcast(bf16) if k in BF16_CONSTANTS else v for k, v in a.items()}


def layouts(inputs):
    f = {k: np.asarray(v) for k, v in inputs.items()}
    x, c = f["x"], f["ctx_1024"]
    a = {}
    a["x_th"] = x.reshape(B, S // 8, P, 32).transpose(0, 2, 1, 3).reshape(B, P, S * 4)
    a["v_th"] = c.reshape(B, S // 8, P, 32).transpose(0, 2, 1, 3).reshape(B, P, S * 4)
    a["kT_th"] = c.reshape(B, S // 32, 4, P, 32).transpose(0, 2, 4, 1, 3).reshape(B, P, S // 32, P)
    a["gates"] = np.tile(np.concatenate([f["g_xattn"], f["g_ffn"]]), (P, 1))
    p = np.arange(P)
    a["idf"] = np.eye(P, dtype=np.float32)
    a["idb"] = bf16_bits(np.eye(P))
    same = p[:, None] // 16 == p[None, :] // 16
    a["blockmean"] = (same / D).astype(np.float32)
    a["mask_th"] = bf16_bits(np.tile(np.where(same & (p[None, :] <= p[:, None]), 0, NEG), (1, 4)))
    def wT(w):
        return w.T.reshape(w.shape[1] // P, P, w.shape[0]).transpose(1, 0, 2)

    def col(v):
        return v.reshape(-1, P).T

    a["wqkvT"], a["woutlT"] = wT(f["L0_ffn_Wqkv"]), wT(f["L0_ffn_Wout_l"])
    a["rt"] = np.tile(np.stack([f["L0_ffn_rt_q"][0], f["L0_ffn_rt_kv"][0]])[None], (P, 1, 1))
    a["ln_w"], a["ln_b"] = col(f["L0_ffn_ln_w"]), col(f["L0_ffn_ln_b"])
    a["neg64"] = bf16_bits(np.full((P, 64), -1e9))
    k_of = [min(256 * 9.0 / 8.0, float(S)), min(512 * 9.0 / 8.0, float(S))]
    a["router_k"] = np.repeat([[np.log(S) - np.log(k), 1 / k] for k in k_of], B, axis=0).astype(np.float32)
    a["batch_base"] = np.tile(S * np.arange(B, dtype=np.float32)[None], (P, 1))
    wkv = f["L0_ffn_Wkv"].reshape(8, 2, 64, D)
    a["hwqT"], a["hwoT"] = wT(f["L0_ffn_Wq"]), wT(f["L0_ffn_Wout_h"])
    a["hwkT"], a["hwvT"] = wT(wkv[:, 0].reshape(D, D)), wT(wkv[:, 1].reshape(D, D))
    a["gamma"] = col(f["L0_ffn_gamma"])
    nk, nv = f["L0_ffn_null_kv"]
    nkb, nvb = np.zeros((P, 4, 2), np.float32), np.zeros((P, 4, P), np.float32)
    for h in range(8):
        o = 64 * (h % 2)
        nkb[o:o + 64, h // 2, h % 2] = nk[h]
        nvb[h, h // 2, o:o + 64] = nv[h]
    a["null_k"], a["null_v"] = nkb, nvb
    a["null_q"] = np.tile(f["L0_ffn_null_q"][None], (P, 1))
    a["ctxT"] = c.transpose(0, 2, 1).reshape(B, CT, P, S).transpose(0, 2, 1, 3)
    for n in "qkvo":
        a[f"xw{n}T"] = wT(f[f"L1_xattn_w{n}"])
    a["xbq"], a["xbk"] = col(f["L1_xattn_bq"]), col(f["L1_xattn_bk"])
    a["xbv"], a["xbo"] = (np.tile(f[k][None], (P, 1)) for k in ("L1_xattn_bv", "L1_xattn_bo"))
    r, k = p[:, None], p[None, :]
    a["mask_w"] = bf16_bits(np.concatenate([np.where(k >= r, 0, NEG), 0.0 * (k + r), np.where(k <= r, 0, NEG)], 1))
    a["wfcT"], a["wprojT"] = wT(f["L1_ffn_W_fc"]), wT(f["L1_ffn_W_proj"])
    a["afc"], a["aproj"] = f["L1_ffn_A_fc"], f["L1_ffn_A_proj"]
    a["bfcT"], a["bprojT"] = f["L1_ffn_B_fc"].T, f["L1_ffn_B_proj"].T
    a["b_fc"], a["b_proj"] = col(f["L1_ffn_b_fc"]), np.tile(f["L1_ffn_b_proj"][None], (P, 1))
    return {k: np.ascontiguousarray(v) for k, v in a.items()}


def kernel(**inputs):
    import concourse.bacc as _bacc
    from concourse.bass_utils import run_bass_kernel_spmd as _run

    nc = _bacc.Bacc("TRN2", target_bir_lowering=False, num_devices=1)
    arrays = layouts(inputs)
    a = dram_inputs(nc, arrays)
    out = nc.dram_tensor("out_0", (B, S, D), f32, kind="ExternalOutput").ap()
    scratch = {k: nc.dram_tensor(f"s_{k}", shape, mybir.dt.uint32 if k == "qidx" else f32).ap() for k, shape in SCRATCH.items()}
    program(nc, a, out, **scratch)
    r = _run(nc, [{f"in_{k}": v for k, v in arrays.items()}], core_ids=[0])
    return r.results[0]["out_0"]


SCRATCH = {"x1": (B, S, D), "x1l": (B, S, D), "xr": (B, S, D), "s_route": (B, P, 2 * TT), "sel": (P, TT, 3 * B),
           "qsel": (P, 2, B), "qidx": (P, 2, B), "x2": (B, S, D), "x3": (B, S, D)}
```
